# Optimizing a Trainium2 kernel written in Bass

```python
import numpy as np
import jax
import jax.numpy as jnp

def _softmax(x, axis=-1):
    return jax.nn.softmax(x, axis=axis)

def _gelu(x):
    return jax.nn.gelu(x, approximate=True)

def _silu(x):
    return jax.nn.silu(x)

def _sigmoid(x):
    return jax.nn.sigmoid(x)

def _layernorm(x, axis=-1, eps=1e-05):
    m = jnp.mean(x, axis=axis, keepdims=True)
    v = jnp.var(x, axis=axis, keepdims=True)
    return (x - m) / jnp.sqrt(v + eps)

def _scatter_add(tgt, idx, src, axis=0):
    return tgt.at[idx].add(src)

def _segment_sum(src, seg, n):
    return jax.ops.segment_sum(src, seg, n)
kernel_name = 'mk_gnn_resnorm_d4_gnn_r64_2067ad'

def setup_inputs(seed: int=0):
    np.random.seed(seed)
    _w = jnp.asarray

    def _rec_inputs():
        import jax
        import jax.numpy as jnp
        _gk = jax.random.key(seed)
        x = -0.0001006 + 1 * jax.random.normal(jax.random.fold_in(_gk, 1), (100000, 48), jnp.float32)
        src = jax.random.randint(jax.random.fold_in(_gk, 2), (25000,), 0, 100000, jnp.int32)
        dst = jax.random.randint(jax.random.fold_in(_gk, 3), (25000,), 0, 100000, jnp.int32)
        _o = jnp.argsort(dst, stable=True)
        src = src[_o]
        dst = dst[_o]
        edge_attr_40 = jax.random.uniform(jax.random.fold_in(_gk, 13), (25000, 40), jnp.float32, 0.0, 1)
        edge_weight = jax.random.uniform(jax.random.fold_in(_gk, 15), (25000,), jnp.float32, 0.0, 0.999999)
        node_type_119 = jax.random.randint(jax.random.fold_in(_gk, 16), (100000,), 0, 119, jnp.int32)
        node_vec = jax.random.uniform(jax.random.fold_in(_gk, 17), (100000,), jnp.float32, 0.0, 1.49999)
        return (x, src, dst, edge_attr_40, edge_weight, node_type_119, node_vec)
    x, src, dst, edge_attr_40, edge_weight, node_type_119, node_vec = _rec_inputs()

    def _L0_gnn_setup():
        import jax, jax.numpy as jnp
        import numpy as np
        N_NODES = 100000
        N_EDGES = 25000
        D_FEAT = 48
        K = 10
        ALPHA = 0.1
        key = jax.random.key(seed)
        k1, k2, k3 = jax.random.split(key, 3)
        x = jax.random.normal(k1, (N_NODES, D_FEAT), dtype=jnp.float32)
        edge_index = jax.random.randint(k2, (2, N_EDGES), 0, N_NODES, dtype=jnp.int64)
        edge_weight = jax.random.uniform(k3, (N_EDGES,), dtype=jnp.float32)
        return {'x': x, 'edge_index': edge_index, 'edge_weight': edge_weight}
    _L0_gnn_all = _L0_gnn_setup()
    _L0_gnn_in = {k: v for k, v in _L0_gnn_all.items() if k in ()}
    del _L0_gnn_all

    def _L1_gnn_setup():
        import jax, jax.numpy as jnp
        import numpy as np
        N_NODES = 100000
        N_EDGES = 25000
        D_IN = 48
        D_OUT = 48
        key = jax.random.key(seed)
        k1, k2, k3, k4, k5, k6 = jax.random.split(key, 6)
        inputs = jax.random.normal(k1, (N_NODES, D_IN), dtype=jnp.float32)
        edge_row = jnp.sort(jax.random.randint(k2, (N_EDGES,), 0, N_NODES, dtype=jnp.int64))
        edge_col = jax.random.randint(k3, (N_EDGES,), 0, N_NODES, dtype=jnp.int64)
        edge_val = jax.random.uniform(k4, (N_EDGES,), dtype=jnp.float32)
        std = float(np.sqrt(2.0 / (D_IN + D_OUT)))
        weight = jax.random.normal(k5, (D_IN, D_OUT), dtype=jnp.float32) * std
        bias = jnp.zeros((D_OUT,), dtype=jnp.float32)
        return {'inputs': inputs, 'edge_row': edge_row, 'edge_col': edge_col, 'edge_val': edge_val, 'weight': weight, 'bias': bias}
    _L1_gnn_all = _L1_gnn_setup()
    _L1_gnn_in = {k: v for k, v in _L1_gnn_all.items() if k in ('weight', 'bias')}
    del _L1_gnn_all

    def _L2_gnn_setup():
        import jax, jax.numpy as jnp
        import numpy as np
        N_NODES = 100000
        N_EDGES = 25000
        IN_F = 48
        OUT_F = 48
        key = jax.random.key(seed)
        k1, k2, k3, k4 = jax.random.split(key, 4)
        x = jax.random.normal(k1, (N_NODES, IN_F), dtype=jnp.float32)
        edge_index = jax.random.randint(k2, (2, N_EDGES), 0, N_NODES, dtype=jnp.int32)
        bound = 1.0 / np.sqrt(IN_F)
        W = jax.random.uniform(k3, (OUT_F, IN_F), minval=-bound, maxval=bound, dtype=jnp.float32)
        b = jax.random.uniform(k4, (OUT_F,), minval=-bound, maxval=bound, dtype=jnp.float32)
        return {'x': x, 'edge_index': edge_index, 'W': W, 'b': b}
    _L2_gnn_all = _L2_gnn_setup()
    _L2_gnn_in = {k: v for k, v in _L2_gnn_all.items() if k in ('W', 'b')}
    del _L2_gnn_all

    def _L3_gnn_setup():
        import jax, jax.numpy as jnp
        import numpy as np
        CUTOFF = 6.0
        LN_EPS = 1e-05
        key = jax.random.key(seed)
        ks = jax.random.split(key, 16)
        N, E, H, R, NEL, G = (50000, 12500, 48, 40, 119, 32)
        inp = {'h': jax.random.normal(ks[0], (N, H), jnp.float32), 'edge_index': jax.random.randint(ks[1], (2, E), 0, N, jnp.int64), 'edge_attr': jax.random.uniform(ks[2], (E, R), jnp.float32), 'distances': jax.random.uniform(ks[3], (E,), jnp.float32) * 7.0, 'atom_z': jax.random.randint(ks[4], (N,), 0, NEL, jnp.int64), 'node_mult': jax.random.uniform(ks[5], (N,), jnp.float32) + 0.5, 'batch': jnp.zeros((N,), jnp.int64), 'W1': jax.random.normal(ks[6], (H, R), jnp.float32) / np.sqrt(R), 'b1': jax.random.normal(ks[7], (H,), jnp.float32) * 0.01, 'W2': jax.random.normal(ks[8], (H, H), jnp.float32) / np.sqrt(H), 'b2': jax.random.normal(ks[9], (H,), jnp.float32) * 0.01, 'emb': jax.random.normal(ks[10], (NEL, G), jnp.float32) * 0.01, 'adaptW': jax.random.normal(ks[11], (G, G), jnp.float32) * 0.01, 'gamma': jnp.ones((H,), jnp.float32), 'beta': jnp.zeros((H,), jnp.float32)}
        return inp
    _L3_gnn_all = _L3_gnn_setup()
    _L3_gnn_in = {k: v for k, v in _L3_gnn_all.items() if k in ('W1', 'b1', 'W2', 'b2', 'emb', 'adaptW', 'gamma', 'beta')}
    del _L3_gnn_all
    return {'x': x, 'src': src, 'dst': dst, 'edge_attr_40': edge_attr_40, 'edge_weight': edge_weight, 'node_type_119': node_type_119, 'node_vec': node_vec, 'L1_gnn_weight': _L1_gnn_in['weight'], 'L1_gnn_bias': _L1_gnn_in['bias'], 'L2_gnn_W': _L2_gnn_in['W'], 'L2_gnn_b': _L2_gnn_in['b'], 'L3_gnn_W1': _L3_gnn_in['W1'], 'L3_gnn_b1': _L3_gnn_in['b1'], 'L3_gnn_W2': _L3_gnn_in['W2'], 'L3_gnn_b2': _L3_gnn_in['b2'], 'L3_gnn_emb': _L3_gnn_in['emb'], 'L3_gnn_adaptW': _L3_gnn_in['adaptW'], 'L3_gnn_gamma': _L3_gnn_in['gamma'], 'L3_gnn_beta': _L3_gnn_in['beta']}

def reference(x, src, dst, edge_attr_40, edge_weight, node_type_119, node_vec, L1_gnn_weight, L1_gnn_bias, L2_gnn_W, L2_gnn_b, L3_gnn_W1, L3_gnn_b1, L3_gnn_W2, L3_gnn_b2, L3_gnn_emb, L3_gnn_adaptW, L3_gnn_gamma, L3_gnn_beta):
    import jax
    import jax.numpy as jnp

    def _L0_gnn_ref(x, edge_index, edge_weight):
        import jax, jax.numpy as jnp
        import numpy as np
        N_NODES = 100000
        N_EDGES = 25000
        D_FEAT = 48
        K = 10
        ALPHA = 0.1
        row, col = (edge_index[0], edge_index[1])
        deg_w = jax.ops.segment_sum(edge_weight, row, num_segments=N_NODES)
        norm = edge_weight / (deg_w[row] + 1e-10)

        def step(h, _):
            msg = jax.ops.segment_sum(norm[:, None] * h[col], row, num_segments=N_NODES)
            h_new = (1.0 - ALPHA) * msg + ALPHA * x
            return (h_new, None)
        h, _ = jax.lax.scan(step, x, None, length=K)
        return h

    def _L1_gnn_ref(inputs, edge_row, edge_col, edge_val, weight, bias):
        import jax, jax.numpy as jnp
        import numpy as np
        N_NODES = 100000
        N_EDGES = 25000
        D_IN = 48
        D_OUT = 48
        msgs = edge_val[:, None] * inputs[edge_col]
        agg = jax.ops.segment_sum(msgs, edge_row, num_segments=N_NODES)
        return agg @ weight + bias

    def _L2_gnn_ref(x, edge_index, W, b):
        import jax, jax.numpy as jnp
        import numpy as np
        N_NODES = 100000
        N_EDGES = 25000
        IN_F = 48
        OUT_F = 48
        row, col = (edge_index[0], edge_index[1])
        n = x.shape[0]
        deg = jnp.bincount(row, length=n).astype(x.dtype)
        deg_inv_sqrt = jnp.where(deg > 0, jax.lax.rsqrt(jnp.where(deg > 0, deg, 1.0)), 0.0)
        norm = deg_inv_sqrt[row] * deg_inv_sqrt[col]
        msg = norm[:, None] * x[col]
        agg = jax.ops.segment_sum(msg, row, num_segments=n)
        out = agg @ W.T + b
        return jax.nn.relu(out)

    def _L3_gnn_ref(h, edge_index, edge_attr, distances, atom_z, node_mult, batch, W1, b1, W2, b2, emb, adaptW, gamma, beta):
        import jax, jax.numpy as jnp
        import numpy as np
        CUTOFF = 6.0
        LN_EPS = 1e-05
        src, dst = (edge_index[0], edge_index[1])
        N = h.shape[0]
        gate = jax.nn.silu(edge_attr @ W1.T + b1) @ W2.T + b2
        ei = emb[atom_z[src]]
        ej = emb[atom_z[dst]]
        adapt_logit = jnp.sum(ei * (ej @ adaptW.T), axis=-1, keepdims=True)
        gate = gate + adapt_logit
        cw = jnp.where(distances < CUTOFF, 0.5 * (jnp.cos(jnp.pi * distances / CUTOFF) + 1.0), 0.0)
        mj = node_mult[dst]
        msg = gate * h[dst] * (cw * mj)[:, None]
        agg = jax.ops.segment_sum(msg, src, num_segments=N)
        tot = jax.ops.segment_sum(mj, src, num_segments=N)
        agg = agg / jnp.clip(tot, 1e-08, None)[:, None]
        x = h + agg
        mu = jnp.mean(x, axis=-1, keepdims=True)
        var = jnp.mean(jnp.square(x - mu), axis=-1, keepdims=True)
        return (x - mu) / jnp.sqrt(var + LN_EPS) * gamma + beta
    edge_index = jnp.stack([src, dst])
    batch0 = jnp.zeros((100000,), jnp.int32)
    x = _layernorm(x + _L0_gnn_ref(x, edge_index, edge_weight), axis=-1)
    x = _layernorm(x + _L1_gnn_ref(x, src, dst, edge_weight, L1_gnn_weight, L1_gnn_bias), axis=-1)
    x = _layernorm(x + _L2_gnn_ref(x, edge_index, L2_gnn_W, L2_gnn_b), axis=-1)
    x = _layernorm(x + _L3_gnn_ref(x, edge_index, edge_attr_40, edge_weight, node_type_119, node_vec, batch0, L3_gnn_W1, L3_gnn_b1, L3_gnn_W2, L3_gnn_b2, L3_gnn_emb, L3_gnn_adaptW, L3_gnn_gamma, L3_gnn_beta), axis=-1)
    return x

_drawn_inputs = setup_inputs


def setup_inputs(seed=0):
    import zlib

    import numpy as np

    out = dict(_drawn_inputs(seed))
    spreads = {'L1_gnn_bias': (0.0, 0.1), 'L3_gnn_gamma': (1.0, 0.2), 'L3_gnn_beta': (0.0, 0.1)}
    factors = {'node_vec': 50.343,
     'L3_gnn_b1': 43.525,
     'L3_gnn_b2': 25.816,
     'L3_gnn_emb': 64.0,
     'L3_gnn_adaptW': 64.0}
    for name, (base, spread) in spreads.items():
        noise = np.random.default_rng([zlib.crc32(name.encode()), seed]).standard_normal(out[name].shape)
        drawn = base * np.exp(spread * noise) if base else spread * noise
        out[name] = jnp.asarray(drawn.astype(out[name].dtype))
    for name, factor in factors.items():
        out[name] = (out[name] * factor).astype(out[name].dtype)
    return out
```

```python
from contextlib import ExitStack

import numpy as np

import concourse.bass as bass
from concourse import mybir

P = 128
NODES, EDGES, F = 100000, 25000, 48
TILES = -(-EDGES // P)
EPAD = TILES * P
CH = 14
CHUNKS = TILES // CH
BODIES = CHUNKS // 2
GR = 7
GC = GR * P
NB = -(-NODES // (P * P))
NPAD = NB * P * P
SPARE = NPAD - 1
BINS = NB * P
FAR = 1.0e6
ALPHA, K_STEPS = 0.1, 10
CUTOFF = 6.0
EPS = 1e-5
H, R_ATTR = 48, 40
NTYPE, EMB = 119, 32
FW = F + 1
XW = F + 3
NODE_W = F + 2
EDGE_W = R_ATTR + 1
C_SRCX, C_ATTR, C_W, C_KEY, C_PTR = NODE_W, 2 * NODE_W, 2 * NODE_W + R_ATTR, 2 * NODE_W + R_ATTR + 1, 2 * NODE_W + R_ATTR + 2
REC = C_PTR + 1
DROWS = 784
UNITS = DROWS // CH

DVE_COUNTS = [0, 25, 24, 12, 14, 26]

ALU = mybir.AluOpType
ACT = mybir.ActivationFunctionType
F32, F16, I32 = mybir.dt.float32, mybir.dt.float16, mybir.dt.int32
AX_X = mybir.AxisListType.X

K_ID, K_PART, K_NEXT, K_NEXTT, K_BEFORE, K_DELTA, K_ROW, K_ONE = 0, 128, 135, 263, 391, 519, 519 + CH, 647 + CH
K_W = K_ONE + 1
J_IOTA, J_EARLIER, J_ID = 0, BINS, BINS + GC
J_W = J_ID + P


def constants():
    f = np.zeros((P, K_W), np.float32)
    p = np.arange(P)
    f[p, K_ID + p] = 1.0
    f[:, K_PART:K_PART + NB] = p[:, None] + P * np.arange(NB)
    f[p[1:], K_NEXT + p[:-1]] = 1.0
    f[0, K_NEXTT + P - 1] = 1.0
    f[:, K_BEFORE:K_BEFORE + P] = p[:, None] < p[None, :]
    c = np.arange(CH)
    f[c, K_DELTA + c] = 1.0
    f[:, K_ROW:K_ROW + P] = p[None, :]
    f[:, K_ONE] = 1.0
    h = np.zeros((P, J_W), np.float16)
    h[:, J_IOTA:J_IOTA + BINS] = np.arange(BINS)
    h[:, J_EARLIER:J_EARLIER + GC - P] = 1.0
    h[:, J_EARLIER + GC - P:J_EARLIER + GC] = p[None, :] < p[:, None]
    h[p, J_ID + p] = 1.0
    return f, h


class Chain:

    def __init__(self, eng, sem):
        self.eng, self.sem, self.base, self.k = eng, sem, 0, 0

    def add(self, ins):
        ins.then_inc(self.sem, 1)
        self.k += 1

    def sync(self):
        self.eng.wait_ge(self.sem, self.base + self.k)

    def link(self, ins):
        self.add(ins)
        self.sync()

    def loop(self, start, stop, per, body):
        base, k = self.base, self.k
        with self.eng.Fori(start, stop) as i:
            self.base, self.k = i * per + (base + (k - start * per)), 0
            body(i)
            assert self.k == per, f"{self.sem}: a body counts {self.k}, not {per}"
        self.base, self.k = base, k + (stop - start) * per


def build(nc, node_table, x_dense, edge_table, index_chunks, src_cols, src_rows, cf_in, ch_in, w1, b1, w2t, b2,
          g1t, gb1, g2t, gb2, embt, adaptt, gamma, beta, out):
    with ExitStack() as ctx:
        def sb(name, shape, dt=F32):
            return ctx.enter_context(nc.sbuf_tensor(name, shape, dt))

        def sem(name):
            return ctx.enter_context(nc.semaphore(name))

        def sems(name):
            return [sem(f"{name}{u}") for u in range(2)]

        def dram(name, shape, dt=F32):
            return nc.dram_tensor(name, shape, dt).ap()

        d_hilo = dram("d_hilo", (2, EPAD), F16)
        d_src = dram("d_src", (1, EPAD))
        d_ptr = dram("d_ptr", (NPAD, 1))
        d_sorted = dram("d_sorted", (EPAD, REC))
        d_table = [dram(f"d_table{b}", (EPAD, FW)) for b in range(2)]
        d_pref = [dram(f"d_pref{l}", (P, TILES * FW)) for l in range(4)]
        d_y = [dram(f"d_y{b}", (P, TILES * F)) for b in range(2)]
        d_gate = dram("d_gate", (P, TILES * F))
        sorted_pt = d_sorted.rearrange("(p t) c -> p t c", t=TILES)
        table_pt = [t.rearrange("(p t) c -> p (t c)", t=TILES) for t in d_table]

        cf = sb("cf", [P, K_W])
        cj = sb("cj", [P, J_W], F16)
        ident = cf[:, K_ID:K_ID + P]
        ident16 = cj[:, J_ID:J_ID + P]
        part0 = cf[:, K_PART:K_PART + 1]
        delta = cf[0:CH, K_DELTA:K_DELTA + CH]
        src_i = sb("src_i", [P, TILES], I32)
        src_f = sb("src_f", [P, TILES])
        hi_c = sb("hi_c", [P, TILES])
        lo_c = sb("lo_c", [P, TILES])
        col_i = sb("col_i", [P, 2, TILES], I32)
        w_sb = sb("w_sb", [F, 2, F])
        g1t_sb = sb("g1t_sb", [R_ATTR, H])
        g2t_sb = sb("g2t_sb", [H, F])
        gb1_sb = sb("gb1_sb", [H, 1])
        rows48 = sb("rows48", [P, 6, F])
        embt_sb = sb("embt_sb", [EMB, NTYPE])
        adaptt_sb = sb("adaptt_sb", [EMB, EMB])
        vt_sb = sb("vt_sb", [EMB, NTYPE])
        tab_sb = sb("tab_sb", [NTYPE, NTYPE])
        eps_c = sb("eps_c", [P, 2])
        same = sb("same", [P, TILES * P])

        def arena16(at, n):
            return same[:, at:at + n // 2].bitcast(F16)

        oht = [arena16(b * 3136, GR * BINS) for b in range(2)]
        ohh = [arena16(6272 + b * 3136, GR * BINS) for b in range(2)]
        ohl = [arena16(12544 + b * 448, GR * P) for b in range(2)]
        hi_b = [arena16(13440 + b * 448, GC) for b in range(2)]
        lo_b = [arena16(14336 + b * 448, GC) for b in range(2)]
        src_b = [same[:, 15232 + b * GC:15232 + (b + 1) * GC] for b in range(2)]
        hit = [same[:, 17024 + b * GC:17024 + (b + 1) * GC] for b in range(2)]
        tab_a = [arena16(18816 + b * 448, BINS) for b in range(2)]
        tab_b = [arena16(19712 + b * 448, BINS) for b in range(2)]
        junk = arena16(20608, 28 * P)
        base_a, base_b = arena16(22400, BINS), arena16(22848, BINS)
        zero16 = arena16(23296, 512)
        cnt, incl, base, ones_w = (same[:, k * BINS:(k + 1) * BINS] for k in range(4))
        last_i, low_i, high_i = (same[:, (4 + k) * BINS:(5 + k) * BINS].bitcast(I32) for k in range(3))
        empty_f, qf = (same[:, 17024 + k * BINS:17024 + (k + 1) * BINS] for k in range(2))
        ptr_i = same[:, 15232:15232 + BINS].bitcast(I32)

        off_c = sb("off_c", [P, 1])
        eqs = sb("eqs", [P, 2, GR])
        rank_i = sb("rank_i", [P, 3, GR], I32)
        qidx = sb("qidx", [P, 2, CH], I32)
        idx = sb("idx", [P, 2, 2 * CH], I32)
        shared = sb("shared", [P, 2 * CH * (FW + XW + F)])
        rec = shared[:, 0:2 * CH * REC].rearrange("p (u t c) -> p u t c", u=2, t=CH)
        o1, o2 = 2 * CH * FW, 2 * CH * (FW + XW)
        stage = shared[:, 0:o1].rearrange("p (u t c) -> p u t c", u=2, t=CH)
        msg_f = shared[:, o1:o2].rearrange("p (u x) -> p u x", u=2)
        yb = shared[:, o2:o2 + 2 * CH * F].rearrange("p (u t c) -> p u t c", u=2, t=CH)
        key = sb("key", [P, TILES + 2])
        wcol = sb("wcol", [P, TILES])
        ptr = sb("ptr", [P, TILES], I32)
        vec_d = sb("vec_d", [P, TILES])
        typ_s = sb("typ_s", [P, TILES])
        first_k = sb("first_k", [P, TILES])
        last_k = sb("last_k", [P, TILES + 1])
        chainf = sb("chainf", [P, TILES])
        chaint = sb("chaint", [P, TILES])
        cwmj = sb("cwmj", [P, TILES])
        cw_i = sb("cw_i", [P, TILES], I32)
        cw_t = sb("cw_t", [P, 3, TILES])
        out_i = sb("out_i", [P, TILES], I32)
        coef = sb("coef", [P, TILES])
        dis = sb("dis", [P, TILES])
        rtot = sb("rtot", [P, TILES])
        small = sb("small", [P, 4, CH])
        logit = sb("logit", [P, 2, GR])
        edgec = sb("edgec", [CH, 3])
        cont_m = sb("cont_m", [CH, CHUNKS * P])
        state = sb("state", [XW, 2, CH + 1])
        cont_s = sb("cont_s", [CH, 2, P])
        key_s = sb("key_s", [P, 2, CH + 1])
        typ_f = sb("typ_f", [P, 2, CH])
        ob = sb("ob", [P, 2, CH, FW])
        gb = sb("gb", [P, 2, CH, F])
        cm = sb("cm", [CH, 2, CH * XW])
        aggt = sb("aggt", [XW, CH * P])
        lnb = sb("lnb", [P, 3, CH, F])
        lns = sb("lns", [P, 4, CH])
        pidx = sb("pidx", [P, 2, CH], I32)
        unit = sb("unit", [P, CH * (4 * F + 4 * FW)])
        rows_i = unit[0:TILES // 2, 0:6 * P].bitcast(I32).rearrange("p (k c) -> p k c", k=3)
        rows_h = unit[0:TILES // 2, 6 * P:8 * P].bitcast(F16).rearrange("p (k c) -> p k c", k=2)
        rows_f = unit[0:TILES // 2, 8 * P:10 * P]
        ux = unit[:, 0:CH * F].rearrange("p (t c) -> p t c", c=F)
        unb = unit[:, CH * F:4 * CH * F].rearrange("p (k t c) -> p k t c", k=3, c=F)
        uo = unit[:, 4 * CH * F:].rearrange("p (k t c) -> p k t c", k=4, c=FW)
        uns = sb("uns", [P, 4, CH])
        attr_t = unit[0:R_ATTR, 0:GC]
        h1_t = unit[0:H, GC:2 * GC]
        oh_td = unit[:, 2 * GC:3 * GC]
        ujunk = unit[:, 3 * GC:3 * GC + GR * NTYPE].rearrange("p (k c) -> p k c", c=NTYPE)
        gst = unit[:, 3 * GC + GR * NTYPE:3 * GC + GR * NTYPE + 2 * GR * F].rearrange("p (u t c) -> p u t c", u=2, c=F)

        ps = ctx.enter_context(nc.psum_tensor("ps", [P, 8 * 512], F32))

        def bank(b, n=512, parts=P, at=0):
            return ps[0:parts, b * 512 + at:b * 512 + at + n]

        s_settled = sem("s_settled")
        s_const, s_eps, s_rows, s_hilo_w, s_src = sem("s_const"), sem("s_eps"), sem("s_rows"), sem("s_hilo_w"), sem("s_src")
        s_zero, s_seed, s_oh, s_hist = sem("s_zero"), sem("s_seed"), sems("s_oh"), sems("s_hist")
        s_incl, s_off, s_base, s_seed2, s_ptr, s_ptrw = (sem(n) for n in ("s_incl", "s_off", "s_base", "s_seed2", "s_ptr", "s_ptrw"))
        s_bc, s_oht, s_ohh, s_eq = sems("s_bc"), sems("s_oht"), sems("s_ohh"), sems("s_eq")
        s_ta, s_tb, s_look, s_upd = sems("s_ta"), sems("s_tb"), sems("s_look"), sems("s_upd")
        s_hit, s_sum, s_q, s_qh = sems("s_hit"), sems("s_sum"), sems("s_q"), sems("s_qh")
        s_idx, s_gath, s_edge, s_keyc, s_scat = sems("s_idx"), sems("s_gath"), sems("s_edge"), sems("s_keyc"), sems("s_scat")
        s_clear = sem("s_clear")
        s_own_v, s_own_p = sem("s_own_v"), sem("s_own_p")
        s_rec, s_cols, s_pref, s_prefw = sems("s_rec"), sems("s_cols"), sems("s_pref"), sems("s_prefw")
        s_kb, s_same, s_kt, s_cont = sem("s_kb"), sem("s_same"), sem("s_kt"), sem("s_cont")
        s_tdb, s_ohtd, s_u, s_logit = sem("s_tdb"), sem("s_ohtd"), sem("s_u"), sem("s_logit")
        s_at, s_atc, s_h1, s_h1s, s_gate, s_gst, s_gw = sem("s_at"), sem("s_atc"), sem("s_h1"), sem("s_h1s"), sem("s_gate"), sem("s_gst"), sems("s_gw")
        s_vt, s_vtc, s_tab, s_tabc = sem("s_vt"), sem("s_vtc"), sem("s_tab"), sem("s_tabc")
        s_next, s_outi, s_ang, s_sin, s_flags = sem("s_next"), sem("s_outi"), sem("s_ang"), sem("s_sin"), sem("s_flags")
        s_st, s_y, s_g = sems("s_st"), sems("s_y"), sems("s_g")
        s_pidx, s_gat = sems("s_pidx"), sems("s_gat")
        s_msg, s_tail, s_state, s_stt, s_cm, s_agg = sems("s_msg"), sems("s_tail"), sems("s_state"), sems("s_stt"), sems("s_cm"), sems("s_agg")
        s_out, s_outw, s_yo = sems("s_out"), sems("s_outw"), sems("s_yo")
        s_aggt, s_conts = sems("s_aggt"), sems("s_conts")
        ln_chunk = (sem("s_cen"), sem("s_sq"), sem("s_var"), sem("s_sd"), lnb, lns)
        ln_unit = (sem("s_ucen"), sem("s_usq"), sem("s_uvar"), sem("s_usd"), unb, uns)
        s_cnt, s_rt = sem("s_cnt"), sem("s_rt")
        s_ux, s_uo, s_uow, s_ufree = sem("s_ux"), sem("s_uo"), sem("s_uow"), sem("s_ufree")
        s_last, s_final = sems("s_last"), sems("s_final")

        block = ctx.enter_context(nc.Block())
        consts = [(cf[:], cf_in), (cj[:], ch_in), (src_i[:], src_cols), (rows_i[:, 0, :], src_rows),
                  (w_sb[:, 0, :], w1), (w_sb[:, 1, :], w2t), (g1t_sb[:], g1t), (g2t_sb[:], g2t), (gb1_sb[:], gb1),
                  (rows48[:, 0, :], b1.partition_broadcast(P)), (rows48[:, 1, :], b2.partition_broadcast(P)),
                  (rows48[:, 2, :], gb2.partition_broadcast(P)), (rows48[:, 3, :], gamma.partition_broadcast(P)),
                  (rows48[:, 4, :], beta.partition_broadcast(P)), (embt_sb[:], embt), (adaptt_sb[:], adaptt)]
        N_CONST = 16 * len(consts)

        FIRST, STEP, LAST, LAYER1, LAYER2, LAYER3 = range(6)
        STEPS = K_STEPS - 2
        EDGE_LN, DENSE_LN = 3, 5
        SCAT_ALL = BODIES * CH * 16
        UOW_ALL = (STEPS * BODIES + 2 * BODIES * EDGE_LN) * 16

        def settled(eng):
            eng.sem_inc(s_settled, 1)

        def peeled(eng, chain, body):
            k0 = chain.k if chain else 0
            body(0, True)
            if chain:
                chain.loop(1, BODIES, chain.k - k0, lambda i: body(i, False))
            else:
                with eng.Fori(1, BODIES) as i:
                    body(i, False)

        def run_passes(eng, chain, per, one, between=None):
            def rolled(kind, p, half):
                if between:
                    between(kind, p, half)
                if chain:
                    chain.loop(0, BODIES, per[kind], lambda i: one(kind, p, half, i, False))
                else:
                    with eng.Fori(0, BODIES) as i:
                        one(kind, p, half, i, False)

            peeled(eng, chain, lambda i, first: one(FIRST, 0, 0, i, first))
            if chain:
                chain.loop(0, STEPS // 2, 2 * BODIES * per[STEP],
                           lambda o: [rolled(STEP, o * 2 + (1 + half), half) for half in range(2)])
            else:
                with eng.Fori(0, STEPS // 2) as o:
                    for half in range(2):
                        rolled(STEP, o * 2 + (1 + half), half)
            for n, kind in enumerate((LAST, LAYER1, LAYER2, LAYER3)):
                rolled(kind, K_STEPS - 1 + n, n % 2)

        def ln_of_unit(kind, p, i, j):
            if kind == FIRST:
                return i * EDGE_LN + j
            if kind == STEP:
                return (p * BODIES + i) * DENSE_LN + (BODIES * (EDGE_LN - DENSE_LN) + j)
            return i * EDGE_LN + (BODIES * (EDGE_LN + STEPS * DENSE_LN) + j)

        def ln_of_chunk(kind, i, u, j=0):
            if kind == LAYER3:
                return i * 4 + (6 * BODIES + 2 * u + j)
            return i * 2 + ((kind - LAST) * 2 * BODIES + u)

        def chunk_cols(i, u, width=1, extra=0):
            return bass.ds(i * (2 * CH * width) + (u * CH * width + extra), CH * width)

        @block.sync
        def _(sp):
            for dst, src in consts:
                sp.dma_start(dst, src).then_inc(s_const, 16)
            sp.wait_ge(s_rows, 1)
            for k in range(2):
                sp.dma_start(d_hilo[k].rearrange("(q c) -> q c", c=2 * P), rows_h[:, k, :]).then_inc(s_hilo_w, 16)
            sp.dma_start(d_src[0].rearrange("(q c) -> q c", c=2 * P), rows_f).then_inc(s_hilo_w, 16)
            sp.wait_ge(s_hilo_w, 48)
            sp.wait_ge(s_ptr, 1)
            sp.dma_start(d_ptr.rearrange("(b p l) c -> p b (l c)", b=NB, p=P),
                         ptr_i.bitcast(F32).rearrange("p (b l) -> p b l", b=NB)).then_inc(s_ptrw, 16)
            sp.wait_ge(s_ptrw, 16)

            def rank_loads(i, first):
                for u in range(2):
                    for h in range(2):
                        if not (first and u == 0):
                            sp.wait_ge(s_hit[h], i * 2 + u)
                            sp.wait_ge(s_eq[h], i * 2 + u)
                        at = bass.ds(i * (4 * GC) + (2 * u + h) * GC, GC)
                        sp.dma_start(hi_b[h], d_hilo[0, at].partition_broadcast(P)).then_inc(s_bc[h], 16)
                        sp.dma_start(lo_b[h], d_hilo[1, at].partition_broadcast(P)).then_inc(s_bc[h], 16)
                        sp.dma_start(src_b[h], d_src[0, at].partition_broadcast(P)).then_inc(s_bc[h], 16)
            peeled(sp, None, rank_loads)
            for u in range(2):
                sp.wait_ge(s_scat[u], SCAT_ALL)

            def record_loads(i, first):
                for u in range(2):
                    if not first:
                        sp.wait_ge(s_prefw[u], i * 32)
                        sp.wait_ge(s_pref[u], i)
                        sp.wait_ge(s_cols[u], i)
                        sp.wait_ge(s_at, i * 4 + (2 * u - 2))
                    sp.dma_start(rec[:, u], sorted_pt[:, bass.ds(i * (2 * CH) + u * CH, CH), :]).then_inc(s_rec[u], 16)
            peeled(sp, None, record_loads)
            for u in range(2):
                sp.wait_ge(s_prefw[u], BODIES * 32)
                sp.wait_ge(s_gw[u], 2 * BODIES * 16)
            sp.wait_ge(s_outi, 1)

            def before(kind, p, half):
                if kind >= LAYER1:
                    n = kind - LAYER1
                    if n == 0:
                        sp.wait_ge(s_uow, UOW_ALL)
                    for u in range(2):
                        sp.wait_ge(s_yo[u], (n + 1) * BODIES * 16)

            def pass_loads(kind, p, half, i, first):
                m = p * BODIES + i
                for u in range(2):
                    if not first:
                        sp.wait_ge(s_msg[u], m)
                    tiles = bass.ds(i * (2 * CH) + u * CH, CH)
                    if kind == FIRST:
                        sp.dma_start(stage[:, u, :, 0:F], sorted_pt[:, tiles, 0:F]).then_inc(s_st[u], 16)
                    else:
                        sp.dma_start(stage[:, u].rearrange("p t c -> p (t c)"),
                                     d_pref[max(0, kind - LAST)][:, chunk_cols(i, u, FW)]).then_inc(s_st[u], 16)
                    if kind == LAYER3:
                        sp.wait_ge(s_out[u], m)
                        sp.dma_start(gb[:, u].rearrange("p t c -> p (t c)"),
                                     d_gate[:, chunk_cols(i, u, F)]).then_inc(s_g[u], 16)
                    if not first:
                        sp.wait_ge(s_out[u], m)
                    sp.dma_start(yb[:, u].rearrange("p t c -> p (t c)"),
                                 d_y[kind in (LAYER1, LAYER3)][:, chunk_cols(i, u, F)]).then_inc(s_y[u], 16)
                    if u == 0 and kind <= LAST:
                        if not first:
                            sp.wait_ge(s_ufree, m)
                        if kind == STEP:
                            sp.dma_start(ux.rearrange("p t c -> p (t c)"),
                                         x_dense[:, bass.ds((p * BODIES + i) * (CH * F) + (-BODIES * CH * F), CH * F)]).then_inc(s_ux, 16)
                        else:
                            sp.dma_start(ux, sorted_pt[:, bass.ds(i * CH + (kind == LAST) * BODIES * CH, CH), 0:F]).then_inc(s_ux, 16)
            run_passes(sp, None, None, pass_loads, before)

            for u in range(2):
                sp.wait_ge(s_yo[u], 4 * BODIES * 16)

            def last_rows(i, first):
                for u in range(2):
                    if first:
                        sp.wait_ge(s_out[u], (K_STEPS + 3) * BODIES)
                    else:
                        sp.wait_ge(s_final[u], i * (16 * CH))
                    sp.dma_start(yb[:, u].rearrange("p t c -> p (t c)"), d_y[0][:, chunk_cols(i, u, F)]).then_inc(s_last[u], 16)
            peeled(sp, None, last_rows)

        @block.gpsimd
        def _(pool):
            own = Chain(pool, s_own_p)
            pool.memset(shared[:], 0.0).then_inc(s_clear, 1)
            pool.wait_ge(s_clear, 1)

            def gather(dst, table, index, rows, done):
                pool.indirect_dma_start(dst, None, table, bass.IndirectOffsetOnAxis(ap=index, axis=0),
                                        bounds_check=rows - 1, oob_is_err=False).then_inc(done, 16)

            def scatter(table, index, rows, src, done):
                pool.indirect_dma_start(table, bass.IndirectOffsetOnAxis(ap=index, axis=0), src, None,
                                        bounds_check=rows - 1, oob_is_err=False).then_inc(done, 16)

            def records(i, first):
                for u in range(2):
                    pool.wait_ge(s_idx[u], i * 16 + 16)
                    if not first:
                        pool.wait_ge(s_scat[u], i * (16 * CH))
                    settled(pool)
                    for k in range(CH):
                        gather(rec[:, u, k, 0:NODE_W], node_table, idx[:, u, k:k + 1], NODES, s_gath[u])
                        gather(rec[:, u, k, C_SRCX:C_SRCX + NODE_W], node_table, idx[:, u, CH + k:CH + k + 1], NODES, s_gath[u])
                if first:
                    pool.wait_ge(s_ptrw, 16)
                for u in range(2):
                    settled(pool)
                    for k in range(CH):
                        gather(rec[:, u, k, C_PTR:C_PTR + 1], d_ptr, idx[:, u, k:k + 1], NPAD, s_gath[u])
                for u in range(2):
                    pool.wait_ge(s_gath[u], i * (16 * 3 * CH) + 16 * 3 * CH)
                    pool.wait_ge(s_edge[u], i * 16 + 16)
                    pool.wait_ge(s_keyc[u], i + 1)
                    pool.wait_ge(s_qh[u], i + 1)
                    settled(pool)
                    for k in range(CH):
                        scatter(d_sorted, qidx[:, u, k:k + 1], EPAD, rec[:, u, k, :], s_scat[u])
            peeled(pool, None, records)

            own.add(pool.memset(key[:], -1.0))
            own.add(pool.memset(key_s[:], -1.0))
            own.sync()

            def small_columns(i, first):
                for u in range(2):
                    at = chunk_cols(i, u)
                    pool.wait_ge(s_rec[u], i * 16 + 16)
                    if not first:
                        pool.wait_ge(s_same, i * 4 + (2 * u - 2))
                        pool.wait_ge(s_kt, i * 2 + (u - 1))
                        pool.wait_ge(s_tdb, i * 4 + (2 * u - 2))
                    if not (first and u == 0):
                        settled(pool)
                        own.link(pool.tensor_copy(key_s[:, u, 0:1], key_s[:, 1 - u, CH:CH + 1]))
                    settled(pool)
                    own.add(pool.tensor_copy(key_s[:, u, 1:CH + 1], rec[:, u, :, C_KEY]))
                    own.add(pool.tensor_copy(typ_f[:, u, :], rec[:, u, :, F + 1].bitcast(I32)))
                    own.sync()
                    settled(pool)
                    pool.tensor_copy(key[:, chunk_cols(i, u, 1, 1)], rec[:, u, :, C_KEY])
                    pool.tensor_copy(wcol[:, at], rec[:, u, :, C_W])
                    pool.tensor_copy(ptr[:, at], rec[:, u, :, C_PTR].bitcast(I32))
                    pool.tensor_copy(vec_d[:, at], rec[:, u, :, F])
                    pool.tensor_copy(typ_s[:, at], rec[:, u, :, C_SRCX + F + 1].bitcast(I32)).then_inc(s_cols[u], 1)
            small_columns(0, True)
            own.loop(1, BODIES, 6, lambda i: small_columns(i, False))

            def before(kind, p, half):
                if kind != FIRST:
                    for u in range(2):
                        pool.wait_ge(s_outw[u], p * (16 * BODIES))
                    settled(pool)

            def pass_gathers(kind, p, half, i, first):
                if kind == FIRST:
                    return
                m = p * BODIES + i
                table = half if kind == STEP else (kind - LAST) % 2
                for u in range(2):
                    pool.wait_ge(s_msg[u], m)
                    settled(pool)
                    pool.tensor_copy(pidx[:, u, :], ptr[:, chunk_cols(i, u)]).then_inc(s_pidx[u], 1)
                    pool.wait_ge(s_pidx[u], m + (1 - BODIES))
                    pool.wait_ge(s_st[u], m * 16 + 16)
                    settled(pool)
                    for k in range(CH):
                        gather(stage[:, u, k, :], d_table[table], pidx[:, u, k:k + 1], EPAD, s_gat[u])

            with pool.Fori(0, STEPS // 2) as o:
                for half in range(2):
                    before(STEP, o * 2 + (1 + half), half)
                    with pool.Fori(0, BODIES) as i:
                        pass_gathers(STEP, o * 2 + (1 + half), half, i, False)
            for n, kind in enumerate((LAST, LAYER1, LAYER2, LAYER3)):
                before(kind, K_STEPS - 1 + n, 0)
                with pool.Fori(0, BODIES) as i:
                    pass_gathers(kind, K_STEPS - 1 + n, 0, i, False)

            pool.wait_ge(s_outi, 1)
            pool.wait_ge(s_uow, UOW_ALL)

            def final_rows(i, first):
                for u in range(2):
                    if not first:
                        pool.wait_ge(s_final[u], i * (16 * CH))
                    else:
                        pool.wait_ge(s_msg[u], (K_STEPS + 3) * BODIES)
                    settled(pool)
                    pool.tensor_copy(pidx[:, u, :], out_i[:, chunk_cols(i, u)]).then_inc(s_pidx[u], 1)
                    pool.wait_ge(s_pidx[u], i + ((K_STEPS + 2) * BODIES + 1))
                    pool.wait_ge(s_last[u], i * 16 + 16)
                    settled(pool)
                    for k in range(CH):
                        scatter(out, pidx[:, u, k:k + 1], NODES, yb[:, u, k, :], s_final[u])
            peeled(pool, None, final_rows)
            for u in range(2):
                pool.wait_ge(s_final[u], SCAT_ALL)

        @block.scalar
        def _(act):
            act.wait_ge(s_vt, 1)
            nc.scalar.copy(vt_sb[:], bank(7, NTYPE, EMB)).then_inc(s_vtc, 1)
            act.wait_ge(s_clear, 1)

            def group_tables(i, first):
                for u in range(2):
                    if not first:
                        act.wait_ge(s_scat[u], i * (16 * CH))
                    act.dma_start(idx[:, u, :], index_chunks[:, chunk_cols(i, u, 2)]).then_inc(s_idx[u], 16)
                    act.dma_start(rec[:, u, :, C_ATTR:C_ATTR + EDGE_W],
                                  edge_table[:, chunk_cols(i, u, EDGE_W)].rearrange("p (t c) -> p t c", c=EDGE_W)).then_inc(s_edge[u], 16)
                    if first and u == 0:
                        act.wait_ge(s_src, 1)
                    nc.scalar.copy(rec[:, u, :, C_KEY], src_f[:, chunk_cols(i, u)]).then_inc(s_keyc[u], 1)
                for u in range(2):
                    for h in range(2):
                        n = i * 2 + u
                        if h == 1:
                            act.wait_ge(s_upd[0], n + 1)
                        elif first and u == 0:
                            act.wait_ge(s_seed2, 1)
                        else:
                            act.wait_ge(s_upd[1], n)
                        if not (first and u == 0):
                            act.wait_ge(s_look[h], n)
                        nc.scalar.copy(tab_a[h], ps[:, 0:BINS]).then_inc(s_ta[h], 1)
            peeled(act, None, group_tables)

            def act_gates(i, first):
                for u in range(2):
                    act.wait_ge(s_rec[u], i * 16 + 16)
                    if not first:
                        act.wait_ge(s_prefw[u], i * 32)
                    nc.scalar.mul(ob[:, u, :, 0:F], rec[:, u, :, 0:F], ALPHA).then_inc(s_pref[u], 1)
                    act.wait_ge(s_pref[u], i + 1)
                    act.dma_start(d_pref[0][:, chunk_cols(i, u, FW)], ob[:, u].rearrange("p t c -> p (t c)")).then_inc(s_prefw[u], 16)
                    act.dma_start(d_y[0][:, chunk_cols(i, u, F)].rearrange("p (t c) -> p t c", c=F),
                                  rec[:, u, :, C_SRCX:C_SRCX + F]).then_inc(s_prefw[u], 16)
                    for h in range(2):
                        q = i * 4 + (2 * u + h)
                        free = not (first and u == 0 and h == 0)
                        act.wait_ge(s_at, q + 1)
                        if free:
                            act.wait_ge(s_h1, q)
                        nc.scalar.copy(attr_t, bank(4, GC, R_ATTR)).then_inc(s_atc, 1)
                        act.wait_ge(s_h1, q + 1)
                        if free:
                            act.wait_ge(s_gate, q)
                        nc.scalar.activation(h1_t, bank(6, GC, H), ACT.Silu, bias=gb1_sb[:, 0:1]).then_inc(s_h1s, 1)
                        act.wait_ge(s_gst, q + 1)
                        act.dma_start(d_gate[:, bass.ds(i * (4 * GR * F) + (2 * u + h) * GR * F, GR * F)],
                                      gst[:, h].rearrange("p t c -> p (t c)")).then_inc(s_gw[h], 16)
            act.wait_ge(s_tab, 1)
            nc.scalar.copy(tab_sb[:], bank(7, NTYPE, NTYPE, 128)).then_inc(s_tabc, 1)
            act.wait_ge(s_const, N_CONST)
            act.wait_ge(s_eps, 1)
            peeled(act, None, act_gates)
            act.wait_ge(s_ang, 1)
            nc.scalar.activation(cw_t[:, 2, :], cw_t[:, 1, :], ACT.Sin, bias=eps_c[:, 1:2], scale=-float(np.pi) / CUTOFF).then_inc(s_sin, 1)

            def square(ln, n):
                cen, sq, _, _, buf, _ = ln
                act.wait_ge(cen, n + 1)
                nc.scalar.activation(buf[:, 1], buf[:, 0], ACT.Square).then_inc(sq, 1)

            def root(ln, n):
                _, _, var, sd, _, st = ln
                act.wait_ge(var, n + 1)
                nc.scalar.activation(st[:, 2], st[:, 1], ACT.Sqrt, bias=eps_c[:, 0:1], scale=1.0 / F).then_inc(sd, 1)

            def act_pass(kind, p, half, i, first):
                m = p * BODIES + i

                def unit_ln(j):
                    if kind <= LAST:
                        square(ln_unit, ln_of_unit(kind, p, i, j))
                        root(ln_unit, ln_of_unit(kind, p, i, j))

                def chunk_end(u):
                    if kind == FIRST:
                        act.wait_ge(s_cnt, m * 2 + (u + 1))
                        nc.scalar.activation(small[:, 1], small[:, 0], ACT.Sqrt).then_inc(s_rt, 1)
                    if kind >= LAST:
                        for j in range(2 if kind == LAYER3 else 1):
                            square(ln_chunk, ln_of_chunk(kind, i, u, j))
                            root(ln_chunk, ln_of_chunk(kind, i, u, j))

                def sums(u):
                    width = XW if kind == FIRST else F
                    if not first:
                        act.wait_ge(s_agg[u], m)
                    nc.scalar.copy(cont_s[:, u, :], cont_m[:, bass.ds(i * (2 * P) + u * P, P)]).then_inc(s_conts[u], 1)
                    act.wait_ge(s_tail[u], m + 1)
                    if not (first and u == 0):
                        act.wait_ge(s_agg[1 - u], m + u)
                    nc.scalar.copy(aggt[0:width, :], ps[0:width, 0:CH * P]).then_inc(s_aggt[u], 1)

                def store(u):
                    act.wait_ge(s_out[u], m + 1)
                    if kind != LAYER3:
                        table = (half + 1) % 2 if kind == STEP else {FIRST: 0, LAST: 1, LAYER1: 0, LAYER2: 1}[kind]
                        act.dma_start(table_pt[table][:, chunk_cols(i, u, FW)], ob[:, u].rearrange("p t c -> p (t c)")).then_inc(s_outw[u], 16)
                    if kind >= LAST:
                        act.dma_start(d_y[kind in (LAST, LAYER2)][:, chunk_cols(i, u, F)].rearrange("p (t c) -> p t c", c=F),
                                      ob[:, u, :, 0:F]).then_inc(s_yo[u], 16)

                def store_unit():
                    act.wait_ge(s_uo, m + 1)
                    if kind == STEP:
                        act.dma_start(out_dense[:, bass.ds((p * BODIES + i) * (CH * F) + (-BODIES * CH * F), CH * F)].rearrange("p (t c) -> p t c", c=F),
                                      uo[:, 3, :, 0:F]).then_inc(s_uow, 16)
                    else:
                        at = bass.ds(i * (CH * FW) + (kind == LAST) * BODIES * CH * FW, CH * FW)
                        for l in range(EDGE_LN):
                            act.dma_start(d_pref[l + 1][:, at], uo[:, l].rearrange("p t c -> p (t c)")).then_inc(s_uow, 16)

                sums(0)
                unit_ln(0)
                chunk_end(0)
                store(0)
                unit_ln(1)
                if kind == STEP:
                    unit_ln(2)
                    sums(1)
                    unit_ln(3)
                    chunk_end(1)
                    store(1)
                    unit_ln(4)
                    store_unit()
                else:
                    sums(1)
                    unit_ln(2)
                    chunk_end(1)
                    store(1)
                    if kind <= LAST:
                        store_unit()
            out_dense = out[0:P * DROWS].rearrange("(p t) c -> p (t c)", p=P)
            run_passes(act, None, None, act_pass)

        @block.vector
        def _(dve):
            own = Chain(dve, s_own_v)
            v = nc.vector

            v.memset(eps_c[:, 0:1], EPS)
            v.memset(eps_c[:, 1:2], float(np.pi) / 2).then_inc(s_eps, 1)
            v.memset(zero16, 0.0).then_inc(s_zero, 1)
            own.add(v.memset(ob[:], 0.0))
            own.add(v.memset(state[:], 0.0))
            own.add(v.memset(last_k[:], -1.0))
            dve.wait_ge(s_const, N_CONST)
            own.add(v.tensor_scalar(rows_i[:, 1, :], rows_i[:, 0, :], 7, None, ALU.arith_shift_right))
            own.add(v.tensor_scalar(rows_i[:, 2, :], rows_i[:, 0, :], P - 1, None, ALU.bitwise_and))
            own.sync()
            own.add(v.tensor_copy(rows_h, rows_i[:, 1:3, :]))
            own.add(v.tensor_scalar(rows48[:, 5, :], rows48[:, 1, :], 0.0, None, ALU.max))
            own.sync()
            v.tensor_copy(rows_f, rows_i[:, 0, :]).then_inc(s_rows, 1)
            own.add(v.tensor_scalar(col_i[:, 0, :], src_i[:], 7, None, ALU.arith_shift_right))
            own.add(v.tensor_scalar(col_i[:, 1, :], src_i[:], P - 1, None, ALU.bitwise_and))
            own.sync()
            own.add(v.tensor_copy(hi_c[:], col_i[:, 0, :]))
            own.add(v.tensor_copy(lo_c[:], col_i[:, 1, :]))
            own.sync()
            v.tensor_copy(src_f[:], src_i[:]).then_inc(s_src, 1)
            iota = cj[:, J_IOTA:J_IOTA + BINS]

            def one_hots(h, first_tile, last_sem):
                for k in range(GR):
                    col = bass.ds(first_tile + k, 1) if not isinstance(first_tile, int) else slice(first_tile + k, first_tile + k + 1)
                    v.tensor_scalar(ohh[h][:, k * BINS:(k + 1) * BINS], iota, hi_c[:, col], None, ALU.is_equal)
                    ins = v.tensor_scalar(ohl[h][:, k * P:(k + 1) * P], iota[:, 0:P], lo_c[:, col], None, ALU.is_equal)
                ins.then_inc(last_sem, 1)

            def histogram(i, first):
                for u in range(2):
                    for h in range(2):
                        if not (first and u == 0):
                            dve.wait_ge(s_hist[h], i * 2 + u)
                        one_hots(h, i * (2 * CH) + (u * CH + h * GR), s_oh[h])
            peeled(dve, None, histogram)

            for h in range(2):
                dve.wait_ge(s_hist[h], 2 * BODIES)
            own.add(v.tensor_copy(cnt, ps[:, 0:BINS]))
            own.add(v.memset(ones_w, 1.0))
            own.sync()
            v.tensor_tensor_scan(incl, ones_w, cnt, 0.0, ALU.mult, ALU.add).then_inc(s_incl, 1)
            dve.wait_ge(s_off, 1)
            own.link(v.tensor_copy(off_c[:], bank(2, 1)))
            own.link(v.scalar_tensor_tensor(base, incl, off_c[:, 0:1], cnt, ALU.add, ALU.subtract))
            own.link(v.tensor_copy(base_a, base))
            v.tensor_tensor(base_b, base, base_a, ALU.subtract).then_inc(s_base, 1)
            own.link(v.scalar_tensor_tensor(last_i, base, -1.0, cnt, ALU.add, ALU.add))
            own.add(v.tensor_scalar(low_i, last_i, P - 1, None, ALU.bitwise_and))
            own.add(v.tensor_scalar(high_i, last_i, 7, None, ALU.arith_shift_right))
            own.add(v.tensor_scalar(empty_f, cnt, 0.0, FAR, ALU.is_equal, ALU.mult))
            own.sync()
            own.link(v.scalar_tensor_tensor(qf, low_i, float(TILES), high_i, ALU.mult, ALU.add))
            v.tensor_tensor(ptr_i, qf, empty_f, ALU.add).then_inc(s_ptr, 1)
            dve.wait_ge(s_ptr, 1)
            dve.wait_ge(s_seed2, 1)

            def ranks(i, first):
                for u in range(2):
                    for h in range(2):
                        n = i * 2 + u
                        fresh = first and u == 0
                        dve.wait_ge(s_bc[h], n * 48 + 48)
                        if not fresh:
                            dve.wait_ge(s_look[h], n)
                            dve.wait_ge(s_upd[h], n)
                        for b in range(NB):
                            ins = v.tensor_scalar(oht[h][:, b * GC:(b + 1) * GC], hi_b[h], cf[:, K_PART + b:K_PART + b + 1], None, ALU.is_equal)
                        ins.then_inc(s_oht[h], 1)
                        one_hots(h, i * (2 * CH) + (u * CH + h * GR), s_ohh[h])
                        dve.wait_ge(s_ta[h], n + 1)
                        v.tensor_tensor(tab_b[h], ps[:, 0:BINS], tab_a[h], ALU.subtract).then_inc(s_tb[h], 1)
                        if not (fresh and h == 0):
                            dve.wait_ge(s_eq[1 - h], n + (h if True else 0))
                        for k in range(GR):
                            w = (k + 1) * P
                            at = (k * (k + 1) // 2) * P
                            col = bass.ds(i * (2 * CH) + (u * CH + h * GR + k), 1)
                            ins = v.scalar_tensor_tensor(junk[:, at:at + w], src_b[h][:, 0:w], src_f[:, col],
                                                         cj[:, J_EARLIER + GC - w:J_EARLIER + GC], ALU.is_equal, ALU.mult,
                                                         accum_out=eqs[:, h, k:k + 1])
                        ins.then_inc(s_eq[h], 1)
                        dve.wait_ge(s_look[h], n + 1)
                        if not fresh:
                            dve.wait_ge(s_sum[h], n)
                        v.scalar_tensor_tensor(hit[h], lo_b[h], part0, ps[:, (2 + 2 * h) * 512:(2 + 2 * h) * 512 + GC],
                                               ALU.is_equal, ALU.mult).then_inc(s_hit[h], 1)
                        dve.wait_ge(s_sum[h], n + 1)
                        dve.wait_ge(s_eq[h], n + 1)
                        v.tensor_tensor(rank_i[:, 0, :], bank(6 + h, GR), eqs[:, h, :], ALU.add).then_inc(s_q[h], 1)
                        dve.wait_ge(s_q[h], n + 1)
                        own.add(v.tensor_scalar(rank_i[:, 1, :], rank_i[:, 0, :], P - 1, None, ALU.bitwise_and))
                        own.add(v.tensor_scalar(rank_i[:, 2, :], rank_i[:, 0, :], 7, None, ALU.arith_shift_right))
                        own.sync()
                        if h == 0 and not first:
                            dve.wait_ge(s_scat[u], i * (16 * CH))
                        ins = v.scalar_tensor_tensor(qidx[:, u, h * GR:(h + 1) * GR], rank_i[:, 1, :], float(TILES),
                                                     rank_i[:, 2, :], ALU.mult, ALU.add)
                        if h == 0:
                            own.link(ins)
                        else:
                            ins.then_inc(s_qh[u], 1)
                            dve.wait_ge(s_qh[u], i + 1)
            peeled(dve, own, ranks)

            dve.wait_ge(s_own_p, 2)

            def gates(i, first):
                for u in range(2):
                    for h in range(2):
                        q = i * 4 + (2 * u + h)
                        fresh = first and u == 0 and h == 0
                        t0 = i * (2 * CH) + (u * CH + h * GR)
                        dve.wait_ge(s_kb, q + 1)
                        kb = ps[:, 0:GC].rearrange("p (k c) -> p k c", c=P)
                        own.add(v.tensor_copy(first_k[:, bass.ds(t0, GR)], kb[:, :, 0]))
                        own.add(v.tensor_copy(last_k[:, bass.ds(t0 + 1, GR)], kb[:, :, P - 1]))
                        v.tensor_tensor(same[:, bass.ds(t0 * P, GC)].rearrange("p (k c) -> p k c", c=P), kb,
                                        key[:, bass.ds(t0 + 1, GR)].unsqueeze(2).broadcast_to([P, GR, P]),
                                        ALU.is_equal).then_inc(s_same, 1)
                        dve.wait_ge(s_tdb, q + 1)
                        if not fresh:
                            dve.wait_ge(s_u, q)
                        v.tensor_scalar(oh_td, ps[:, 1024:1024 + GC], part0, None, ALU.is_equal).then_inc(s_ohtd, 1)
                        if h == 1:
                            dve.wait_ge(s_kt, i * 2 + (u + 1))
                            own.add(v.tensor_copy(edgec[:, 0:1], bank(0, 1, CH)))
                            own.add(v.tensor_copy(edgec[:, 1:2], bank(1, 1, CH, P - 1)))
                            own.sync()
                            own.link(v.tensor_tensor(edgec[:, 2:3], edgec[:, 0:1], edgec[:, 1:2], ALU.is_equal))
                            v.tensor_scalar(cont_m[:, bass.ds(i * (2 * P) + u * P, P)], bank(0, P, CH), edgec[:, 0:1], edgec[:, 2:3],
                                            ALU.is_equal, ALU.mult).then_inc(s_cont, 1)
                            dve.wait_ge(s_cont, i * 2 + (u + 1))
                        dve.wait_ge(s_u, q + 1)
                        if not fresh:
                            dve.wait_ge(s_logit, q)
                            dve.wait_ge(s_gst, q)
                        for k in range(GR):
                            at = 1024 + (k * NTYPE if k < 4 else 512 + (k - 4) * NTYPE)
                            ins = v.scalar_tensor_tensor(ujunk[:, k, :], cf[:, K_ROW:K_ROW + NTYPE], typ_s[:, bass.ds(t0 + k, 1)],
                                                         ps[:, at:at + NTYPE], ALU.is_equal, ALU.mult, accum_out=logit[:, h, k:k + 1])
                        ins.then_inc(s_logit, 1)
                        dve.wait_ge(s_gate, q + 1)
                        if not (first and u == 0):
                            dve.wait_ge(s_gw[h], (i * 2 + u) * 16)
                        own.link(v.tensor_tensor(gst[:, h], bank(4, GR * F).rearrange("p (k c) -> p k c", c=F),
                                                 rows48[:, 2:3, :].broadcast_to([P, GR, F]), ALU.add))
                        dve.wait_ge(s_logit, q + 1)
                        v.tensor_tensor(gst[:, h], gst[:, h], logit[:, h, :].unsqueeze(2).broadcast_to([P, GR, F]), ALU.add).then_inc(s_gst, 1)
            peeled(dve, own, gates)

            own.sync()
            own.add(v.tensor_tensor(chainf[:], first_k[:], last_k[:, 1:TILES + 1], ALU.is_equal))
            own.add(v.tensor_tensor(chaint[:], first_k[:], last_k[:, 0:TILES], ALU.is_equal))
            own.sync()
            v.tensor_tensor(chainf[:], chainf[:], chaint[:], ALU.mult).then_inc(s_flags, 1)
            for u in range(2):
                dve.wait_ge(s_cols[u], BODIES)
            own.link(v.tensor_scalar(cw_i[:], wcol[:], 1.0 / (2 * CUTOFF), None, ALU.mult))
            own.link(v.scalar_tensor_tensor(cw_t[:, 0, :], cw_i[:], -2 * CUTOFF, wcol[:], ALU.mult, ALU.add))
            own.link(v.scalar_tensor_tensor(cw_t[:, 1, :], cw_t[:, 0, :], -1.0, cw_t[:, 0, :], ALU.mult, ALU.max))
            own.link(v.tensor_scalar(cw_t[:, 0, :], cw_t[:, 1, :], -CUTOFF, None, ALU.add))
            v.scalar_tensor_tensor(cw_t[:, 1, :], cw_t[:, 0, :], -1.0, cw_t[:, 0, :], ALU.mult, ALU.max).then_inc(s_ang, 1)
            dve.wait_ge(s_sin, 1)
            own.link(v.tensor_scalar(cw_t[:, 0, :], cw_t[:, 2, :], -0.5, 0.5, ALU.mult, ALU.add))
            own.link(v.scalar_tensor_tensor(cw_t[:, 1, :], wcol[:], CUTOFF, cw_t[:, 0, :], ALU.is_lt, ALU.mult))
            own.link(v.tensor_tensor(cwmj[:], cw_t[:, 1, :], vec_d[:], ALU.mult))
            dve.wait_ge(s_next, 1)
            own.link(v.tensor_tensor(cw_t[:, 0, :], bank(0, TILES), key[:, 1:TILES + 1], ALU.is_equal))
            v.scalar_tensor_tensor(out_i[:], cw_t[:, 0, :], FAR, key[:, 1:TILES + 1], ALU.mult, ALU.add).then_inc(s_outi, 1)
            for h in range(2):
                dve.wait_ge(s_gw[h], 2 * BODIES * 16)
            own.link(v.memset(uo, 0.0))

            def center(ln, n, x):
                cen, _, _, _, buf, st = ln
                own.link(v.tensor_reduce(st[:, 0], x, AX_X, ALU.add))
                v.scalar_tensor_tensor(buf[:, 0], st[:, 0].unsqueeze(2).broadcast_to([P, CH, F]), -1.0 / F, x, ALU.mult, ALU.add).then_inc(cen, 1)

            def variance(ln, n):
                _, sq, var, _, buf, st = ln
                dve.wait_ge(sq, n + 1)
                v.tensor_reduce(st[:, 1], buf[:, 1], AX_X, ALU.add).then_inc(var, 1)

            def scaled(ln, n, dst):
                cen, _, _, sd, buf, st = ln
                dve.wait_ge(cen, n + 1)
                dve.wait_ge(sd, n + 1)
                own.link(v.reciprocal(st[:, 3], st[:, 2]))
                return v.tensor_tensor(dst, buf[:, 0], st[:, 3].unsqueeze(2).broadcast_to([P, CH, F]), ALU.mult)

            def row(r):
                return rows48[:, r:r + 1, :].broadcast_to([P, CH, F])

            def agg_of(u, width, lo, hi):
                return ps[:, (4 + 2 * u) * 512:(6 + 2 * u) * 512].rearrange("p (b x) -> p b x", b=2)[:, :, 0:GR * width].rearrange(
                    "p b (t c) -> p b t c", c=width)[:, :, :, lo:hi]

            def halves(ap):
                return ap.rearrange("p (b t) c -> p b t c", b=2)

            def dve_pass(kind, p, half, i, first):
                m = p * BODIES + i
                width = XW if kind == FIRST else F

                def message(u):
                    msg = msg_f[:, u, 0:CH * width].rearrange("p (t c) -> p t c", c=width)
                    at = chunk_cols(i, u)
                    if kind == FIRST:
                        dve.wait_ge(s_st[u], i * 16 + 16)
                    else:
                        dve.wait_ge(s_gat[u], (m - BODIES) * (16 * CH) + 16 * CH if isinstance(m, int) else i * (16 * CH) + p * (16 * CH * BODIES) + (16 * CH - 16 * CH * BODIES))
                    if not first:
                        dve.wait_ge(s_agg[u], m)
                    if kind == FIRST:
                        own.add(v.tensor_copy(msg[:, :, F], wcol[:, at]))
                        own.add(v.memset(msg[:, :, F + 1:F + 2], 1.0))
                        own.add(v.tensor_copy(msg[:, :, F + 2], vec_d[:, at]))
                    x = stage[:, u, :, 0:F]
                    if kind == LAYER3:
                        dve.wait_ge(s_g[u], i * 16 + 16)
                        own.link(v.tensor_tensor(msg, x, gb[:, u], ALU.mult))
                        x = msg
                    scale = {LAYER2: stage[:, u, :, F:FW], LAYER3: cwmj[:, at].unsqueeze(2)}.get(kind, wcol[:, at].unsqueeze(2))
                    v.tensor_tensor(msg[:, :, 0:F], x, scale.broadcast_to([P, CH, F]), ALU.mult).then_inc(s_msg[u], 1)

                def carry(u):
                    dve.wait_ge(s_aggt[u], m + 1)
                    if not first:
                        dve.wait_ge(s_stt[u], m)
                    if not (first and u == 0):
                        dve.wait_ge(s_state[1 - u], m + u)
                        own.link(v.tensor_copy(state[:, u, 0:1], state[:, 1 - u, CH:CH + 1]))
                    else:
                        own.link(v.memset(state[:, u, 0:1], 0.0))
                    v.tensor_tensor_scan(state[0:width, u, 1:CH + 1], chainf[0:width, chunk_cols(i, u)],
                                         aggt[0:width, :].rearrange("p (t c) -> p t c", c=P)[:, :, P - 1],
                                         state[0:width, u, 0:1], ALU.mult, ALU.add).then_inc(s_state[u], 1)

                def spread(u):
                    dve.wait_ge(s_stt[u], m + 1)
                    v.tensor_tensor(cm[:, u, 0:CH * width].rearrange("p (t c) -> p t c", c=width),
                                    ps[0:CH, CH * P:CH * P + width].unsqueeze(1).broadcast_to([CH, CH, width]),
                                    delta.unsqueeze(2).broadcast_to([CH, CH, width]), ALU.mult).then_inc(s_cm[u], 1)

                def finish(u):
                    at = chunk_cols(i, u)
                    dve.wait_ge(s_agg[u], m + 1)
                    dve.wait_ge(s_y[u], m * 16 + 16)
                    if not first and kind != LAYER3:
                        dve.wait_ge(s_outw[u], m * 16)
                    if kind == FIRST and first:
                        dve.wait_ge(s_prefw[u], BODIES * 32)
                    if kind >= LAYER1:
                        dve.wait_ge(s_yo[u], i * 16 + (kind - LAST) * BODIES * 16)
                    if kind == LAYER3:
                        dve.wait_ge(s_outw[u], (K_STEPS + 2) * BODIES * 16)
                    y, o = yb[:, u], ob[:, u, :, 0:F]
                    agg = agg_of(u, width, 0, F)
                    t1 = lnb[:, 2]
                    if kind == FIRST:
                        def per_position(c):
                            return agg_of(u, width, c, c + 1).rearrange("p b t c -> p b (t c)")

                        def pair(ap):
                            return ap.rearrange("p (b t) -> p b t", b=2)
                        v.tensor_copy(pair(small[:, 0]), per_position(F + 1)).then_inc(s_cnt, 1)
                        own.add(v.tensor_scalar(pair(small[:, 2]), per_position(F), 1e-10, None, ALU.add))
                        own.add(v.tensor_scalar(pair(small[:, 3]), per_position(F + 2), 1e-8, None, ALU.max))
                        own.sync()
                        own.add(v.reciprocal(rtot[:, at], small[:, 3]))
                        own.link(v.reciprocal(small[:, 2], small[:, 2]))
                        own.link(v.tensor_scalar(coef[:, at], small[:, 2], 1.0 - ALPHA, None, ALU.mult))
                        dve.wait_ge(s_rt, m * 2 + (u + 1))
                        own.link(v.reciprocal(dis[:, at], small[:, 1]))
                    settled(dve)
                    own.link(v.tensor_copy(ob[:, u, :, F], dis[:, at]))
                    if kind <= LAST:
                        own.link(v.tensor_tensor(halves(t1), agg, halves(coef[:, at].unsqueeze(2).broadcast_to([P, CH, F])), ALU.mult))
                        step = v.scalar_tensor_tensor(o, y, ALPHA, t1, ALU.mult, ALU.add)
                    if kind < LAST:
                        step.then_inc(s_out[u], 1)
                        return
                    if kind == LAST:
                        own.link(step)
                        own.link(v.tensor_tensor(t1, o, y, ALU.add))
                    elif kind in (LAYER1, LAYER2):
                        bias = rows48[:, kind - LAYER1:kind - LAYER1 + 1, :].broadcast_to([P, CH, F])
                        if kind == LAYER1:
                            own.link(v.tensor_tensor(halves(t1), agg, halves(bias), ALU.add))
                        else:
                            own.link(v.tensor_tensor(halves(t1), agg, halves(dis[:, at].unsqueeze(2).broadcast_to([P, CH, F])), ALU.mult))
                            own.link(v.tensor_tensor(t1, t1, bias, ALU.add))
                        if kind == LAYER1:
                            own.link(v.tensor_tensor(t1, t1, y, ALU.add))
                        else:
                            own.link(v.scalar_tensor_tensor(t1, t1, 0.0, y, ALU.max, ALU.add))
                    else:
                        own.link(v.tensor_tensor(halves(t1), agg, halves(rtot[:, at].unsqueeze(2).broadcast_to([P, CH, F])), ALU.mult))
                        own.link(v.tensor_tensor(t1, t1, y, ALU.add))
                        n = ln_of_chunk(kind, i, u, 0)
                        center(ln_chunk, n, t1)
                        variance(ln_chunk, n)
                        own.link(scaled(ln_chunk, n, t1))
                        own.link(v.tensor_tensor(t1, t1, row(3), ALU.mult))
                        own.link(v.tensor_tensor(t1, t1, row(4), ALU.add))
                        own.link(v.tensor_tensor(t1, t1, y, ALU.add))
                    n = ln_of_chunk(kind, i, u, 1 if kind == LAYER3 else 0)
                    center(ln_chunk, n, t1)
                    variance(ln_chunk, n)
                    scaled(ln_chunk, n, o).then_inc(s_out[u], 1)

                def unit_a(j):
                    n = ln_of_unit(kind, p, i, j)
                    t = unb[:, 2]
                    if j == 0:
                        dve.wait_ge(s_ux, m * 16 + 16)
                        v.scalar_tensor_tensor(t, ux, ALPHA, ux, ALU.mult, ALU.add).then_inc(s_ufree, 1)
                        dve.wait_ge(s_ufree, m + 1)
                    elif j < 3:
                        own.link(v.tensor_tensor(t, uo[:, j - 1, :, 0:F], row(0 if j == 1 else 5), ALU.add))
                    elif j == 4:
                        own.link(v.tensor_tensor(t, t, row(3), ALU.mult))
                        own.link(v.tensor_tensor(t, t, row(4), ALU.add))
                        own.link(v.tensor_tensor(t, t, uo[:, 2, :, 0:F], ALU.add))
                    center(ln_unit, n, uo[:, 2, :, 0:F] if j == 3 else t)

                def unit_b(j):
                    variance(ln_unit, ln_of_unit(kind, p, i, j))

                def unit_c(j):
                    n = ln_of_unit(kind, p, i, j)
                    if j == 0 and not first:
                        if kind == FIRST:
                            dve.wait_ge(s_uow, i * (16 * EDGE_LN))
                        elif kind == STEP:
                            dve.wait_ge(s_uow, m * 16 + BODIES * 16 * (EDGE_LN - 1))
                        else:
                            dve.wait_ge(s_uow, i * (16 * EDGE_LN) + BODIES * 16 * (EDGE_LN + STEPS))
                    if j == 3:
                        own.link(scaled(ln_unit, n, unb[:, 2]))
                    elif j == (EDGE_LN if kind != STEP else DENSE_LN) - 1:
                        scaled(ln_unit, n, uo[:, min(j, 3), :, 0:F]).then_inc(s_uo, 1)
                    else:
                        own.link(scaled(ln_unit, n, uo[:, j, :, 0:F]))

                with_unit = kind <= LAST
                if kind == STEP:
                    message(0); unit_a(0); carry(0); unit_b(0); spread(0); unit_c(0); finish(0)
                    unit_a(1); unit_b(1); unit_c(1); unit_a(2); unit_b(2); unit_c(2)
                    message(1); unit_a(3); carry(1); unit_b(3); spread(1); unit_c(3); finish(1)
                    unit_a(4); unit_b(4); unit_c(4)
                elif with_unit:
                    message(0); unit_a(0); carry(0); unit_b(0); spread(0); unit_c(0); finish(0)
                    unit_a(1); unit_b(1); unit_c(1)
                    message(1); unit_a(2); carry(1); unit_b(2); spread(1); unit_c(2); finish(1)
                else:
                    for u in range(2):
                        message(u); carry(u); spread(u); finish(u)
            run_passes(dve, own, DVE_COUNTS, dve_pass)

        @block.tensor
        def _(pe):
            mm = nc.tensor.matmul
            pe.wait_ge(s_const, N_CONST)
            mm(bank(7, NTYPE, EMB), adaptt_sb[:], embt_sb[:], start=True, stop=True).then_inc(s_vt, 1)
            pe.wait_ge(s_vtc, 1)
            pe.wait_ge(s_zero, 1)
            mm(bank(0), ident16, zero16, start=True, stop=True)
            mm(bank(1), ident16, zero16, start=True, stop=True)

            def count_edges(h):
                for k in range(GR):
                    for b in range(NB):
                        ins = mm(ps[:, b * P:(b + 1) * P], ohh[h][:, k * BINS + b * P:k * BINS + (b + 1) * P],
                                 ohl[h][:, k * P:(k + 1) * P], start=False, stop=(k == GR - 1), skip_group_check=True)
                return ins

            def histogram(i, first):
                for u in range(2):
                    for h in range(2):
                        pe.wait_ge(s_oh[h], i * 2 + (u + 1))
                        count_edges(h).then_inc(s_hist[h], 1)
            peeled(pe, None, histogram)
            pe.wait_ge(s_incl, 1)
            mm(bank(2, 1), cf[:, K_BEFORE:K_BEFORE + P], incl[:, BINS - 1:BINS], start=True, stop=True).then_inc(s_off, 1)
            pe.wait_ge(s_base, 1)
            for b, n in ((0, 512), (1, BINS - 512)):
                mm(bank(b, n), ident16, base_a[:, b * 512:b * 512 + n], start=True, stop=False)
                ins = mm(bank(b, n), ident16, base_b[:, b * 512:b * 512 + n], start=False, stop=True)
            ins.then_inc(s_seed2, 1)

            def ranks(i, first):
                for u in range(2):
                    for h in range(2):
                        n = i * 2 + u
                        fresh = first and u == 0
                        pe.wait_ge(s_oht[h], n + 1)
                        pe.wait_ge(s_tb[h], n + 1)
                        if not fresh:
                            pe.wait_ge(s_hit[h], n)
                        for at, w in ((0, 512), (512, GC - 512)):
                            for b in range(NB):
                                for t, tab in enumerate((tab_a[h], tab_b[h])):
                                    ins = mm(ps[:, (2 + 2 * h) * 512 + at:(2 + 2 * h) * 512 + at + w], tab[:, b * P:(b + 1) * P],
                                             oht[h][:, b * GC + at:b * GC + at + w], start=(b == 0 and t == 0), stop=(b == NB - 1 and t == 1))
                        ins.then_inc(s_look[h], 1)
                        pe.wait_ge(s_ohh[h], n + 1)
                        count_edges(h).then_inc(s_upd[h], 1)
                        pe.wait_ge(s_hit[h], n + 1)
                        if not fresh:
                            pe.wait_ge(s_q[h], n)
                        for k in range(GR):
                            ins = mm(bank(6 + h, 1, P, k), hit[h][:, k * P:(k + 1) * P], cf[:, K_ONE:K_ONE + 1], start=True, stop=True)
                        ins.then_inc(s_sum[h], 1)
            peeled(pe, None, ranks)

            for h in range(2):
                pe.wait_ge(s_q[h], 2 * BODIES)
            mm(bank(7, NTYPE, NTYPE, 128), vt_sb[:], embt_sb[:], start=True, stop=True).then_inc(s_tab, 1)
            pe.wait_ge(s_tabc, 1)

            def gates(i, first):
                for u in range(2):
                    for h in range(2):
                        q = i * 4 + (2 * u + h)
                        fresh = first and u == 0 and h == 0
                        t0 = i * (2 * CH) + (u * CH + h * GR)
                        pe.wait_ge(s_cols[u], i + 1)
                        if not fresh:
                            pe.wait_ge(s_same, q)
                            if u + h:
                                pass
                            pe.wait_ge(s_cont, i * 2 + u)
                        for k in range(GR):
                            ins = mm(ps[:, k * P:(k + 1) * P], key_s[:, u, h * GR + k + 1:h * GR + k + 2].broadcast_to([P, P]), ident, start=True, stop=True)
                        ins.then_inc(s_kb, 1)
                        if not fresh:
                            pe.wait_ge(s_logit, q)
                        for k in range(GR):
                            ins = mm(ps[:, 1024 + k * P:1024 + (k + 1) * P], typ_f[:, u, h * GR + k:h * GR + k + 1].broadcast_to([P, P]), ident, start=True, stop=True)
                        ins.then_inc(s_tdb, 1)
                        pe.wait_ge(s_rec[u], i * 16 + 16)
                        if not fresh:
                            pe.wait_ge(s_gst, q)
                            pe.wait_ge(s_atc, q)
                        settled(pe)
                        for k in range(GR):
                            ins = nc.tensor.transpose(ps[0:R_ATTR, 2048 + k * P:2048 + (k + 1) * P],
                                                      rec[:, u, h * GR + k, C_ATTR:C_ATTR + R_ATTR], ident)
                        ins.then_inc(s_at, 1)
                        pe.wait_ge(s_atc, q + 1)
                        if not fresh:
                            pe.wait_ge(s_h1s, q)
                        settled(pe)
                        mm(bank(6, 512, H), g1t_sb[:], attr_t[:, 0:512], start=True, stop=True)
                        mm(bank(7, GC - 512, H), g1t_sb[:], attr_t[:, 512:GC], start=True, stop=True).then_inc(s_h1, 1)
                        if h == 1:
                            pe.wait_ge(s_same, q + 1)
                            settled(pe)
                            nc.tensor.transpose(bank(0, P, CH), key_s[:, u, 1:CH + 1], ident)
                            nc.tensor.transpose(bank(1, P, CH), key_s[:, u, 0:CH], ident).then_inc(s_kt, 1)
                        pe.wait_ge(s_ohtd, q + 1)
                        for k in range(GR):
                            at = 1024 + (k * NTYPE if k < 4 else 512 + (k - 4) * NTYPE)
                            ins = mm(ps[:, at:at + NTYPE], oh_td[0:NTYPE, k * P:(k + 1) * P], tab_sb[:], start=True, stop=True)
                        ins.then_inc(s_u, 1)
                        pe.wait_ge(s_h1s, q + 1)
                        for k in range(GR):
                            ins = mm(ps[:, 2048 + k * F:2048 + (k + 1) * F], h1_t[:, k * P:(k + 1) * P], g2t_sb[:], start=True, stop=True)
                        ins.then_inc(s_gate, 1)
            peeled(pe, None, gates)
            pe.wait_ge(s_same, 2 * CHUNKS)
            pe.wait_ge(s_flags, 1)
            mm(bank(0, TILES), cf[:, K_NEXT:K_NEXT + P], key[:, 1:TILES + 1], start=True, stop=False)
            mm(bank(0, TILES), cf[:, K_NEXTT:K_NEXTT + P], key[:, 2:TILES + 2], start=False, stop=True).then_inc(s_next, 1)
            pe.wait_ge(s_outi, 1)
            pe.wait_ge(s_gst, 2 * CHUNKS)

            def pe_pass(kind, p, half, i, first):
                m = p * BODIES + i
                width = XW if kind == FIRST else F
                through = w_sb[:, kind - LAYER1, :] if kind in (LAYER1, LAYER2) else ident[0:width, 0:width]
                for u in range(2):
                    pe.wait_ge(s_msg[u], m + 1)
                    if not (first and u == 0):
                        pe.wait_ge(s_aggt[1 - u], m + u)
                        pe.wait_ge(s_cm[1 - u], m + u)
                    if not first:
                        pe.wait_ge(s_out[u], m)
                    for k in range(CH):
                        ins = mm(ps[0:width, k * P:(k + 1) * P], msg_f[:, u, k * width:(k + 1) * width],
                                 same[:, bass.ds(i * (2 * CH * P) + (u * CH + k) * P, P)], start=True, stop=True)
                    ins.then_inc(s_tail[u], 1)
                    pe.wait_ge(s_state[u], m + 1)
                    settled(pe)
                    mm(ps[0:CH, CH * P:CH * P + width], state[0:width, u, 0:CH], through, start=True, stop=True).then_inc(s_stt[u], 1)
                    pe.wait_ge(s_aggt[u], m + 1)
                    for k in range(CH):
                        mm(bank(4 + 2 * u + k // GR, width, P, (k % GR) * width), aggt[0:width, k * P:(k + 1) * P], through,
                           start=(k % GR == 0), stop=False)
                    pe.wait_ge(s_cm[u], m + 1)
                    pe.wait_ge(s_conts[u], m + 1)
                    for b in range(2):
                        ins = mm(bank(4 + 2 * u + b, GR * width), cont_s[:, u, :],
                                 cm[:, u, b * GR * width:(b + 1) * GR * width], start=False, stop=True)
                    ins.then_inc(s_agg[u], 1)
            run_passes(pe, None, None, pe_pass)


_OUT = (P * DROWS, F)


def kernel(**inputs):
    import concourse.bacc as bacc
    from concourse.bass_utils import run_bass_kernel_spmd as run

    a = {k: np.asarray(v) for k, v in inputs.items()}
    pad = EPAD - EDGES

    def tiles(x):
        x = np.concatenate([x, np.zeros((pad,) + x.shape[1:], x.dtype)])
        return np.ascontiguousarray(x.reshape(TILES, P, -1).transpose(1, 0, 2).reshape(P, -1))

    spare = np.full(pad, SPARE, a["src"].dtype)
    src, dst = (np.concatenate([a[n], spare]) for n in ("src", "dst"))
    by_chunk = np.stack([x.reshape(CHUNKS, CH, P) for x in (dst, src)], 1)
    x = a["x"]
    f, h = constants()
    arrays = {
        "node_table": np.concatenate([x, a["node_vec"][:, None], a["node_type_119"][:, None].view(np.float32)], 1),
        "x_dense": np.concatenate([x, np.zeros((P * DROWS - NODES, F), x.dtype)]).reshape(P, DROWS * F),
        "edge_table": tiles(np.concatenate([a["edge_attr_40"], a["edge_weight"][:, None]], 1)),
        "index_chunks": np.ascontiguousarray(by_chunk.transpose(3, 0, 1, 2).reshape(P, -1)),
        "src_cols": np.ascontiguousarray(src.reshape(TILES, P).T),
        "src_rows": src.reshape(TILES // 2, 2 * P),
        "const_f": f,
        "const_h": h,
        "w1": a["L1_gnn_weight"],
        "b1": a["L1_gnn_bias"],
        "w2t": np.ascontiguousarray(a["L2_gnn_W"].T),
        "b2": a["L2_gnn_b"],
        "g1t": np.ascontiguousarray(a["L3_gnn_W1"].T),
        "gb1": a["L3_gnn_b1"][:, None],
        "g2t": np.ascontiguousarray(a["L3_gnn_W2"].T),
        "gb2": a["L3_gnn_b2"],
        "embt": np.ascontiguousarray(a["L3_gnn_emb"].T),
        "adaptt": np.ascontiguousarray(a["L3_gnn_adaptW"].T),
        "gamma": a["L3_gnn_gamma"],
        "beta": a["L3_gnn_beta"],
    }
    nc = bacc.Bacc("TRN2", target_bir_lowering=False, num_devices=1)
    arrays = {f"in_{k}": np.ascontiguousarray(v) for k, v in arrays.items()}
    args = [nc.dram_tensor(k, v.shape, mybir.dt.from_np(v.dtype), kind="ExternalInput").ap() for k, v in arrays.items()]
    out = nc.dram_tensor("out", _OUT, F32, kind="ExternalOutput").ap()
    build(nc, *args, out)
    r = run(nc, [arrays], core_ids=[0])
    return r.results[0]["out"][:NODES]
```

```python
from contextlib import ExitStack

import numpy as np

import concourse.bass as bass
from concourse import mybir

P = 128
NODES, EDGES, F = 100000, 25000, 48
TILES = -(-EDGES // P)
EPAD = TILES * P
CH = 14
CHUNKS = TILES // CH
BODIES = CHUNKS // 2
GR = 7
GC = GR * P
NB = -(-NODES // (P * P))
NPAD = NB * P * P
SPARE = NPAD - 1
BINS = NB * P
FAR = 1.0e6
ALPHA, K_STEPS = 0.1, 10
CUTOFF = 6.0
EPS = 1e-5
H, R_ATTR = 48, 40
NTYPE, EMB = 119, 32
FW = F + 1
XW = F + 3
NODE_W = F + 2
EDGE_W = R_ATTR + 1
C_SRCX, C_ATTR, C_W, C_KEY, C_PTR = NODE_W, 2 * NODE_W, 2 * NODE_W + R_ATTR, 2 * NODE_W + R_ATTR + 1, 2 * NODE_W + R_ATTR + 2
REC = C_PTR + 1
DROWS = 784
UNITS = DROWS // CH

CHUNK_COUNTS = [24, 6, 6, 12, 12, 14, 26]
UNIT_COUNTS = [6, 28]

ALU = mybir.AluOpType
ACT = mybir.ActivationFunctionType
F32, F16, I32 = mybir.dt.float32, mybir.dt.float16, mybir.dt.int32
AX_X = mybir.AxisListType.X

K_ID, K_PART, K_NEXT, K_NEXTT, K_BEFORE, K_DELTA, K_ROW, K_ONE = 0, 128, 135, 263, 391, 519, 519 + CH, 647 + CH
K_LIMIT, K_ALL = K_ONE + 1, K_ONE + 1 + BODIES - 2
K_W = K_ALL + P
J_IOTA, J_EARLIER, J_ID = 0, BINS, BINS + GC
J_W = J_ID + P


def constants():
    f = np.zeros((P, K_W), np.float32)
    p = np.arange(P)
    f[p, K_ID + p] = 1.0
    f[:, K_PART:K_PART + NB] = p[:, None] + P * np.arange(NB)
    f[p[1:], K_NEXT + p[:-1]] = 1.0
    f[0, K_NEXTT + P - 1] = 1.0
    f[:, K_BEFORE:K_BEFORE + P] = p[:, None] < p[None, :]
    c = np.arange(CH)
    f[c, K_DELTA + c] = 1.0
    f[:, K_ROW:K_ROW + P] = p[None, :]
    f[:, K_ONE] = 1.0
    f[:, K_LIMIT:K_LIMIT + BODIES - 2] = np.arange(2, BODIES) * (2 * CH * P)
    f[:, K_ALL:K_ALL + P] = 1.0
    h = np.zeros((P, J_W), np.float16)
    h[:, J_IOTA:J_IOTA + BINS] = np.arange(BINS)
    h[:, J_EARLIER:J_EARLIER + GC - P] = 1.0
    h[:, J_EARLIER + GC - P:J_EARLIER + GC] = p[None, :] < p[:, None]
    h[p, J_ID + p] = 1.0
    return f, h


class Chain:

    def __init__(self, eng, sem):
        self.eng, self.sem, self.base, self.k = eng, sem, 0, 0

    def add(self, ins):
        ins.then_inc(self.sem, 1)
        self.k += 1

    def sync(self):
        self.eng.wait_ge(self.sem, self.base + self.k)

    def link(self, ins):
        self.add(ins)
        self.sync()

    def loop(self, start, stop, per, body):
        base, k = self.base, self.k
        with self.eng.Fori(start, stop) as i:
            self.base, self.k = i * per + (base + (k - start * per)), 0
            body(i)
            assert self.k == per, f"{self.sem}: a body counts {self.k}, not {per}"
        self.base, self.k = base, k + (stop - start) * per


def build(nc, node_table, x_dense, edge_table, index_chunks, src_cols, edge_rows, cf_in, ch_in, w1, b1, w2t, b2,
          g1t, gb1, g2t, gb2, embt, adaptt, gamma, beta, out):
    with ExitStack() as ctx:
        def sb(name, shape, dt=F32):
            return ctx.enter_context(nc.sbuf_tensor(name, shape, dt))

        def sem(name):
            return ctx.enter_context(nc.semaphore(name))

        def sems(name):
            return [sem(f"{name}{u}") for u in range(2)]

        def dram(name, shape, dt=F32):
            return nc.dram_tensor(name, shape, dt).ap()

        d_hilo = dram("d_hilo", (2, 2, EPAD), F16)
        d_src = dram("d_src", (1, EPAD))
        d_ptr = dram("d_ptr", (NPAD, 1))
        d_sorted = dram("d_sorted", (EPAD, REC))
        d_table = [dram(f"d_table{b}", (EPAD, FW)) for b in range(3)]
        d_pref = [dram(f"d_pref{l}", (P, TILES * FW)) for l in range(4)]
        d_y = [dram(f"d_y{b}", (P, TILES * F)) for b in range(2)]
        d_gate = dram("d_gate", (P, TILES * F))
        sorted_pt = d_sorted.rearrange("(p t) c -> p t c", t=TILES)
        table_pt = [t.rearrange("(p t) c -> p (t c)", t=TILES) for t in d_table]

        cf = sb("cf", [P, K_W])
        cj = sb("cj", [P, J_W], F16)
        ident = cf[:, K_ID:K_ID + P]
        ident16 = cj[:, J_ID:J_ID + P]
        part0 = cf[:, K_PART:K_PART + 1]
        delta = cf[0:CH, K_DELTA:K_DELTA + CH]
        src_i = sb("src_i", [P, TILES], I32)
        src_f = sb("src_f", [P, TILES])
        hi_c = sb("hi_c", [P, TILES])
        lo_c = sb("lo_c", [P, TILES])
        col_i = sb("col_i", [P, 2, TILES], I32)
        w_sb = sb("w_sb", [F, 2, F])
        g1t_sb = sb("g1t_sb", [R_ATTR, H])
        g2t_sb = sb("g2t_sb", [H, F])
        gb1_sb = sb("gb1_sb", [H, 1])
        rows48 = sb("rows48", [P, 7, F])
        rsum = sb("rsum", [P, 2])
        embt_sb = sb("embt_sb", [EMB, NTYPE])
        adaptt_sb = sb("adaptt_sb", [EMB, EMB])
        vt_sb = sb("vt_sb", [EMB, NTYPE])
        tab_sb = sb("tab_sb", [NTYPE, NTYPE])
        eps_c = sb("eps_c", [P, 3])
        same = sb("same", [P, TILES * P])

        def arena16(at, n):
            return same[:, at:at + n // 2].bitcast(F16)

        oht = [arena16(b * 3136, GR * BINS) for b in range(2)]
        ohh = [arena16(6272 + b * 3136, GR * BINS) for b in range(2)]
        ohl = [arena16(12544 + b * 448, GR * P) for b in range(2)]
        hi_b = [arena16(13440 + b * 448, GC) for b in range(2)]
        lo_b = [arena16(14336 + b * 448, GC) for b in range(2)]
        src_b = [same[:, 15232 + b * GC:15232 + (b + 1) * GC] for b in range(2)]
        hit = [same[:, 17024 + b * GC:17024 + (b + 1) * GC] for b in range(2)]
        tab_a = [arena16(18816 + b * 448, BINS) for b in range(2)]
        tab_b = [arena16(19712 + b * 448, BINS) for b in range(2)]
        junk = arena16(20608, 28 * P)
        base_a, base_b = arena16(22400, BINS), arena16(22848, BINS)
        zero16 = arena16(23296, 512)
        rows_i = same[0:TILES // 2, 0:12 * P].bitcast(I32).rearrange("p (k c) -> p k c", k=3)
        rows_h = same[0:TILES // 2, 12 * P:16 * P].bitcast(F16).rearrange("p (k c) -> p k c", k=2)
        rows_f = same[0:TILES // 2, 16 * P:18 * P]
        cnt, has16 = same[:, 20608:20608 + BINS], arena16(20608 + BINS, BINS)
        incl, base, ones_w, cnt_a, cnt_b, incl_b, is_a, base_x = (same[:, (7 + k) * BINS:(8 + k) * BINS] for k in range(8))
        last_i, low_i, high_i = (same[:, k * BINS:(k + 1) * BINS].bitcast(I32) for k in range(3))
        empty_f, qf = (same[:, 17024 + k * BINS:17024 + (k + 1) * BINS] for k in range(2))
        ptr_i = same[:, 15232:15232 + BINS].bitcast(I32)

        off_c = sb("off_c", [P, 4])
        flag = sb("flag", [P, 2, GR])
        nb_f = sb("nb_f", [1, BODIES])
        nb_i = sb("nb_i", [1, 1], I32)
        eqs = sb("eqs", [P, 2, GR])
        rank_i = sb("rank_i", [P, 3, GR], I32)
        qidx = sb("qidx", [P, 2, CH], I32)
        idx = sb("idx", [P, 2, 2 * CH], I32)
        shared = sb("shared", [P, 2 * CH * (FW + XW + F)])
        rec = shared[:, 0:2 * CH * REC].rearrange("p (u t c) -> p u t c", u=2, t=CH)
        o1, o2 = 2 * CH * FW, 2 * CH * (FW + XW)
        stage = shared[:, 0:o1].rearrange("p (u t c) -> p u t c", u=2, t=CH)
        msg_f = shared[:, o1:o2].rearrange("p (u x) -> p u x", u=2)
        yb = shared[:, o2:o2 + 2 * CH * F].rearrange("p (u t c) -> p u t c", u=2, t=CH)
        key = sb("key", [P, TILES + 2])
        wcol = sb("wcol", [P, TILES])
        ptr = sb("ptr", [P, TILES], I32)
        vec_d = sb("vec_d", [P, TILES])
        typ_s = sb("typ_s", [P, TILES])
        first_k = sb("first_k", [P, TILES])
        last_k = sb("last_k", [P, TILES + 1])
        chainf = sb("chainf", [P, TILES])
        chaint = sb("chaint", [P, TILES])
        cwmj = sb("cwmj", [P, TILES])
        cw_i = sb("cw_i", [P, TILES], I32)
        out_i = sb("out_i", [P, TILES], I32)
        coef = sb("coef", [P, TILES])
        dis = sb("dis", [P, TILES])
        rtot = sb("rtot", [P, TILES])
        small = sb("small", [P, 4, CH])
        logit = sb("logit", [P, 2, GR])
        edgec = sb("edgec", [CH, 3])
        cont_m = sb("cont_m", [CH, CHUNKS * P])
        state = sb("state", [XW, 2, CH + 1])
        cont_s = sb("cont_s", [CH, 2, P])
        key_s = sb("key_s", [P, 2, CH + 1])
        typ_f = sb("typ_f", [P, 2, CH])
        cm = sb("cm", [CH, 2, CH * XW])
        aggt = sb("aggt", [XW, CH * P])
        lns = sb("lns", [P, 4, CH])
        pidx = sb("pidx", [P, 2, CH], I32)
        STT_AT = GR * XW + 3
        UNIT_W = CH * (5 * F + 3 * FW)
        late = sb("late", [P, CH * (2 * FW + 5 * F) + UNIT_W])
        ob = late[:, 0:2 * CH * FW].rearrange("p (u t c) -> p u t c", u=2, t=CH)
        gb = late[:, 2 * CH * FW:2 * CH * (FW + F)].rearrange("p (u t c) -> p u t c", u=2, t=CH)
        lnb = late[:, 2 * CH * (FW + F):CH * (2 * FW + 5 * F)].rearrange("p (k t c) -> p k t c", k=3, t=CH)
        unit = late[:, CH * (2 * FW + 5 * F):]
        cw_t = late[:, 2 * CH * (FW + F):2 * CH * (FW + F) + 3 * TILES].rearrange("p (k t) -> p k t", k=3)
        xd = late[:, 0:TILES * NODE_W].rearrange("p (t c) -> p t c", c=NODE_W)
        ux, ut, usq, udone = (unit[:, 2 * k * CH * F:2 * (k + 1) * CH * F].rearrange("p (v t c) -> p v t c", v=2, c=F)
                              for k in range(4))
        uo = unit[:, 5 * CH * F:].rearrange("p (k t c) -> p k t c", k=3, c=FW)
        uns = sb("uns", [P, 6, 2, CH])
        attr_t = unit[0:R_ATTR, 0:GC]
        h1_t = unit[0:H, GC:2 * GC]
        oh_td = unit[:, 2 * GC:3 * GC]
        ujunk = unit[:, 3 * GC:3 * GC + GR * NTYPE].rearrange("p (k c) -> p k c", c=NTYPE)
        gst = unit[:, 3 * GC + GR * NTYPE:3 * GC + GR * NTYPE + 2 * GR * F].rearrange("p (u t c) -> p u t c", u=2, c=F)

        ps = ctx.enter_context(nc.psum_tensor("ps", [P, 8 * 512], F32))

        def bank(b, n=512, parts=P, at=0):
            return ps[0:parts, b * 512 + at:b * 512 + at + n]

        s_settled = sem("s_settled")
        s_const, s_eps, s_rows, s_hilo_w, s_src = sem("s_const"), sem("s_eps"), sem("s_rows"), sem("s_hilo_w"), sem("s_src")
        s_zero, s_oh, s_hist = sem("s_zero"), sems("s_oh"), sems("s_hist")
        s_incl, s_off, s_base, s_seed2, s_ptr, s_ptrw = (sem(n) for n in ("s_incl", "s_off", "s_base", "s_seed2", "s_ptr", "s_ptrw"))
        s_bd, s_doht, s_dlook, s_dhit, s_dsum = (sems(n) for n in ("s_bd", "s_doht", "s_dlook", "s_dhit", "s_dsum"))
        s_cnt1, s_nb, s_obz = sem("s_cnt1"), sem("s_nb"), sem("s_obz")
        s_gd, s_xres, s_xput = sems("s_gd"), sems("s_xres"), sems("s_xput")
        s_own_c, s_own_u = sem("s_own_c"), sem("s_own_u")
        s_bc, s_oht, s_ohh, s_eq = sems("s_bc"), sems("s_oht"), sems("s_ohh"), sems("s_eq")
        s_ta, s_tb, s_look, s_upd = sems("s_ta"), sems("s_tb"), sems("s_look"), sems("s_upd")
        s_hit, s_sum, s_q, s_qh = sems("s_hit"), sems("s_sum"), sems("s_q"), sems("s_qh")
        s_idx, s_gath, s_edge, s_keyc, s_scat = sems("s_idx"), sems("s_gath"), sems("s_edge"), sems("s_keyc"), sems("s_scat")
        s_clear = sem("s_clear")
        s_own_v, s_own_p = sem("s_own_v"), sem("s_own_p")
        s_rec, s_cols, s_pref, s_prefw = sems("s_rec"), sems("s_cols"), sems("s_pref"), sems("s_prefw")
        s_kb, s_same, s_kt, s_cont = sem("s_kb"), sem("s_same"), sem("s_kt"), sem("s_cont")
        s_tdb, s_ohtd, s_u, s_logit = sem("s_tdb"), sem("s_ohtd"), sem("s_u"), sem("s_logit")
        s_at, s_atc, s_h1, s_h1s, s_gate, s_gst, s_gw = sem("s_at"), sem("s_atc"), sem("s_h1"), sem("s_h1s"), sem("s_gate"), sem("s_gst"), sems("s_gw")
        s_vt, s_vtc, s_tab, s_tabc = sem("s_vt"), sem("s_vtc"), sem("s_tab"), sem("s_tabc")
        s_next, s_outi, s_ang, s_sin, s_flags = sem("s_next"), sem("s_outi"), sem("s_ang"), sem("s_sin"), sem("s_flags")
        s_st, s_y, s_g = sems("s_st"), sems("s_y"), sems("s_g")
        s_pidx, s_gat = sems("s_pidx"), sems("s_gat")
        s_msg, s_tail, s_state, s_stt, s_cm, s_agg = sems("s_msg"), sems("s_tail"), sems("s_state"), sems("s_stt"), sems("s_cm"), sems("s_agg")
        s_out, s_outw, s_yo = sems("s_out"), sems("s_outw"), sems("s_yo")
        s_aggt, s_conts = sems("s_aggt"), sems("s_conts")
        ln_chunk = (sem("s_cen"), sem("s_sq"), sem("s_var"), sem("s_sd"), lnb, lns)
        s_ucen, s_usq, s_uvar, s_usd = sem("s_ucen"), sem("s_usq"), sem("s_uvar"), sem("s_usd")
        s_cnt, s_rt = sem("s_cnt"), sem("s_rt")
        s_ux, s_uo, s_uow = sem("s_ux"), sem("s_uo"), sem("s_uow")
        s_xvar, s_xsd = sem("s_xvar"), sem("s_xsd")
        s_final = sems("s_final")

        block = ctx.enter_context(nc.Block())
        consts = [(cf[:], cf_in), (cj[:], ch_in), (src_i[:], src_cols), (rows_i[:, 0, :], edge_rows),
                  (w_sb[:, 0, :], w1), (w_sb[:, 1, :], w2t), (g1t_sb[:], g1t), (g2t_sb[:], g2t), (gb1_sb[:], gb1),
                  (rows48[:, 0, :], b1.partition_broadcast(P)), (rows48[:, 1, :], b2.partition_broadcast(P)),
                  (rows48[:, 2, :], gb2.partition_broadcast(P)), (rows48[:, 3, :], gamma.partition_broadcast(P)),
                  (rows48[:, 4, :], beta.partition_broadcast(P)), (embt_sb[:], embt), (adaptt_sb[:], adaptt)]
        N_CONST = 16 * len(consts)

        FIRST, SECOND, STEP, LAST, LAYER1, LAYER2, LAYER3 = range(7)
        STEPS = K_STEPS - 3
        FULL = 2
        EDGE_LN, DENSE_LN = 3, 4
        PAIRS = 4
        SCAT_ALL = BODIES * CH * 16
        UOW_ALL = (UNITS // 2 + 2 * BODIES * EDGE_LN) * 16
        assert UNITS == STEPS * PAIRS * 2
        GATHERED = {SECOND: 0, LAST: 2, LAYER1: 0, LAYER2: 1, LAYER3: 2}
        WRITTEN = {FIRST: 0, SECOND: 1, LAST: 0, LAYER1: 1, LAYER2: 2}

        def bodies_before(kind, s, nb):
            if kind <= SECOND:
                return kind * BODIES
            if kind == STEP:
                return s * nb + FULL * BODIES
            return nb * STEPS + (FULL + kind - LAST) * BODIES

        def gathers_before(kind, s, nb):
            if kind == SECOND:
                return 0
            return (s * nb if kind == STEP else nb * (STEPS + (kind - LAST))) + nb

        def counted_before(kind, s, nb):
            c = CHUNK_COUNTS
            if kind == FIRST:
                return 0
            if kind == SECOND:
                return c[FIRST] * BODIES
            if kind == STEP:
                return (s * nb) * c[STEP] + (c[FIRST] + c[SECOND]) * BODIES
            return (nb * STEPS) * c[STEP] + (c[FIRST] + c[SECOND] + sum(c[LAST:kind])) * BODIES

        def table_writes(kind, s, nb, i):
            if kind == FIRST:
                return i * 16
            if kind == SECOND:
                return i * 32 + BODIES * 16
            return (bodies_before(kind, s, nb) + i) * 16 + BODIES * 16

        def pair_no(s, p):
            return s * PAIRS + p

        def counted_units(kind, s, j):
            e, d = UNIT_COUNTS
            if kind == FIRST:
                return j * e
            if kind == STEP:
                return s * (PAIRS * d) + (j * d + BODIES * e)
            return j * e + (BODIES * e + UNITS // 2 * d)

        def settled(eng):
            eng.sem_inc(s_settled, 1)

        def peeled(eng, chain, body):
            k0 = chain.k if chain else 0
            body(0, True)
            if chain:
                chain.loop(1, BODIES, chain.k - k0, lambda i: body(i, False))
            else:
                with eng.Fori(1, BODIES) as i:
                    body(i, False)

        def rest(eng, nb, body):
            with eng.If(nb > 2):
                with eng.Fori(2, nb) as i:
                    body(i)
            with eng.Else():
                settled(eng)

        def some_bodies(eng, nb, body):
            body(0)
            body(1)
            rest(eng, nb, body)

        def all_bodies(eng, nb, body):
            with eng.Fori(0, nb) as i:
                body(i, True)
            with eng.If(nb < BODIES):
                with eng.Fori(nb, BODIES) as i:
                    body(i, False)
            with eng.Else():
                settled(eng)

        def run_steps(eng, one_step):
            with eng.Fori(0, STEPS // 2) as o:
                for half in range(2):
                    one_step(o * 2 + half, half)
            one_step(STEPS - 1, 0)

        def load_bodies(eng):
            eng.wait_ge(s_nb, 1)
            return eng.value_load(nb_i[0:1, 0:1], min_val=2, max_val=BODIES)

        def ln_of_unit(kind, s, j, l):
            if kind == FIRST:
                return j * EDGE_LN + l
            if kind == STEP:
                return s * (PAIRS * DENSE_LN * 2) + (j * (DENSE_LN * 2) + BODIES * EDGE_LN + 2 * l)
            return j * EDGE_LN + (BODIES * EDGE_LN + UNITS * DENSE_LN + l)

        def ln_of_chunk(kind, i, u, j=0):
            if kind == LAYER3:
                return i * 4 + (6 * BODIES + 2 * u + j)
            return i * 2 + ((kind - LAST) * 2 * BODIES + u)

        def chunk_cols(i, u, width=1, extra=0):
            return bass.ds(i * (2 * CH * width) + (u * CH * width + extra), CH * width)

        @block.sync
        def _(sp):
            for dst, src in consts:
                sp.dma_start(dst, src).then_inc(s_const, 16)
            sp.wait_ge(s_rows, 1)
            for k in range(2):
                sp.dma_start(d_hilo[k].rearrange("w (q c) -> q w c", c=2 * P),
                             rows_h[:, k, :].rearrange("q (w c) -> q w c", w=2)).then_inc(s_hilo_w, 16)
            sp.dma_start(d_src[0].rearrange("(q c) -> q c", c=2 * P), rows_f).then_inc(s_hilo_w, 16)
            sp.wait_ge(s_hilo_w, 48)

            def flag_loads(i, first):
                for u in range(2):
                    for h in range(2):
                        if not (first and u == 0):
                            sp.wait_ge(s_dhit[h], i * 2 + u)
                        at = bass.ds(i * (4 * GC) + (2 * u + h) * GC, GC)
                        sp.dma_start(hi_b[h], d_hilo[0, 1, at].partition_broadcast(P)).then_inc(s_bd[h], 16)
                        sp.dma_start(lo_b[h], d_hilo[1, 1, at].partition_broadcast(P)).then_inc(s_bd[h], 16)
            peeled(sp, None, flag_loads)
            sp.wait_ge(s_ptr, 1)
            sp.dma_start(d_ptr.rearrange("(b p l) c -> p b (l c)", b=NB, p=P),
                         ptr_i.bitcast(F32).rearrange("p (b l) -> p b l", b=NB)).then_inc(s_ptrw, 16)
            sp.wait_ge(s_ptrw, 16)

            def rank_loads(i, first):
                for u in range(2):
                    for h in range(2):
                        if not (first and u == 0):
                            sp.wait_ge(s_hit[h], i * 2 + u)
                            sp.wait_ge(s_eq[h], i * 2 + u)
                        at = bass.ds(i * (4 * GC) + (2 * u + h) * GC, GC)
                        sp.dma_start(hi_b[h], d_hilo[0, 0, at].partition_broadcast(P)).then_inc(s_bc[h], 16)
                        sp.dma_start(lo_b[h], d_hilo[1, 0, at].partition_broadcast(P)).then_inc(s_bc[h], 16)
                        sp.dma_start(src_b[h], d_src[0, at].partition_broadcast(P)).then_inc(s_bc[h], 16)
            peeled(sp, None, rank_loads)
            for u in range(2):
                sp.wait_ge(s_scat[u], SCAT_ALL)

            def record_loads(i, first):
                for u in range(2):
                    if not first:
                        sp.wait_ge(s_prefw[u], i * 32)
                        sp.wait_ge(s_pref[u], i)
                        sp.wait_ge(s_cols[u], i)
                        sp.wait_ge(s_at, i * 4 + (2 * u - 2))
                    sp.dma_start(rec[:, u], sorted_pt[:, bass.ds(i * (2 * CH) + u * CH, CH), :]).then_inc(s_rec[u], 16)
            peeled(sp, None, record_loads)
            for u in range(2):
                sp.wait_ge(s_prefw[u], BODIES * 32)
                sp.wait_ge(s_gw[u], 2 * BODIES * 16)
            sp.wait_ge(s_outi, 1)

            nb = load_bodies(sp)

            def chunk_loads(kind, s, i, first=False):
                m = bodies_before(kind, s, nb) + i
                for u in range(2):
                    if not first:
                        sp.wait_ge(s_msg[u], m)
                    tiles = bass.ds(i * (2 * CH) + u * CH, CH)
                    if kind == FIRST:
                        sp.dma_start(stage[:, u, :, 0:F], sorted_pt[:, tiles, 0:F]).then_inc(s_st[u], 16)
                    else:
                        sp.dma_start(stage[:, u].rearrange("p t c -> p (t c)"),
                                     d_pref[max(0, kind - LAST)][:, chunk_cols(i, u, FW)]).then_inc(s_st[u], 16)
                    if kind == LAYER3:
                        sp.dma_start(gb[:, u].rearrange("p t c -> p (t c)"),
                                     d_gate[:, chunk_cols(i, u, F)]).then_inc(s_g[u], 16)
                for u in range(2):
                    if not first:
                        sp.wait_ge(s_out[u], m)
                    sp.dma_start(yb[:, u].rearrange("p t c -> p (t c)"),
                                 d_y[kind in (LAYER1, LAYER3)][:, chunk_cols(i, u, F)]).then_inc(s_y[u], 16)

            peeled(sp, None, lambda i, first: chunk_loads(FIRST, 0, i, first))
            with sp.Fori(0, BODIES) as i:
                chunk_loads(SECOND, 0, i)
            run_steps(sp, lambda s, half: some_bodies(sp, nb, lambda i: chunk_loads(STEP, s, i)))
            for n, kind in enumerate((LAST, LAYER1, LAYER2, LAYER3)):
                if kind == LAYER1:
                    sp.wait_ge(s_uow, UOW_ALL)
                for u in range(2):
                    if n:
                        sp.wait_ge(s_yo[u], n * BODIES * 16)
                with sp.Fori(0, BODIES) as i:
                    chunk_loads(kind, 0, i)

            for u in range(2):
                sp.wait_ge(s_yo[u], 4 * BODIES * 16)

            def last_rows(i, first):
                for u in range(2):
                    if first:
                        sp.wait_ge(s_out[u], bodies_before(LAYER3 + 1, 0, nb))
                    else:
                        sp.wait_ge(s_final[u], i * (16 * CH))
                    sp.dma_start(yb[:, u].rearrange("p t c -> p (t c)"), d_y[0][:, chunk_cols(i, u, F)]).then_inc(s_y[u], 16)
            peeled(sp, None, last_rows)

        @block.gpsimd
        def _(pool):
            own = Chain(pool, s_own_p)
            pool.memset(shared[:], 0.0).then_inc(s_clear, 1)
            pool.wait_ge(s_clear, 1)

            def gather(dst, table, index, rows, done):
                pool.indirect_dma_start(dst, None, table, bass.IndirectOffsetOnAxis(ap=index, axis=0),
                                        bounds_check=rows - 1, oob_is_err=False).then_inc(done, 16)

            def scatter(table, index, rows, src, done):
                pool.indirect_dma_start(table, bass.IndirectOffsetOnAxis(ap=index, axis=0), src, None,
                                        bounds_check=rows - 1, oob_is_err=False).then_inc(done, 16)

            def at_dst(i, first):
                for u in range(2):
                    pool.wait_ge(s_idx[u], i * 16 + 16)
                    if not first:
                        pool.wait_ge(s_xres[u], i)
                    settled(pool)
                    for k in range(CH):
                        gather(rec[:, u, k, 0:NODE_W], node_table, idx[:, u, k:k + 1], NODES, s_gd[u])
            peeled(pool, None, at_dst)

            def records(i, first):
                for u in range(2):
                    pool.wait_ge(s_idx[u], i * 16 + (16 * BODIES + 16))
                    if not first:
                        pool.wait_ge(s_scat[u], i * (16 * CH))
                    settled(pool)
                    for k in range(CH):
                        gather(rec[:, u, k, C_SRCX:C_SRCX + NODE_W], node_table, idx[:, u, CH + k:CH + k + 1], NODES, s_gath[u])
                if first:
                    pool.wait_ge(s_ptrw, 16)
                for u in range(2):
                    settled(pool)
                    for k in range(CH):
                        gather(rec[:, u, k, C_PTR:C_PTR + 1], d_ptr, idx[:, u, k:k + 1], NPAD, s_gath[u])
                for u in range(2):
                    pool.wait_ge(s_gath[u], i * (16 * 2 * CH) + 16 * 2 * CH)
                    pool.wait_ge(s_xput[u], i + 1)
                    pool.wait_ge(s_edge[u], i * 16 + 16)
                    pool.wait_ge(s_keyc[u], i + 1)
                    pool.wait_ge(s_qh[u], i + 1)
                    settled(pool)
                    for k in range(CH):
                        scatter(d_sorted, qidx[:, u, k:k + 1], EPAD, rec[:, u, k, :], s_scat[u])
            peeled(pool, None, records)

            own.add(pool.memset(key[:], -1.0))
            own.add(pool.memset(key_s[:], -1.0))
            own.sync()

            def small_columns(i, first):
                for u in range(2):
                    at = chunk_cols(i, u)
                    pool.wait_ge(s_rec[u], i * 16 + 16)
                    if not first:
                        pool.wait_ge(s_same, i * 4 + (2 * u - 2))
                        pool.wait_ge(s_kt, i * 2 + (u - 1))
                        pool.wait_ge(s_tdb, i * 4 + (2 * u - 2))
                    if not (first and u == 0):
                        settled(pool)
                        own.link(pool.tensor_copy(key_s[:, u, 0:1], key_s[:, 1 - u, CH:CH + 1]))
                    settled(pool)
                    own.add(pool.tensor_copy(key_s[:, u, 1:CH + 1], rec[:, u, :, C_KEY]))
                    own.add(pool.tensor_copy(typ_f[:, u, :], rec[:, u, :, F + 1]))
                    own.sync()
                    settled(pool)
                    pool.tensor_copy(key[:, chunk_cols(i, u, 1, 1)], rec[:, u, :, C_KEY])
                    pool.tensor_copy(wcol[:, at], rec[:, u, :, C_W])
                    pool.tensor_copy(ptr[:, at], rec[:, u, :, C_PTR].bitcast(I32))
                    pool.tensor_copy(vec_d[:, at], rec[:, u, :, F])
                    pool.tensor_copy(typ_s[:, at], rec[:, u, :, C_SRCX + F + 1].bitcast(I32)).then_inc(s_cols[u], 1)
            small_columns(0, True)
            own.loop(1, BODIES, 6, lambda i: small_columns(i, False))

            nb = load_bodies(pool)

            def pass_gathers(kind, s, table, i):
                m = bodies_before(kind, s, nb) + i
                g = gathers_before(kind, s, nb) + i if kind != SECOND else i
                for u in range(2):
                    pool.wait_ge(s_msg[u], m)
                    settled(pool)
                    pool.tensor_copy(pidx[:, u, :], ptr[:, chunk_cols(i, u)]).then_inc(s_pidx[u], 1)
                    pool.wait_ge(s_pidx[u], g + 1)
                    pool.wait_ge(s_st[u], m * 16 + 16)
                    settled(pool)
                    for k in range(CH):
                        gather(stage[:, u, k, :], d_table[table], pidx[:, u, k:k + 1], EPAD, s_gat[u])

            def gather_pass(kind, s, table):
                for u in range(2):
                    pool.wait_ge(s_outw[u], table_writes(kind, s, nb, 0))
                settled(pool)
                some_bodies(pool, nb, lambda i: pass_gathers(kind, s, table, i))
            gather_pass(SECOND, 0, GATHERED[SECOND])
            run_steps(pool, lambda s, half: gather_pass(STEP, s, 1 + half))
            for kind in (LAST, LAYER1, LAYER2, LAYER3):
                gather_pass(kind, 0, GATHERED[kind])

            pool.wait_ge(s_outi, 1)
            pool.wait_ge(s_uow, UOW_ALL)

            def final_rows(i, first):
                for u in range(2):
                    if not first:
                        pool.wait_ge(s_final[u], i * (16 * CH))
                    else:
                        pool.wait_ge(s_msg[u], bodies_before(LAYER3 + 1, 0, nb))
                    settled(pool)
                    pool.tensor_copy(pidx[:, u, :], out_i[:, chunk_cols(i, u)]).then_inc(s_pidx[u], 1)
                    pool.wait_ge(s_pidx[u], nb * (STEPS + 5) + (i + 1))
                    pool.wait_ge(s_y[u], (bodies_before(LAYER3 + 1, 0, nb) + i) * 16 + 16)
                    settled(pool)
                    for k in range(CH):
                        scatter(out, pidx[:, u, k:k + 1], NODES, yb[:, u, k, :], s_final[u])
            peeled(pool, None, final_rows)
            for u in range(2):
                pool.wait_ge(s_final[u], SCAT_ALL)

        @block.scalar
        def _(act):
            act.wait_ge(s_vt, 1)
            nc.scalar.copy(vt_sb[:], bank(7, NTYPE, EMB)).then_inc(s_vtc, 1)
            act.wait_ge(s_clear, 1)

            def keep_dst(i, first):
                for u in range(2):
                    if not first:
                        act.wait_ge(s_gd[u], i * (16 * CH))
                    act.dma_start(idx[:, u, :], index_chunks[:, chunk_cols(i, u, 2)]).then_inc(s_idx[u], 16)
                for u in range(2):
                    act.wait_ge(s_gd[u], i * (16 * CH) + 16 * CH)
                    tiles = bass.ds(i * (2 * CH) + u * CH, CH)
                    nc.scalar.copy(xd[:, tiles, 0:F + 1], rec[:, u, :, 0:F + 1])
                    nc.scalar.copy(xd[:, tiles, F + 1:F + 2], rec[:, u, :, F + 1:F + 2].bitcast(I32)).then_inc(s_xres[u], 1)
            peeled(act, None, keep_dst)
            for u in range(2):
                act.wait_ge(s_xres[u], BODIES)

            def group_tables(i, first):
                for u in range(2):
                    if not first:
                        act.wait_ge(s_scat[u], i * (16 * CH))
                    nc.scalar.copy(rec[:, u, :, 0:NODE_W], xd[:, bass.ds(i * (2 * CH) + u * CH, CH), :]).then_inc(s_xput[u], 1)
                    act.dma_start(idx[:, u, :], index_chunks[:, chunk_cols(i, u, 2)]).then_inc(s_idx[u], 16)
                    act.dma_start(rec[:, u, :, C_ATTR:C_ATTR + EDGE_W],
                                  edge_table[:, chunk_cols(i, u, EDGE_W)].rearrange("p (t c) -> p t c", c=EDGE_W)).then_inc(s_edge[u], 16)
                    if first and u == 0:
                        act.wait_ge(s_src, 1)
                    nc.scalar.copy(rec[:, u, :, C_KEY], src_f[:, chunk_cols(i, u)]).then_inc(s_keyc[u], 1)
                for u in range(2):
                    for h in range(2):
                        n = i * 2 + u
                        if h == 1:
                            act.wait_ge(s_upd[0], n + 1)
                        elif first and u == 0:
                            act.wait_ge(s_seed2, 1)
                        else:
                            act.wait_ge(s_upd[1], n)
                        if not (first and u == 0):
                            act.wait_ge(s_look[h], n)
                        nc.scalar.copy(tab_a[h], ps[:, 0:BINS]).then_inc(s_ta[h], 1)
            peeled(act, None, group_tables)

            def act_gates(i, first):
                for u in range(2):
                    act.wait_ge(s_rec[u], i * 16 + 16)
                    if not first:
                        act.wait_ge(s_prefw[u], i * 32)
                    nc.scalar.mul(ob[:, u, :, 0:F], rec[:, u, :, 0:F], ALPHA).then_inc(s_pref[u], 1)
                    act.wait_ge(s_pref[u], i + 1)
                    act.dma_start(d_pref[0][:, chunk_cols(i, u, FW)], ob[:, u].rearrange("p t c -> p (t c)")).then_inc(s_prefw[u], 16)
                    act.dma_start(d_y[0][:, chunk_cols(i, u, F)].rearrange("p (t c) -> p t c", c=F),
                                  rec[:, u, :, C_SRCX:C_SRCX + F]).then_inc(s_prefw[u], 16)
                    for h in range(2):
                        q = i * 4 + (2 * u + h)
                        free = not (first and u == 0 and h == 0)
                        act.wait_ge(s_at, q + 1)
                        if free:
                            act.wait_ge(s_h1, q)
                        nc.scalar.copy(attr_t, bank(4, GC, R_ATTR)).then_inc(s_atc, 1)
                        act.wait_ge(s_h1, q + 1)
                        if free:
                            act.wait_ge(s_gate, q)
                        nc.scalar.activation(h1_t, bank(6, GC, H), ACT.Silu, bias=gb1_sb[:, 0:1]).then_inc(s_h1s, 1)
                        act.wait_ge(s_gst, q + 1)
                        act.dma_start(d_gate[:, bass.ds(i * (4 * GR * F) + (2 * u + h) * GR * F, GR * F)],
                                      gst[:, h].rearrange("p t c -> p (t c)")).then_inc(s_gw[h], 16)
            act.wait_ge(s_tab, 1)
            nc.scalar.copy(tab_sb[:], bank(7, NTYPE, NTYPE, 128)).then_inc(s_tabc, 1)
            act.wait_ge(s_const, N_CONST)
            act.wait_ge(s_eps, 1)
            act.wait_ge(s_obz, 1)
            peeled(act, None, act_gates)
            act.wait_ge(s_ang, 1)
            nc.scalar.activation(cw_t[:, 2, :], cw_t[:, 1, :], ACT.Sin, bias=eps_c[:, 1:2], scale=-float(np.pi) / CUTOFF).then_inc(s_sin, 1)

            def square(n):
                cen, sq, _, _, buf, _ = ln_chunk
                act.wait_ge(cen, n + 1)
                nc.scalar.activation(buf[:, 1], buf[:, 0], ACT.Square).then_inc(sq, 1)

            def root(n):
                _, _, var, sd, _, st = ln_chunk
                act.wait_ge(var, n + 1)
                nc.scalar.activation(st[:, 2], st[:, 1], ACT.Sqrt, bias=eps_c[:, 0:1], scale=1.0 / F).then_inc(sd, 1)

            def unit_squares(n, units=1):
                for w in range(units):
                    act.wait_ge(s_ucen, n + (w + 1))
                    nc.scalar.activation(usq[:, w], ut[:, w], ACT.Square).then_inc(s_usq, 1)

            def unit_roots(n, l, units=1):
                for w in range(units):
                    act.wait_ge(s_uvar, n + (w + 1))
                    eps = eps_c[:, 2:3] if l == 0 else eps_c[:, 0:1]
                    nc.scalar.activation(uns[:, 2, w], uns[:, 1, w], ACT.Sqrt, bias=eps, scale=1.0 / F).then_inc(s_usd, 1)

            nb = load_bodies(act)

            out_dense = out.rearrange("(p t) c -> p (t c)", p=P)

            def load_unit(kind, j):
                act.dma_start(ux[:, 0], sorted_pt[:, bass.ds(j * CH + (kind == LAST) * BODIES * CH, CH), 0:F]).then_inc(s_ux, 16)

            def load_pair(q):
                act.dma_start(ux.rearrange("p v t c -> p (v t c)"),
                              x_dense[:, bass.ds(q * (2 * CH * F), 2 * CH * F)]).then_inc(s_ux, 16)

            def store_unit(kind, j):
                act.wait_ge(s_uo, j + 1 + (kind == LAST) * (BODIES + UNITS // 2))
                at = bass.ds(j * (CH * FW) + (kind == LAST) * BODIES * CH * FW, CH * FW)
                for l in range(EDGE_LN):
                    act.dma_start(d_pref[l + 1][:, at], uo[:, l].rearrange("p t c -> p (t c)")).then_inc(s_uow, 16)

            def positions(kind, s, i, u, first=False):
                if not first:
                    act.wait_ge(s_agg[u], bodies_before(kind, s, nb) + i)
                nc.scalar.copy(cont_s[:, u, :], cont_m[:, bass.ds(i * (2 * P) + u * P, P)]).then_inc(s_conts[u], 1)

            def sums(kind, s, i, u, first=False):
                m = bodies_before(kind, s, nb) + i
                width = XW if kind == FIRST else F
                act.wait_ge(s_tail[u], m + 1)
                if not (first and u == 0):
                    act.wait_ge(s_agg[1 - u], m + u)
                nc.scalar.copy(aggt[0:width, :], ps[0:width, 0:CH * P]).then_inc(s_aggt[u], 1)

            def chunk_end(kind, s, i, u, half=0):
                m = bodies_before(kind, s, nb) + i
                if kind == FIRST:
                    act.wait_ge(s_cnt, i * 2 + (u + 1))
                    nc.scalar.activation(small[:, 1], small[:, 0], ACT.Sqrt).then_inc(s_rt, 1)
                if kind >= LAST:
                    for l in range(2 if kind == LAYER3 else 1):
                        n = ln_of_chunk(kind, i, u, l)
                        square(n)
                        root(n)
                act.wait_ge(s_out[u], m + 1)
                rows = ob[:, u].rearrange("p t c -> p (t c)")
                if kind != LAYER3:
                    table = 2 - half if kind == STEP else WRITTEN[kind]
                    act.dma_start(table_pt[table][:, chunk_cols(i, u, FW)], rows).then_inc(s_outw[u], 16)
                if kind == SECOND:
                    act.dma_start(table_pt[2][:, chunk_cols(i, u, FW)], rows).then_inc(s_outw[u], 16)
                if kind >= LAST:
                    act.dma_start(d_y[kind in (LAST, LAYER2)][:, chunk_cols(i, u, F)].rearrange("p (t c) -> p t c", c=F),
                                  ob[:, u, :, 0:F]).then_inc(s_yo[u], 16)

            def body_with_unit(kind, i, first=False):
                load_unit(kind, i)
                positions(kind, 0, i, 0, first)
                positions(kind, 0, i, 1, first)
                for l in range(EDGE_LN):
                    n = ln_of_unit(kind, 0, i, l)
                    unit_squares(n)
                    unit_roots(n, l)
                    if l == 0:
                        sums(kind, 0, i, 0, first)
                sums(kind, 0, i, 1, first)
                store_unit(kind, i)
                chunk_end(kind, 0, i, 0)
                chunk_end(kind, 0, i, 1)

            def plain_body(kind, s, i, half=0):
                positions(kind, s, i, 0)
                positions(kind, s, i, 1)
                sums(kind, s, i, 0)
                sums(kind, s, i, 1)
                chunk_end(kind, s, i, 0, half)
                chunk_end(kind, s, i, 1, half)

            def act_pair(s, p, i, half):
                q = pair_no(s, p)
                if i is not None:
                    positions(STEP, s, i, 0)
                    positions(STEP, s, i, 1)
                for l in range(DENSE_LN):
                    n = ln_of_unit(STEP, s, p, l)
                    unit_squares(n, 2)
                    if l == 0 and (p < PAIRS - 1 or not isinstance(s, int)):
                        load_pair(q + 1)
                    unit_roots(n, l, 2)
                    if l == 0 and i is not None:
                        sums(STEP, s, i, 0)
                    if l == 2:
                        for w in range(2):
                            act.wait_ge(s_xvar, q * 2 + (w + 1))
                            nc.scalar.activation(uns[:, 5, w], uns[:, 4, w], ACT.Sqrt, bias=eps_c[:, 0:1], scale=1.0 / F).then_inc(s_xsd, 1)
                        if i is not None:
                            sums(STEP, s, i, 1)
                            chunk_end(STEP, s, i, 0, half)
                act.wait_ge(s_uo, q + (BODIES + 1))
                act.dma_start(out_dense[:, bass.ds(q * (2 * CH * F), 2 * CH * F)], udone.rearrange("p v t c -> p (v t c)")).then_inc(s_uow, 16)
                if i is not None:
                    chunk_end(STEP, s, i, 1, half)

            def act_step(s, half):
                act_pair(s, 0, 0, half)
                act_pair(s, 1, 1, half)
                rest(act, nb, lambda i: plain_body(STEP, s, i, half))
                for p in range(2, PAIRS):
                    act_pair(s, p, None, half)

            peeled(act, None, lambda i, first: body_with_unit(FIRST, i, first))
            with act.Fori(0, BODIES) as i:
                plain_body(SECOND, 0, i)
            act.wait_ge(s_uow, BODIES * EDGE_LN * 16)
            load_pair(0)
            run_steps(act, act_step)
            with act.Fori(0, BODIES) as i:
                body_with_unit(LAST, i)
            for kind in (LAYER1, LAYER2, LAYER3):
                with act.Fori(0, BODIES) as i:
                    plain_body(kind, 0, i)

        @block.vector
        def _(dve):
            own, own_c, own_u = Chain(dve, s_own_v), Chain(dve, s_own_c), Chain(dve, s_own_u)
            v = nc.vector

            v.memset(eps_c[:, 0:1], EPS)
            v.memset(eps_c[:, 2:3], EPS / (1.0 + ALPHA) ** 2)
            v.memset(eps_c[:, 1:2], float(np.pi) / 2).then_inc(s_eps, 1)
            v.memset(zero16, 0.0).then_inc(s_zero, 1)
            own.add(v.memset(state[:], 0.0))
            own.add(v.memset(last_k[:], -1.0))
            dve.wait_ge(s_const, N_CONST)
            own.add(v.tensor_scalar(rows_i[:, 1, :], rows_i[:, 0, :], 7, None, ALU.arith_shift_right))
            own.add(v.tensor_scalar(rows_i[:, 2, :], rows_i[:, 0, :], P - 1, None, ALU.bitwise_and))
            own.sync()
            own.add(v.tensor_copy(rows_h, rows_i[:, 1:3, :]))
            own.add(v.tensor_scalar(rows48[:, 5, :], rows48[:, 1, :], 0.0, None, ALU.max))
            own.sync()
            v.tensor_copy(rows_f, rows_i[:, 0, 0:2 * P]).then_inc(s_rows, 1)
            own.add(v.tensor_copy(rows48[:, 6, :], rows48[:, 0, :]))
            own.sync()
            own.link(v.tensor_reduce(rsum[:], rows48[:, 5:7, :], AX_X, ALU.add))
            own.link(v.scalar_tensor_tensor(rows48[:, 5:7, :], rsum[:].unsqueeze(2).broadcast_to([P, 2, F]), -1.0 / F,
                                            rows48[:, 5:7, :], ALU.mult, ALU.add))
            own.add(v.tensor_scalar(col_i[:, 0, :], src_i[:], 7, None, ALU.arith_shift_right))
            own.add(v.tensor_scalar(col_i[:, 1, :], src_i[:], P - 1, None, ALU.bitwise_and))
            own.sync()
            own.add(v.tensor_copy(hi_c[:], col_i[:, 0, :]))
            own.add(v.tensor_copy(lo_c[:], col_i[:, 1, :]))
            own.sync()
            v.tensor_copy(src_f[:], src_i[:]).then_inc(s_src, 1)
            iota = cj[:, J_IOTA:J_IOTA + BINS]

            def one_hots_high(h, first_tile):
                for k in range(GR):
                    v.tensor_scalar(ohh[h][:, k * BINS:(k + 1) * BINS], iota, hi_c[:, bass.ds(first_tile + k, 1)], None, ALU.is_equal)

            def one_hots_low(h, first_tile, done, flags=None):
                for k in range(GR):
                    args = (None, ALU.is_equal) if flags is None else (flags[:, k:k + 1], ALU.is_equal, ALU.mult)
                    ins = v.tensor_scalar(ohl[h][:, k * P:(k + 1) * P], iota[:, 0:P], lo_c[:, bass.ds(first_tile + k, 1)], *args)
                ins.then_inc(done, 1)

            def one_hots(h, first_tile, done):
                one_hots_high(h, first_tile)
                one_hots_low(h, first_tile, done)

            def one_hots_across(h, done):
                for b in range(NB):
                    ins = v.tensor_scalar(oht[h][:, b * GC:(b + 1) * GC], hi_b[h], cf[:, K_PART + b:K_PART + b + 1], None, ALU.is_equal)
                ins.then_inc(done, 1)

            def pick(h, done):
                v.scalar_tensor_tensor(hit[h], lo_b[h], part0, ps[:, (2 + 2 * h) * 512:(2 + 2 * h) * 512 + GC],
                                       ALU.is_equal, ALU.mult).then_inc(done, 1)

            def histogram(i, first):
                for u in range(2):
                    for h in range(2):
                        if not (first and u == 0):
                            dve.wait_ge(s_hist[h], i * 2 + u)
                        one_hots(h, i * (2 * CH) + (u * CH + h * GR), s_oh[h])
            peeled(dve, None, histogram)

            for h in range(2):
                dve.wait_ge(s_hist[h], 2 * BODIES)
            own.link(v.tensor_copy(cnt, ps[:, 0:BINS]))
            v.tensor_scalar(has16, cnt, 0.0, None, ALU.is_gt).then_inc(s_cnt1, 1)

            def active(i, first):
                for u in range(2):
                    for h in range(2):
                        n = i * 2 + u
                        fresh = first and u == 0
                        t0 = i * (2 * CH) + (u * CH + h * GR)
                        dve.wait_ge(s_bd[h], n * 32 + 32)
                        if not fresh:
                            dve.wait_ge(s_dlook[h], n)
                            dve.wait_ge(s_hist[h], n + 2 * BODIES)
                        one_hots_across(h, s_doht[h])
                        one_hots_high(h, t0)
                        dve.wait_ge(s_dlook[h], n + 1)
                        if not fresh:
                            dve.wait_ge(s_dsum[h], n)
                        pick(h, s_dhit[h])
                        dve.wait_ge(s_dsum[h], n + 1)
                        if not fresh:
                            dve.wait_ge(s_oh[h], n + 2 * BODIES)
                        settled(dve)
                        own.link(v.tensor_copy(flag[:, h, :], bank(6 + h, GR)))
                        one_hots_low(h, t0, s_oh[h], flag[:, h, :])
            peeled(dve, own, active)

            for h in range(2):
                dve.wait_ge(s_hist[h], 4 * BODIES)
            own.add(v.tensor_scalar(is_a, ps[:, 0:BINS], 0.0, None, ALU.is_gt))
            own.add(v.memset(ones_w, 1.0))
            own.sync()
            own.link(v.tensor_tensor(cnt_a, cnt, is_a, ALU.mult))
            own.add(v.tensor_tensor(cnt_b, cnt, cnt_a, ALU.subtract))
            own.add(v.tensor_tensor_scan(incl, ones_w, cnt_a, 0.0, ALU.mult, ALU.add))
            own.sync()
            v.tensor_tensor_scan(incl_b, ones_w, cnt_b, 0.0, ALU.mult, ALU.add).then_inc(s_incl, 1)
            dve.wait_ge(s_off, 1)
            own.link(v.tensor_copy(off_c[:, 0:3], bank(2, 3)))
            own.link(v.tensor_tensor(off_c[:, 3:4], off_c[:, 1:2], off_c[:, 2:3], ALU.add))
            own.add(v.scalar_tensor_tensor(base_x, incl, off_c[:, 0:1], cnt_a, ALU.add, ALU.subtract))
            own.add(v.scalar_tensor_tensor(base, incl_b, off_c[:, 3:4], cnt_b, ALU.add, ALU.subtract))
            own.sync()
            own.link(v.tensor_tensor(base_x, base_x, base, ALU.subtract))
            own.link(v.tensor_tensor(base_x, base_x, is_a, ALU.mult))
            own.link(v.tensor_tensor(base, base, base_x, ALU.add))
            own.link(v.tensor_copy(base_a, base))
            v.tensor_tensor(base_b, base, base_a, ALU.subtract).then_inc(s_base, 1)
            own.link(v.tensor_scalar(nb_f[:, 0:BODIES - 2], cf[0:1, K_LIMIT:K_LIMIT + BODIES - 2], off_c[0:1, 2:3], None, ALU.is_lt))
            own.link(v.tensor_reduce(nb_f[:, BODIES - 2:BODIES - 1], nb_f[:, 0:BODIES - 2], AX_X, ALU.add))
            v.tensor_scalar(nb_i[:], nb_f[:, BODIES - 2:BODIES - 1], 2.0, None, ALU.add).then_inc(s_nb, 1)
            own.link(v.scalar_tensor_tensor(last_i, base, -1.0, cnt, ALU.add, ALU.add))
            own.add(v.tensor_scalar(low_i, last_i, P - 1, None, ALU.bitwise_and))
            own.add(v.tensor_scalar(high_i, last_i, 7, None, ALU.arith_shift_right))
            own.add(v.tensor_scalar(empty_f, cnt, 0.0, FAR, ALU.is_equal, ALU.mult))
            own.sync()
            own.link(v.scalar_tensor_tensor(qf, low_i, float(TILES), high_i, ALU.mult, ALU.add))
            v.tensor_tensor(ptr_i, qf, empty_f, ALU.add).then_inc(s_ptr, 1)
            dve.wait_ge(s_ptr, 1)
            dve.wait_ge(s_seed2, 1)

            def ranks(i, first):
                for u in range(2):
                    for h in range(2):
                        n = i * 2 + u
                        fresh = first and u == 0
                        dve.wait_ge(s_bc[h], n * 48 + 48)
                        if not fresh:
                            dve.wait_ge(s_look[h], n)
                            dve.wait_ge(s_upd[h], n)
                        one_hots_across(h, s_oht[h])
                        one_hots(h, i * (2 * CH) + (u * CH + h * GR), s_ohh[h])
                        dve.wait_ge(s_ta[h], n + 1)
                        v.tensor_tensor(tab_b[h], ps[:, 0:BINS], tab_a[h], ALU.subtract).then_inc(s_tb[h], 1)
                        if not (fresh and h == 0):
                            dve.wait_ge(s_eq[1 - h], n + (h if True else 0))
                        for k in range(GR):
                            w = (k + 1) * P
                            at = (k * (k + 1) // 2) * P
                            col = bass.ds(i * (2 * CH) + (u * CH + h * GR + k), 1)
                            ins = v.scalar_tensor_tensor(junk[:, at:at + w], src_b[h][:, 0:w], src_f[:, col],
                                                         cj[:, J_EARLIER + GC - w:J_EARLIER + GC], ALU.is_equal, ALU.mult,
                                                         accum_out=eqs[:, h, k:k + 1])
                        ins.then_inc(s_eq[h], 1)
                        dve.wait_ge(s_look[h], n + 1)
                        if not fresh:
                            dve.wait_ge(s_sum[h], n)
                        pick(h, s_hit[h])
                        dve.wait_ge(s_sum[h], n + 1)
                        dve.wait_ge(s_eq[h], n + 1)
                        v.tensor_tensor(rank_i[:, 0, :], bank(6 + h, GR), eqs[:, h, :], ALU.add).then_inc(s_q[h], 1)
                        dve.wait_ge(s_q[h], n + 1)
                        own.add(v.tensor_scalar(rank_i[:, 1, :], rank_i[:, 0, :], P - 1, None, ALU.bitwise_and))
                        own.add(v.tensor_scalar(rank_i[:, 2, :], rank_i[:, 0, :], 7, None, ALU.arith_shift_right))
                        own.sync()
                        if h == 0 and not first:
                            dve.wait_ge(s_scat[u], i * (16 * CH))
                        ins = v.scalar_tensor_tensor(qidx[:, u, h * GR:(h + 1) * GR], rank_i[:, 1, :], float(TILES),
                                                     rank_i[:, 2, :], ALU.mult, ALU.add)
                        if h == 0:
                            own.link(ins)
                        else:
                            ins.then_inc(s_qh[u], 1)
                            dve.wait_ge(s_qh[u], i + 1)
            peeled(dve, own, ranks)

            dve.wait_ge(s_own_p, 2)
            v.memset(ob, 0.0).then_inc(s_obz, 1)

            def gates(i, first):
                for u in range(2):
                    for h in range(2):
                        q = i * 4 + (2 * u + h)
                        fresh = first and u == 0 and h == 0
                        t0 = i * (2 * CH) + (u * CH + h * GR)
                        dve.wait_ge(s_kb, q + 1)
                        kb = ps[:, 0:GC].rearrange("p (k c) -> p k c", c=P)
                        own.add(v.tensor_copy(first_k[:, bass.ds(t0, GR)], kb[:, :, 0]))
                        own.add(v.tensor_copy(last_k[:, bass.ds(t0 + 1, GR)], kb[:, :, P - 1]))
                        v.tensor_tensor(same[:, bass.ds(t0 * P, GC)].rearrange("p (k c) -> p k c", c=P), kb,
                                        key[:, bass.ds(t0 + 1, GR)].unsqueeze(2).broadcast_to([P, GR, P]),
                                        ALU.is_equal).then_inc(s_same, 1)
                        dve.wait_ge(s_tdb, q + 1)
                        if not fresh:
                            dve.wait_ge(s_u, q)
                        v.tensor_scalar(oh_td, ps[:, 1024:1024 + GC], part0, None, ALU.is_equal).then_inc(s_ohtd, 1)
                        if h == 1:
                            dve.wait_ge(s_kt, i * 2 + (u + 1))
                            own.add(v.tensor_copy(edgec[:, 0:1], bank(0, 1, CH)))
                            own.add(v.tensor_copy(edgec[:, 1:2], bank(1, 1, CH, P - 1)))
                            own.sync()
                            own.link(v.tensor_tensor(edgec[:, 2:3], edgec[:, 0:1], edgec[:, 1:2], ALU.is_equal))
                            v.tensor_scalar(cont_m[:, bass.ds(i * (2 * P) + u * P, P)], bank(0, P, CH), edgec[:, 0:1], edgec[:, 2:3],
                                            ALU.is_equal, ALU.mult).then_inc(s_cont, 1)
                            dve.wait_ge(s_cont, i * 2 + (u + 1))
                        dve.wait_ge(s_u, q + 1)
                        if not fresh:
                            dve.wait_ge(s_logit, q)
                            dve.wait_ge(s_gst, q)
                        for k in range(GR):
                            at = 1024 + (k * NTYPE if k < 4 else 512 + (k - 4) * NTYPE)
                            ins = v.scalar_tensor_tensor(ujunk[:, k, :], cf[:, K_ROW:K_ROW + NTYPE], typ_s[:, bass.ds(t0 + k, 1)],
                                                         ps[:, at:at + NTYPE], ALU.is_equal, ALU.mult, accum_out=logit[:, h, k:k + 1])
                        ins.then_inc(s_logit, 1)
                        dve.wait_ge(s_gate, q + 1)
                        if not (first and u == 0):
                            dve.wait_ge(s_gw[h], (i * 2 + u) * 16)
                        own.link(v.tensor_tensor(gst[:, h], bank(4, GR * F).rearrange("p (k c) -> p k c", c=F),
                                                 rows48[:, 2:3, :].broadcast_to([P, GR, F]), ALU.add))
                        dve.wait_ge(s_logit, q + 1)
                        v.tensor_tensor(gst[:, h], gst[:, h], logit[:, h, :].unsqueeze(2).broadcast_to([P, GR, F]), ALU.add).then_inc(s_gst, 1)
            peeled(dve, own, gates)

            own.sync()
            own.add(v.tensor_tensor(chainf[:], first_k[:], last_k[:, 1:TILES + 1], ALU.is_equal))
            own.add(v.tensor_tensor(chaint[:], first_k[:], last_k[:, 0:TILES], ALU.is_equal))
            own.sync()
            v.tensor_tensor(chainf[:], chainf[:], chaint[:], ALU.mult).then_inc(s_flags, 1)
            for u in range(2):
                dve.wait_ge(s_cols[u], BODIES)
            own.link(v.tensor_scalar(cw_i[:], wcol[:], 1.0 / (2 * CUTOFF), None, ALU.mult))
            own.link(v.scalar_tensor_tensor(cw_t[:, 0, :], cw_i[:], -2 * CUTOFF, wcol[:], ALU.mult, ALU.add))
            own.link(v.scalar_tensor_tensor(cw_t[:, 1, :], cw_t[:, 0, :], -1.0, cw_t[:, 0, :], ALU.mult, ALU.max))
            own.link(v.tensor_scalar(cw_t[:, 0, :], cw_t[:, 1, :], -CUTOFF, None, ALU.add))
            v.scalar_tensor_tensor(cw_t[:, 1, :], cw_t[:, 0, :], -1.0, cw_t[:, 0, :], ALU.mult, ALU.max).then_inc(s_ang, 1)
            dve.wait_ge(s_sin, 1)
            own.link(v.tensor_scalar(cw_t[:, 0, :], cw_t[:, 2, :], -0.5, 0.5, ALU.mult, ALU.add))
            own.link(v.scalar_tensor_tensor(cw_t[:, 1, :], wcol[:], CUTOFF, cw_t[:, 0, :], ALU.is_lt, ALU.mult))
            own.link(v.tensor_tensor(cwmj[:], cw_t[:, 1, :], vec_d[:], ALU.mult))
            dve.wait_ge(s_next, 1)
            own.link(v.tensor_tensor(cw_t[:, 0, :], bank(0, TILES), key[:, 1:TILES + 1], ALU.is_equal))
            v.scalar_tensor_tensor(out_i[:], cw_t[:, 0, :], FAR, key[:, 1:TILES + 1], ALU.mult, ALU.add).then_inc(s_outi, 1)
            for h in range(2):
                dve.wait_ge(s_gw[h], 2 * BODIES * 16)
            own.link(v.memset(uo, 0.0))

            def center(chain, ln, n, x):
                cen, _, _, _, buf, st = ln
                chain.link(v.tensor_reduce(st[:, 0], x, AX_X, ALU.add))
                v.scalar_tensor_tensor(buf[:, 0], st[:, 0].unsqueeze(2).broadcast_to([P, CH, F]), -1.0 / F, x, ALU.mult, ALU.add).then_inc(cen, 1)

            def variance(ln, n):
                _, sq, var, _, buf, st = ln
                dve.wait_ge(sq, n + 1)
                v.tensor_reduce(st[:, 1], buf[:, 1], AX_X, ALU.add).then_inc(var, 1)

            def scaled(chain, ln, n, dst):
                cen, _, _, sd, buf, st = ln
                dve.wait_ge(cen, n + 1)
                dve.wait_ge(sd, n + 1)
                chain.link(v.reciprocal(st[:, 3], st[:, 2]))
                return v.tensor_tensor(dst, buf[:, 0], st[:, 3].unsqueeze(2).broadcast_to([P, CH, F]), ALU.mult)

            def row(r):
                return rows48[:, r:r + 1, :].broadcast_to([P, CH, F])

            def agg_of(u, width, lo, hi):
                return ps[:, (4 + 2 * u) * 512:(6 + 2 * u) * 512].rearrange("p (b x) -> p b x", b=2)[:, :, 0:GR * width].rearrange(
                    "p b (t c) -> p b t c", c=width)[:, :, :, lo:hi]

            def halves(ap):
                return ap.rearrange("p (b t) c -> p b t c", b=2)

            def message(kind, s, i, u, first=False, gathers=True):
                m, width = bodies_before(kind, s, nb) + i, XW if kind == FIRST else F
                msg = msg_f[:, u, 0:CH * width].rearrange("p (t c) -> p t c", c=width)
                at = chunk_cols(i, u)
                dve.wait_ge(s_st[u], m * 16 + 16)
                if kind != FIRST and gathers:
                    dve.wait_ge(s_gat[u], (gathers_before(kind, s, nb) + i) * (16 * CH) + 16 * CH)
                if not first:
                    dve.wait_ge(s_agg[u], m)
                if kind == FIRST:
                    own_c.add(v.tensor_copy(msg[:, :, F], wcol[:, at]))
                    own_c.add(v.memset(msg[:, :, F + 1:F + 2], 1.0))
                    own_c.add(v.tensor_copy(msg[:, :, F + 2], vec_d[:, at]))
                x = stage[:, u, :, 0:F]
                if kind == LAYER3:
                    dve.wait_ge(s_g[u], i * 16 + 16)
                    own_c.link(v.tensor_tensor(msg, x, gb[:, u], ALU.mult))
                    x = msg
                scale = {LAYER2: stage[:, u, :, F:FW], LAYER3: cwmj[:, at].unsqueeze(2)}.get(kind, wcol[:, at].unsqueeze(2))
                v.tensor_tensor(msg[:, :, 0:F], x, scale.broadcast_to([P, CH, F]), ALU.mult).then_inc(s_msg[u], 1)

            def carry(kind, s, i, u, first=False):
                m, width = bodies_before(kind, s, nb) + i, XW if kind == FIRST else F
                dve.wait_ge(s_aggt[u], m + 1)
                if not first:
                    dve.wait_ge(s_stt[u], m)
                if not (first and u == 0):
                    dve.wait_ge(s_state[1 - u], m + u)
                    own_c.link(v.tensor_copy(state[:, u, 0:1], state[:, 1 - u, CH:CH + 1]))
                else:
                    own_c.link(v.memset(state[:, u, 0:1], 0.0))
                v.tensor_tensor_scan(state[0:width, u, 1:CH + 1], chainf[0:width, chunk_cols(i, u)],
                                     aggt[0:width, :].rearrange("p (t c) -> p t c", c=P)[:, :, P - 1],
                                     state[0:width, u, 0:1], ALU.mult, ALU.add).then_inc(s_state[u], 1)

            def spread(kind, s, i, u, first=False):
                m, width = bodies_before(kind, s, nb) + i, XW if kind == FIRST else F
                dve.wait_ge(s_stt[u], m + 1)
                v.tensor_tensor(cm[:, u, 0:CH * width].rearrange("p (t c) -> p t c", c=width),
                                bank(5 + 2 * u, width, CH, STT_AT).unsqueeze(1).broadcast_to([CH, CH, width]),
                                delta.unsqueeze(2).broadcast_to([CH, CH, width]), ALU.mult).then_inc(s_cm[u], 1)

            def finish(kind, s, i, u, first=False):
                m, width = bodies_before(kind, s, nb) + i, XW if kind == FIRST else F
                at = chunk_cols(i, u)
                dve.wait_ge(s_agg[u], m + 1)
                dve.wait_ge(s_y[u], m * 16 + 16)
                if not first:
                    dve.wait_ge(s_outw[u], table_writes(kind, s, nb, i if kind != LAYER3 else 0))
                if kind == FIRST and first:
                    dve.wait_ge(s_prefw[u], BODIES * 32)
                if kind >= LAST:
                    dve.wait_ge(s_yo[u], i * 16 + (kind - LAST) * BODIES * 16)
                y, o = yb[:, u], ob[:, u, :, 0:F]
                agg = agg_of(u, width, 0, F)
                t1 = lnb[:, 2]
                if kind == FIRST:
                    def per_position(c):
                        return agg_of(u, width, c, c + 1).rearrange("p b t c -> p b (t c)")

                    def pair(ap):
                        return ap.rearrange("p (b t) -> p b t", b=2)
                    v.tensor_copy(pair(small[:, 0]), per_position(F + 1)).then_inc(s_cnt, 1)
                    own_c.add(v.tensor_scalar(pair(small[:, 2]), per_position(F), 1e-10, None, ALU.add))
                    own_c.add(v.tensor_scalar(pair(small[:, 3]), per_position(F + 2), 1e-8, None, ALU.max))
                    own_c.sync()
                    own_c.add(v.reciprocal(rtot[:, at], small[:, 3]))
                    own_c.link(v.reciprocal(small[:, 2], small[:, 2]))
                    own_c.link(v.tensor_scalar(coef[:, at], small[:, 2], 1.0 - ALPHA, None, ALU.mult))
                    dve.wait_ge(s_rt, m * 2 + (u + 1))
                    own_c.link(v.reciprocal(dis[:, at], small[:, 1]))
                settled(dve)
                own_c.link(v.tensor_copy(ob[:, u, :, F], dis[:, at]))
                if kind <= LAST:
                    own_c.link(v.tensor_tensor(halves(t1), agg, halves(coef[:, at].unsqueeze(2).broadcast_to([P, CH, F])), ALU.mult))
                if kind < LAST:
                    v.scalar_tensor_tensor(o, y, ALPHA, t1, ALU.mult, ALU.add).then_inc(s_out[u], 1)
                    return
                if kind == LAST:
                    own_c.link(v.scalar_tensor_tensor(t1, y, 1.0 + ALPHA, t1, ALU.mult, ALU.add))
                elif kind in (LAYER1, LAYER2):
                    bias = rows48[:, kind - LAYER1:kind - LAYER1 + 1, :].broadcast_to([P, CH, F])
                    if kind == LAYER1:
                        own_c.link(v.tensor_tensor(halves(t1), agg, halves(bias), ALU.add))
                    else:
                        own_c.link(v.tensor_tensor(halves(t1), agg, halves(dis[:, at].unsqueeze(2).broadcast_to([P, CH, F])), ALU.mult))
                        own_c.link(v.tensor_tensor(t1, t1, bias, ALU.add))
                    if kind == LAYER1:
                        own_c.link(v.tensor_tensor(t1, t1, y, ALU.add))
                    else:
                        own_c.link(v.scalar_tensor_tensor(t1, t1, 0.0, y, ALU.max, ALU.add))
                else:
                    own_c.link(v.tensor_tensor(halves(t1), agg, halves(rtot[:, at].unsqueeze(2).broadcast_to([P, CH, F])), ALU.mult))
                    own_c.link(v.tensor_tensor(t1, t1, y, ALU.add))
                center(own_c, ln_chunk, ln_of_chunk(kind, i, u, 0), t1)

            def finish_norm(kind, i, u):
                if kind < LAST:
                    return
                y, o, t1 = yb[:, u], ob[:, u, :, 0:F], lnb[:, 2]
                n = ln_of_chunk(kind, i, u, 0)
                variance(ln_chunk, n)
                if kind == LAYER3:
                    own_c.link(scaled(own_c, ln_chunk, n, t1))
                    own_c.link(v.tensor_tensor(t1, t1, row(3), ALU.mult))
                    own_c.link(v.tensor_tensor(t1, t1, row(4), ALU.add))
                    own_c.link(v.tensor_tensor(t1, t1, y, ALU.add))
                    n = ln_of_chunk(kind, i, u, 1)
                    center(own_c, ln_chunk, n, t1)
                    variance(ln_chunk, n)
                scaled(own_c, ln_chunk, n, o).then_inc(s_out[u], 1)

            def each(units, ins):
                for w in range(units):
                    own_u.add(ins(w))
                own_u.sync()

            def wide(st):
                return st.unsqueeze(2).broadcast_to([P, CH, F])

            def unit_center(n, units, x):
                each(units, lambda w: v.tensor_reduce(uns[:, 0, w], x[:, w], AX_X, ALU.add))
                for w in range(units):
                    v.scalar_tensor_tensor(ut[:, w], wide(uns[:, 0, w]), -1.0 / F, x[:, w], ALU.mult, ALU.add).then_inc(s_ucen, 1)

            def unit_variance(n, units):
                for w in range(units):
                    dve.wait_ge(s_usq, n + (w + 1))
                    v.tensor_reduce(uns[:, 1, w], usq[:, w], AX_X, ALU.add).then_inc(s_uvar, 1)

            def unit_inverse(n, w):
                dve.wait_ge(s_ucen, n + (w + 1))
                dve.wait_ge(s_usd, n + (w + 1))
                own_u.link(v.reciprocal(uns[:, 3, w], uns[:, 2, w]))

            def edge_layer(kind, j, l, first=False):
                n = ln_of_unit(kind, 0, j, l)
                unit_inverse(n, 0)
                if l == 0 and not first:
                    dve.wait_ge(s_uow, j * (16 * EDGE_LN) + (kind == LAST) * (BODIES * EDGE_LN + UNITS // 2) * 16)
                ins = v.tensor_tensor(uo[:, l, :, 0:F], ut[:, 0], wide(uns[:, 3, 0]), ALU.mult)
                if l == EDGE_LN - 1:
                    ins.then_inc(s_uo, 1)
                    assert own_u.k == UNIT_COUNTS[0], f"UNIT_COUNTS 0 counts {own_u.k}"
                else:
                    own_u.link(ins)
                    v.tensor_tensor(ut[:, 0], uo[:, l, :, 0:F], row(6 - l), ALU.add).then_inc(s_ucen, 1)

            def body_with_unit(kind, i, first=False, gathers=True):
                own_c.base, own_c.k = i * CHUNK_COUNTS[kind] + counted_before(kind, 0, nb), 0
                own_u.base, own_u.k = counted_units(kind, 0, i), 0
                message(kind, 0, i, 0, first, gathers)
                message(kind, 0, i, 1, first, gathers)
                dve.wait_ge(s_ux, i * 16 + (16 + (kind == LAST) * (BODIES + UNITS // 2) * 16))
                unit_center(ln_of_unit(kind, 0, i, 0), 1, ux)
                unit_variance(ln_of_unit(kind, 0, i, 0), 1)
                edge_layer(kind, i, 0, first)
                carry(kind, 0, i, 0, first)
                unit_variance(ln_of_unit(kind, 0, i, 1), 1)
                spread(kind, 0, i, 0, first)
                edge_layer(kind, i, 1)
                unit_variance(ln_of_unit(kind, 0, i, 2), 1)
                edge_layer(kind, i, 2)
                finish(kind, 0, i, 0, first)
                carry(kind, 0, i, 1, first)
                spread(kind, 0, i, 1, first)
                finish_norm(kind, i, 0)
                finish(kind, 0, i, 1, first)
                finish_norm(kind, i, 1)
                assert own_c.k == CHUNK_COUNTS[kind], f"CHUNK_COUNTS {kind} counts {own_c.k}"

            def plain_body(kind, s, i, gathers=True):
                own_c.base, own_c.k = i * CHUNK_COUNTS[kind] + counted_before(kind, s, nb), 0
                message(kind, s, i, 0, gathers=gathers)
                message(kind, s, i, 1, gathers=gathers)
                carry(kind, s, i, 0)
                spread(kind, s, i, 0)
                finish(kind, s, i, 0)
                carry(kind, s, i, 1)
                spread(kind, s, i, 1)
                finish_norm(kind, i, 0)
                finish(kind, s, i, 1)
                finish_norm(kind, i, 1)
                assert own_c.k == CHUNK_COUNTS[kind], f"CHUNK_COUNTS {kind} counts {own_c.k}"

            def dve_pair(s, p, i):
                q = pair_no(s, p)
                own_u.base, own_u.k = counted_units(STEP, s, p), 0

                def part(f, u):
                    if i is not None:
                        f(STEP, s, i, u)
                if i is not None:
                    own_c.base, own_c.k = i * CHUNK_COUNTS[STEP] + counted_before(STEP, s, nb), 0
                part(message, 0)
                part(message, 1)
                dve.wait_ge(s_ux, q * 16 + (BODIES * 16 + 16))
                unit_center(ln_of_unit(STEP, s, p, 0), 2, ux)
                for l in range(DENSE_LN):
                    n = ln_of_unit(STEP, s, p, l)
                    unit_variance(n, 2)
                    if l == 1:
                        part(spread, 0)
                    if l == 2:
                        part(finish, 0)
                    for w in range(2):
                        unit_inverse(n, w)
                        if l == 2:
                            own_u.link(v.tensor_tensor(uns[:, 4, w], uns[:, 1, w], uns[:, 3, w], ALU.mult))
                            v.tensor_tensor(uns[:, 4, w], uns[:, 4, w], uns[:, 3, w], ALU.mult).then_inc(s_xvar, 1)
                        if l == DENSE_LN - 1:
                            if w == 0:
                                dve.wait_ge(s_uow, q * 16 + BODIES * EDGE_LN * 16)
                            ins = v.tensor_tensor(udone[:, w], ut[:, w], wide(uns[:, 3, w]), ALU.mult)
                            if w == 1:
                                ins.then_inc(s_uo, 1)
                        else:
                            own_u.add(v.tensor_tensor(ut[:, w], ut[:, w], wide(uns[:, 3, w]), ALU.mult))
                    if l < 2:
                        own_u.sync()
                        for w in range(2):
                            v.tensor_tensor(ut[:, w], ut[:, w], row(6 - l), ALU.add).then_inc(s_ucen, 1)
                        if l == 0:
                            part(carry, 0)
                    if l == 2:
                        for w in range(2):
                            dve.wait_ge(s_xsd, q * 2 + (w + 1))
                            own_u.link(v.reciprocal(uns[:, 4, w], uns[:, 5, w]))
                            own_u.add(v.tensor_tensor(usq[:, w], row(3), wide(uns[:, 4, w]), ALU.mult))
                        own_u.sync()
                        each(2, lambda w: v.scalar_tensor_tensor(ut[:, w], usq[:, w], 1.0, ut[:, w], ALU.add, ALU.mult))
                        part(carry, 1)
                        each(2, lambda w: v.tensor_tensor(ut[:, w], ut[:, w], row(4), ALU.add))
                        unit_center(ln_of_unit(STEP, s, p, 3), 2, ut)
                        part(spread, 1)
                assert own_u.k == UNIT_COUNTS[1], f"UNIT_COUNTS 1 counts {own_u.k}"
                part(finish, 1)
                if i is not None:
                    assert own_c.k == CHUNK_COUNTS[STEP], f"CHUNK_COUNTS {STEP} counts {own_c.k}"

            def dve_step(s, half):
                dve_pair(s, 0, 0)
                dve_pair(s, 1, 1)
                rest(dve, nb, lambda i: plain_body(STEP, s, i))
                for p in range(2, PAIRS):
                    dve_pair(s, p, None)

            nb = load_bodies(dve)
            peeled(dve, None, lambda i, first: body_with_unit(FIRST, i, first))
            all_bodies(dve, nb, lambda i, gathers: plain_body(SECOND, 0, i, gathers))
            run_steps(dve, dve_step)
            dve.wait_ge(s_uow, (BODIES * EDGE_LN + UNITS // 2) * 16)
            own.link(v.memset(uo, 0.0))
            all_bodies(dve, nb, lambda i, gathers: body_with_unit(LAST, i, gathers=gathers))
            for kind in (LAYER1, LAYER2, LAYER3):
                all_bodies(dve, nb, lambda i, gathers: plain_body(kind, 0, i, gathers))

        @block.tensor
        def _(pe):
            mm = nc.tensor.matmul
            pe.wait_ge(s_const, N_CONST)
            mm(bank(7, NTYPE, EMB), adaptt_sb[:], embt_sb[:], start=True, stop=True).then_inc(s_vt, 1)
            pe.wait_ge(s_vtc, 1)
            pe.wait_ge(s_zero, 1)
            mm(bank(0), ident16, zero16, start=True, stop=True)
            mm(bank(1), ident16, zero16, start=True, stop=True)

            def count_edges(h):
                for k in range(GR):
                    for b in range(NB):
                        ins = mm(ps[:, b * P:(b + 1) * P], ohh[h][:, k * BINS + b * P:k * BINS + (b + 1) * P],
                                 ohl[h][:, k * P:(k + 1) * P], start=False, stop=(k == GR - 1), skip_group_check=True)
                return ins

            def look_up(h, tables, done):
                for at, w in ((0, 512), (512, GC - 512)):
                    for b in range(NB):
                        for t, tab in enumerate(tables):
                            ins = mm(ps[:, (2 + 2 * h) * 512 + at:(2 + 2 * h) * 512 + at + w], tab[:, b * P:(b + 1) * P],
                                     oht[h][:, b * GC + at:b * GC + at + w], start=(b == 0 and t == 0),
                                     stop=(b == NB - 1 and t == len(tables) - 1))
                ins.then_inc(done, 1)

            def column_sums(h, done):
                for k in range(GR):
                    ins = mm(bank(6 + h, 1, P, k), hit[h][:, k * P:(k + 1) * P], cf[:, K_ONE:K_ONE + 1], start=True, stop=True)
                ins.then_inc(done, 1)

            def histogram(i, first):
                for u in range(2):
                    for h in range(2):
                        pe.wait_ge(s_oh[h], i * 2 + (u + 1))
                        count_edges(h).then_inc(s_hist[h], 1)
            peeled(pe, None, histogram)
            pe.wait_ge(s_cnt1, 1)
            mm(bank(0), ident16, zero16, start=True, stop=True)
            mm(bank(1), ident16, zero16, start=True, stop=True)

            def active(i, first):
                for u in range(2):
                    for h in range(2):
                        n = i * 2 + u
                        pe.wait_ge(s_doht[h], n + 1)
                        if not (first and u == 0):
                            pe.wait_ge(s_dhit[h], n)
                        look_up(h, (has16,), s_dlook[h])
                        pe.wait_ge(s_dhit[h], n + 1)
                        if not (first and u == 0):
                            pe.wait_ge(s_oh[h], n + 2 * BODIES)
                        column_sums(h, s_dsum[h])
                        pe.wait_ge(s_oh[h], n + (2 * BODIES + 1))
                        count_edges(h).then_inc(s_hist[h], 1)
            peeled(pe, None, active)
            pe.wait_ge(s_incl, 1)
            mm(bank(2, 1), cf[:, K_BEFORE:K_BEFORE + P], incl[:, BINS - 1:BINS], start=True, stop=True)
            mm(bank(2, 1, P, 1), cf[:, K_BEFORE:K_BEFORE + P], incl_b[:, BINS - 1:BINS], start=True, stop=True)
            mm(bank(2, 1, P, 2), cf[:, K_ALL:K_ALL + P], incl[:, BINS - 1:BINS], start=True, stop=True).then_inc(s_off, 1)
            pe.wait_ge(s_base, 1)
            for b, n in ((0, 512), (1, BINS - 512)):
                mm(bank(b, n), ident16, base_a[:, b * 512:b * 512 + n], start=True, stop=False)
                ins = mm(bank(b, n), ident16, base_b[:, b * 512:b * 512 + n], start=False, stop=True)
            ins.then_inc(s_seed2, 1)

            def ranks(i, first):
                for u in range(2):
                    for h in range(2):
                        n = i * 2 + u
                        fresh = first and u == 0
                        pe.wait_ge(s_oht[h], n + 1)
                        pe.wait_ge(s_tb[h], n + 1)
                        if not fresh:
                            pe.wait_ge(s_hit[h], n)
                        look_up(h, (tab_a[h], tab_b[h]), s_look[h])
                        pe.wait_ge(s_ohh[h], n + 1)
                        count_edges(h).then_inc(s_upd[h], 1)
                        pe.wait_ge(s_hit[h], n + 1)
                        if not fresh:
                            pe.wait_ge(s_q[h], n)
                        column_sums(h, s_sum[h])
            peeled(pe, None, ranks)

            for h in range(2):
                pe.wait_ge(s_q[h], 2 * BODIES)
            mm(bank(7, NTYPE, NTYPE, 128), vt_sb[:], embt_sb[:], start=True, stop=True).then_inc(s_tab, 1)
            pe.wait_ge(s_tabc, 1)

            def gates(i, first):
                for u in range(2):
                    for h in range(2):
                        q = i * 4 + (2 * u + h)
                        fresh = first and u == 0 and h == 0
                        t0 = i * (2 * CH) + (u * CH + h * GR)
                        pe.wait_ge(s_cols[u], i + 1)
                        if not fresh:
                            pe.wait_ge(s_same, q)
                            if u + h:
                                pass
                            pe.wait_ge(s_cont, i * 2 + u)
                        for k in range(GR):
                            ins = mm(ps[:, k * P:(k + 1) * P], key_s[:, u, h * GR + k + 1:h * GR + k + 2].broadcast_to([P, P]), ident, start=True, stop=True)
                        ins.then_inc(s_kb, 1)
                        if not fresh:
                            pe.wait_ge(s_logit, q)
                        for k in range(GR):
                            ins = mm(ps[:, 1024 + k * P:1024 + (k + 1) * P], typ_f[:, u, h * GR + k:h * GR + k + 1].broadcast_to([P, P]), ident, start=True, stop=True)
                        ins.then_inc(s_tdb, 1)
                        pe.wait_ge(s_rec[u], i * 16 + 16)
                        if not fresh:
                            pe.wait_ge(s_gst, q)
                            pe.wait_ge(s_atc, q)
                        settled(pe)
                        for k in range(GR):
                            ins = nc.tensor.transpose(ps[0:R_ATTR, 2048 + k * P:2048 + (k + 1) * P],
                                                      rec[:, u, h * GR + k, C_ATTR:C_ATTR + R_ATTR], ident)
                        ins.then_inc(s_at, 1)
                        pe.wait_ge(s_atc, q + 1)
                        if not fresh:
                            pe.wait_ge(s_h1s, q)
                        settled(pe)
                        mm(bank(6, 512, H), g1t_sb[:], attr_t[:, 0:512], start=True, stop=True)
                        mm(bank(7, GC - 512, H), g1t_sb[:], attr_t[:, 512:GC], start=True, stop=True).then_inc(s_h1, 1)
                        if h == 1:
                            pe.wait_ge(s_same, q + 1)
                            settled(pe)
                            nc.tensor.transpose(bank(0, P, CH), key_s[:, u, 1:CH + 1], ident)
                            nc.tensor.transpose(bank(1, P, CH), key_s[:, u, 0:CH], ident).then_inc(s_kt, 1)
                        pe.wait_ge(s_ohtd, q + 1)
                        for k in range(GR):
                            at = 1024 + (k * NTYPE if k < 4 else 512 + (k - 4) * NTYPE)
                            ins = mm(ps[:, at:at + NTYPE], oh_td[0:NTYPE, k * P:(k + 1) * P], tab_sb[:], start=True, stop=True)
                        ins.then_inc(s_u, 1)
                        pe.wait_ge(s_h1s, q + 1)
                        for k in range(GR):
                            ins = mm(ps[:, 2048 + k * F:2048 + (k + 1) * F], h1_t[:, k * P:(k + 1) * P], g2t_sb[:], start=True, stop=True)
                        ins.then_inc(s_gate, 1)
            peeled(pe, None, gates)
            pe.wait_ge(s_same, 2 * CHUNKS)
            pe.wait_ge(s_flags, 1)
            mm(bank(0, TILES), cf[:, K_NEXT:K_NEXT + P], key[:, 1:TILES + 1], start=True, stop=False)
            mm(bank(0, TILES), cf[:, K_NEXTT:K_NEXTT + P], key[:, 2:TILES + 2], start=False, stop=True).then_inc(s_next, 1)
            pe.wait_ge(s_outi, 1)
            pe.wait_ge(s_gst, 2 * CHUNKS)

            nb = load_bodies(pe)

            def pe_body(kind, s, i, first=False):
                m = bodies_before(kind, s, nb) + i
                width = XW if kind == FIRST else F
                through = w_sb[:, kind - LAYER1, :] if kind in (LAYER1, LAYER2) else ident[0:width, 0:width]

                def tail(u):
                    pe.wait_ge(s_msg[u], m + 1)
                    if not (first and u == 0):
                        pe.wait_ge(s_aggt[1 - u], m + u)
                    for k in range(CH):
                        ins = mm(ps[0:width, k * P:(k + 1) * P], msg_f[:, u, k * width:(k + 1) * width],
                                 same[:, bass.ds(i * (2 * CH * P) + (u * CH + k) * P, P)], start=True, stop=True)
                    ins.then_inc(s_tail[u], 1)

                def back(u, b):
                    for k in range(b * GR, (b + 1) * GR):
                        mm(bank(4 + 2 * u + b, width, P, (k % GR) * width), aggt[0:width, k * P:(k + 1) * P], through,
                           start=(k % GR == 0), stop=False)

                def carried(u):
                    pe.wait_ge(s_state[u], m + 1)
                    settled(pe)
                    mm(bank(5 + 2 * u, width, CH, STT_AT), state[0:width, u, 0:CH], through, start=True, stop=True).then_inc(s_stt[u], 1)

                def complete(u):
                    pe.wait_ge(s_cm[u], m + 1)
                    back(u, 1)
                    pe.wait_ge(s_conts[u], m + 1)
                    for b in range(2):
                        ins = mm(bank(4 + 2 * u + b, GR * width), cont_s[:, u, :],
                                 cm[:, u, b * GR * width:(b + 1) * GR * width], start=False, stop=True)
                    ins.then_inc(s_agg[u], 1)

                tail(0)
                for u in range(2):
                    pe.wait_ge(s_aggt[u], m + 1)
                    if not first:
                        pe.wait_ge(s_out[u], m)
                    back(u, 0)
                    carried(u)
                    if u == 0:
                        tail(1)
                    complete(u)

            peeled(pe, None, lambda i, first: pe_body(FIRST, 0, i, first))
            with pe.Fori(0, BODIES) as i:
                pe_body(SECOND, 0, i)
            run_steps(pe, lambda s, half: some_bodies(pe, nb, lambda i: pe_body(STEP, s, i)))
            for kind in (LAST, LAYER1, LAYER2, LAYER3):
                with pe.Fori(0, BODIES) as i:
                    pe_body(kind, 0, i)


_OUT = (P * DROWS, F)


def kernel(**inputs):
    import concourse.bacc as bacc
    from concourse.bass_utils import run_bass_kernel_spmd as run

    a = {k: np.asarray(v) for k, v in inputs.items()}
    pad = EPAD - EDGES

    def tiles(x):
        x = np.concatenate([x, np.zeros((pad,) + x.shape[1:], x.dtype)])
        return np.ascontiguousarray(x.reshape(TILES, P, -1).transpose(1, 0, 2).reshape(P, -1))

    spare = np.full(pad, SPARE, a["src"].dtype)
    src, dst = (np.concatenate([a[n], spare]) for n in ("src", "dst"))
    by_chunk = np.stack([x.reshape(CHUNKS, CH, P) for x in (dst, src)], 1)
    x = a["x"]
    f, h = constants()
    arrays = {
        "node_table": np.concatenate([x, a["node_vec"][:, None], a["node_type_119"][:, None].view(np.float32)], 1),
        "x_dense": np.concatenate([x, np.zeros((P * DROWS - NODES, F), x.dtype)]).reshape(P, DROWS * F),
        "edge_table": tiles(np.concatenate([a["edge_attr_40"], a["edge_weight"][:, None]], 1)),
        "index_chunks": np.ascontiguousarray(by_chunk.transpose(3, 0, 1, 2).reshape(P, -1)),
        "src_cols": np.ascontiguousarray(src.reshape(TILES, P).T),
        "edge_rows": np.concatenate([src.reshape(TILES // 2, 2 * P), dst.reshape(TILES // 2, 2 * P)], 1),
        "const_f": f,
        "const_h": h,
        "w1": a["L1_gnn_weight"],
        "b1": a["L1_gnn_bias"],
        "w2t": np.ascontiguousarray(a["L2_gnn_W"].T),
        "b2": a["L2_gnn_b"],
        "g1t": np.ascontiguousarray(a["L3_gnn_W1"].T),
        "gb1": a["L3_gnn_b1"][:, None],
        "g2t": np.ascontiguousarray(a["L3_gnn_W2"].T),
        "gb2": a["L3_gnn_b2"],
        "embt": np.ascontiguousarray(a["L3_gnn_emb"].T),
        "adaptt": np.ascontiguousarray(a["L3_gnn_adaptW"].T),
        "gamma": a["L3_gnn_gamma"],
        "beta": a["L3_gnn_beta"],
    }
    nc = bacc.Bacc("TRN2", target_bir_lowering=False, num_devices=1)
    arrays = {f"in_{k}": np.ascontiguousarray(v) for k, v in arrays.items()}
    args = [nc.dram_tensor(k, v.shape, mybir.dt.from_np(v.dtype), kind="ExternalInput").ap() for k, v in arrays.items()]
    out = nc.dram_tensor("out", _OUT, F32, kind="ExternalOutput").ap()
    build(nc, *args, out)
    r = run(nc, [arrays], core_ids=[0])
    return r.results[0]["out"][:NODES]
```

```python
from contextlib import ExitStack

import numpy as np

import concourse.bass as bass
from concourse import mybir

P = 128
NODES, EDGES, F = 100000, 25000, 48
TILES = -(-EDGES // P)
EPAD = TILES * P
CH = 14
CHUNKS = TILES // CH
BODIES = CHUNKS // 2
GR = 7
GC = GR * P
NB = -(-NODES // (P * P))
NPAD = NB * P * P
SPARE = NPAD - 1
BINS = NB * P
FAR = 1.0e6
ALPHA, K_STEPS = 0.1, 10
CUTOFF = 6.0
EPS = 1e-5
H, R_ATTR = 48, 40
NTYPE, EMB = 119, 32
FW = F + 1
XW = F + 3
NODE_W = F + 2
EDGE_W = R_ATTR + 1
C_SRCX, C_ATTR, C_W, C_KEY, C_DST = NODE_W, 2 * NODE_W, 2 * NODE_W + R_ATTR, 2 * NODE_W + R_ATTR + 1, 2 * NODE_W + R_ATTR + 2
REC = C_DST + 1
DROWS = 784
UNITS = DROWS // CH

CHUNK_COUNTS = [16, 4, 4, 10, 12, 12, 22]
UNIT_COUNTS = [6, 28]

ALU = mybir.AluOpType
ACT = mybir.ActivationFunctionType
F32, F16, I32 = mybir.dt.float32, mybir.dt.float16, mybir.dt.int32
AX_X = mybir.AxisListType.X

K_ID, K_PART, K_NEXT, K_NEXTT, K_BEFORE, K_DELTA, K_ROW, K_ONE = 0, 128, 135, 263, 391, 519, 519 + CH, 647 + CH
K_LIMIT, K_ALL = K_ONE + 1, K_ONE + 1 + BODIES - 2
K_W = K_ALL + P
J_IOTA, J_EARLIER, J_ID = 0, BINS, BINS + GC
J_W = J_ID + P


def constants():
    f = np.zeros((P, K_W), np.float32)
    p = np.arange(P)
    f[p, K_ID + p] = 1.0
    f[:, K_PART:K_PART + NB] = p[:, None] + P * np.arange(NB)
    f[p[1:], K_NEXT + p[:-1]] = 1.0
    f[0, K_NEXTT + P - 1] = 1.0
    f[:, K_BEFORE:K_BEFORE + P] = p[:, None] < p[None, :]
    c = np.arange(CH)
    f[c, K_DELTA + c] = 1.0
    f[:, K_ROW:K_ROW + P] = p[None, :]
    f[:, K_ONE] = 1.0
    f[:, K_LIMIT:K_LIMIT + BODIES - 2] = np.arange(2, BODIES) * (2 * CH * P)
    f[:, K_ALL:K_ALL + P] = 1.0
    h = np.zeros((P, J_W), np.float16)
    h[:, J_IOTA:J_IOTA + BINS] = np.arange(BINS)
    h[:, J_EARLIER:J_EARLIER + GC - P] = 1.0
    h[:, J_EARLIER + GC - P:J_EARLIER + GC] = p[None, :] < p[:, None]
    h[p, J_ID + p] = 1.0
    return f, h


class Chain:

    def __init__(self, eng, sem):
        self.eng, self.sem, self.base, self.k = eng, sem, 0, 0

    def add(self, ins):
        ins.then_inc(self.sem, 1)
        self.k += 1

    def sync(self):
        self.eng.wait_ge(self.sem, self.base + self.k)

    def link(self, ins):
        self.add(ins)
        self.sync()

    def loop(self, start, stop, per, body):
        base, k = self.base, self.k
        with self.eng.Fori(start, stop) as i:
            self.base, self.k = i * per + (base + (k - start * per)), 0
            body(i)
            assert self.k == per, f"{self.sem}: a body counts {self.k}, not {per}"
        self.base, self.k = base, k + (stop - start) * per


def build(nc, node_table, x_dense, edge_table, index_chunks, src_cols, edge_rows, cf_in, ch_in, w1, b1, w2t, b2,
          g1t, gb1, g2t, gb2, embt, adaptt, gamma, beta, out):
    with ExitStack() as ctx:
        def sb(name, shape, dt=F32):
            return ctx.enter_context(nc.sbuf_tensor(name, shape, dt))

        def sem(name):
            return ctx.enter_context(nc.semaphore(name))

        def sems(name):
            return [sem(f"{name}{u}") for u in range(2)]

        def dram(name, shape, dt=F32):
            return nc.dram_tensor(name, shape, dt).ap()

        d_hilo = dram("d_hilo", (2, 2, EPAD), F16)
        d_src = dram("d_src", (1, EPAD))
        d_ptr = dram("d_ptr", (NPAD, 1), I32)
        d_sorted = dram("d_sorted", (EPAD, REC))
        d_table = [dram(f"d_table{b}", (EPAD, FW)) for b in range(3)]
        d_pref = [dram(f"d_pref{l}", (P, TILES * FW)) for l in range(4)]
        d_y = [dram(f"d_y{b}", (P, TILES * F)) for b in range(2)]
        d_nodes = dram("d_nodes", (P, TILES * 2 * NODE_W))
        d_gate = dram("d_gate", (P, TILES * F))
        sorted_pt = d_sorted.rearrange("(p t) c -> p t c", t=TILES)
        table_pt = [t.rearrange("(p t) c -> p (t c)", t=TILES) for t in d_table]

        cf = sb("cf", [P, K_W])
        cj = sb("cj", [P, J_W], F16)
        ident = cf[:, K_ID:K_ID + P]
        ident16 = cj[:, J_ID:J_ID + P]
        part0 = cf[:, K_PART:K_PART + 1]
        delta = cf[0:CH, K_DELTA:K_DELTA + CH]
        src_i = sb("src_i", [P, TILES], I32)
        src_f = sb("src_f", [P, TILES])
        hi_c = sb("hi_c", [P, TILES])
        lo_c = sb("lo_c", [P, TILES])
        col_i = sb("col_i", [P, 2, TILES], I32)
        w_sb = sb("w_sb", [F, 2, F])
        g1t_sb = sb("g1t_sb", [R_ATTR, H])
        g2t_sb = sb("g2t_sb", [H, F])
        gb1_sb = sb("gb1_sb", [H, 1])
        rows48 = sb("rows48", [P, 7, F])
        rsum = sb("rsum", [P, 2])
        embt_sb = sb("embt_sb", [EMB, NTYPE])
        adaptt_sb = sb("adaptt_sb", [EMB, EMB])
        vt_sb = sb("vt_sb", [EMB, NTYPE])
        tab_sb = sb("tab_sb", [NTYPE, NTYPE])
        eps_c = sb("eps_c", [P, 3])
        same = sb("same", [P, TILES * P])

        def arena16(at, n):
            return same[:, at:at + n // 2].bitcast(F16)

        oht = [arena16(b * 3136, GR * BINS) for b in range(2)]
        ohh = [arena16(6272 + b * 3136, GR * BINS) for b in range(2)]
        ohl = [arena16(12544 + b * 448, GR * P) for b in range(2)]
        hi_b = [arena16(13440 + b * 448, GC) for b in range(2)]
        lo_b = [arena16(14336 + b * 448, GC) for b in range(2)]
        src_b = [same[:, 15232 + b * GC:15232 + (b + 1) * GC] for b in range(2)]
        hit = [same[:, 17024 + b * GC:17024 + (b + 1) * GC] for b in range(2)]
        tab_a = [arena16(18816 + b * 448, BINS) for b in range(2)]
        tab_b = [arena16(19712 + b * 448, BINS) for b in range(2)]
        junk = arena16(20608, 28 * P)
        base_a, base_b = arena16(22400, BINS), arena16(22848, BINS)
        zero16 = arena16(23296, 512)
        rows_i = same[0:TILES // 2, 0:12 * P].bitcast(I32).rearrange("p (k c) -> p k c", k=3)
        rows_h = same[0:TILES // 2, 12 * P:16 * P].bitcast(F16).rearrange("p (k c) -> p k c", k=2)
        rows_f = same[0:TILES // 2, 16 * P:18 * P]
        cnt, has16 = same[:, 20608:20608 + BINS], arena16(20608 + BINS, BINS)
        incl, base, ones_w, cnt_a, cnt_b, incl_b, is_a, base_x = (same[:, (7 + k) * BINS:(8 + k) * BINS] for k in range(8))
        last_i, low_i, high_i = (same[:, k * BINS:(k + 1) * BINS].bitcast(I32) for k in range(3))
        empty_f, qf = (same[:, 17024 + k * BINS:17024 + (k + 1) * BINS] for k in range(2))
        ptr_i = same[:, 15232:15232 + BINS].bitcast(I32)

        off_c = sb("off_c", [P, 4])
        flag = sb("flag", [P, 2, GR])
        nb_f = sb("nb_f", [1, BODIES])
        nb_i = sb("nb_i", [1, 2], I32)
        eqs = sb("eqs", [P, 2, GR])
        rank_i = sb("rank_i", [P, 3, GR], I32)
        qidx = sb("qidx", [P, 2, CH], I32)
        idx = sb("idx", [P, 2, 2 * CH], I32)
        shared = sb("shared", [P, 2 * CH * (FW + XW + F)])
        rec = shared[:, 0:2 * CH * REC].rearrange("p (u t c) -> p u t c", u=2, t=CH)
        o1, o2 = 2 * CH * FW, 2 * CH * (FW + XW)
        stage = shared[:, 0:o1].rearrange("p (u t c) -> p u t c", u=2, t=CH)
        msg_f = shared[:, o1:o2].rearrange("p (u x) -> p u x", u=2)
        yb = shared[:, o2:o2 + 2 * CH * F].rearrange("p (u t c) -> p u t c", u=2, t=CH)
        key = sb("key", [P, TILES + 2])
        wcol = sb("wcol", [P, TILES])
        ptr = sb("ptr", [P, TILES], I32)
        vec_d = sb("vec_d", [P, TILES])
        typ_s = sb("typ_s", [P, TILES])
        first_k = sb("first_k", [P, TILES])
        last_k = sb("last_k", [P, TILES + 1])
        chainf = sb("chainf", [P, TILES])
        chaint = sb("chaint", [P, TILES])
        cwmj = sb("cwmj", [P, TILES])
        cw_i = sb("cw_i", [P, TILES], I32)
        out_i = sb("out_i", [P, TILES], I32)
        coef = sb("coef", [P, TILES])
        dis = sb("dis", [P, TILES])
        rtot = sb("rtot", [P, TILES])
        small = sb("small", [P, 4, CH])
        logit = sb("logit", [P, 2, GR])
        edgec = sb("edgec", [CH, 3])
        cont_m = sb("cont_m", [CH, CHUNKS * P])
        state = sb("state", [XW, 2, CH + 1])
        cont_s = sb("cont_s", [CH, 2, P])
        key_s = sb("key_s", [P, 2, CH + 1])
        typ_f = sb("typ_f", [P, 2, CH])
        cm = sb("cm", [CH, 2, CH * XW])
        aggt = sb("aggt", [XW, CH * P])
        lns = sb("lns", [P, 4, CH])
        pidx = sb("pidx", [P, 2, CH], I32)
        oidx = sb("oidx", [P, 2, CH], I32)
        row_st = sb("row_st", [P, 2, CH], I32)
        STT_AT = GR * XW + 3
        UNIT_W = CH * (5 * F + 3 * FW)
        late = sb("late", [P, CH * (2 * FW + 5 * F) + UNIT_W])
        ob = late[:, 0:2 * CH * FW].rearrange("p (u t c) -> p u t c", u=2, t=CH)
        gb = late[:, 2 * CH * FW:2 * CH * (FW + F)].rearrange("p (u t c) -> p u t c", u=2, t=CH)
        lnb = late[:, 2 * CH * (FW + F):CH * (2 * FW + 5 * F)].rearrange("p (k t c) -> p k t c", k=3, t=CH)
        unit = late[:, CH * (2 * FW + 5 * F):]
        cw_t = late[:, 2 * CH * (FW + F):2 * CH * (FW + F) + 3 * TILES].rearrange("p (k t) -> p k t", k=3)
        idx_all = late[:, 0:2 * TILES].bitcast(I32)
        ux, ut, usq, udone = (unit[:, 2 * k * CH * F:2 * (k + 1) * CH * F].rearrange("p (v t c) -> p v t c", v=2, c=F)
                              for k in range(4))
        uo = unit[:, 5 * CH * F:].rearrange("p (k t c) -> p k t c", k=3, c=FW)
        uns = sb("uns", [P, 6, 2, CH])
        attr_t = unit[0:R_ATTR, 0:GC]
        h1_t = unit[0:H, GC:2 * GC]
        oh_td = unit[:, 2 * GC:3 * GC]
        ujunk = unit[:, 3 * GC:3 * GC + GR * NTYPE].rearrange("p (k c) -> p k c", c=NTYPE)
        gst = unit[:, 3 * GC + GR * NTYPE:3 * GC + GR * NTYPE + 2 * GR * F].rearrange("p (u t c) -> p u t c", u=2, c=F)

        ps = ctx.enter_context(nc.psum_tensor("ps", [P, 8 * 512], F32))

        def bank(b, n=512, parts=P, at=0):
            return ps[0:parts, b * 512 + at:b * 512 + at + n]

        s_settled = sem("s_settled")
        s_const, s_eps, s_rows, s_hilo_w, s_src = sem("s_const"), sem("s_eps"), sem("s_rows"), sem("s_hilo_w"), sem("s_src")
        s_zero, s_oh, s_hist = sem("s_zero"), sems("s_oh"), sems("s_hist")
        s_incl, s_off, s_base, s_seed2, s_ptr, s_ptrw = (sem(n) for n in ("s_incl", "s_off", "s_base", "s_seed2", "s_ptr", "s_ptrw"))
        s_bd, s_dlook, s_dhit = sems("s_bd"), sems("s_dlook"), sems("s_dhit")
        s_cnt1, s_nb = sem("s_cnt1"), sem("s_nb")
        s_gd, s_xres, s_index = sems("s_gd"), sems("s_xres"), sem("s_index")
        s_own_c, s_own_u = sem("s_own_c"), sem("s_own_u")
        s_bc, s_oht, s_ohh, s_eq = sems("s_bc"), sems("s_oht"), sems("s_ohh"), sems("s_eq")
        s_ta, s_tb, s_look, s_upd = sems("s_ta"), sems("s_tb"), sems("s_look"), sems("s_upd")
        s_hit, s_sum, s_q, s_qh = sems("s_hit"), sems("s_sum"), sems("s_q"), sems("s_qh")
        s_idx, s_gath, s_edge, s_keyc, s_scat = sems("s_idx"), sems("s_gath"), sems("s_edge"), sems("s_keyc"), sems("s_scat")
        s_clear = sem("s_clear")
        s_own_v, s_own_p = sem("s_own_v"), sem("s_own_p")
        s_rec, s_cols, s_pref, s_prefw = sems("s_rec"), sems("s_cols"), sems("s_pref"), sems("s_prefw")
        s_kb, s_same, s_kt, s_cont = sem("s_kb"), sem("s_same"), sem("s_kt"), sem("s_cont")
        s_tdb, s_ohtd, s_u, s_logit = sem("s_tdb"), sem("s_ohtd"), sem("s_u"), sem("s_logit")
        s_at, s_atc, s_h1, s_h1s, s_gate, s_gst, s_gw = sem("s_at"), sem("s_atc"), sem("s_h1"), sem("s_h1s"), sem("s_gate"), sem("s_gst"), sems("s_gw")
        s_vt, s_vtc, s_tab, s_tabc = sem("s_vt"), sem("s_vtc"), sem("s_tab"), sem("s_tabc")
        s_next, s_outi, s_ang, s_sin, s_flags = sem("s_next"), sem("s_outi"), sem("s_ang"), sem("s_sin"), sem("s_flags")
        s_st, s_y, s_g = sems("s_st"), sems("s_y"), sems("s_g")
        s_pidx, s_gat = sems("s_pidx"), sems("s_gat")
        s_msg, s_tail, s_state, s_stt, s_cm, s_agg = sems("s_msg"), sems("s_tail"), sems("s_state"), sems("s_stt"), sems("s_cm"), sems("s_agg")
        s_out, s_outw, s_yo = sems("s_out"), sems("s_outw"), sems("s_yo")
        s_aggt, s_conts = sems("s_aggt"), sems("s_conts")
        ln_chunk = (sem("s_cen"), sem("s_sq"), sem("s_var"), sem("s_sd"), lnb, lns)
        s_ucen, s_usq, s_uvar, s_usd = sem("s_ucen"), sem("s_usq"), sem("s_uvar"), sem("s_usd")
        s_cnt, s_rt = sem("s_cnt"), sem("s_rt")
        s_ux, s_uo, s_uow = sem("s_ux"), sem("s_uo"), sem("s_uow")
        s_xvar, s_xsd = sem("s_xvar"), sem("s_xsd")
        s_final, s_oidx, s_gx = sems("s_final"), sems("s_oidx"), sem("s_gx")

        block = ctx.enter_context(nc.Block())
        consts = [(cf[:], cf_in), (cj[:], ch_in), (src_i[:], src_cols), (rows_i[:, 0, :], edge_rows),
                  (w_sb[:, 0, :], w1), (w_sb[:, 1, :], w2t), (g1t_sb[:], g1t), (g2t_sb[:], g2t), (gb1_sb[:], gb1),
                  (rows48[:, 0, :], b1.partition_broadcast(P)), (rows48[:, 1, :], b2.partition_broadcast(P)),
                  (rows48[:, 2, :], gb2.partition_broadcast(P)), (rows48[:, 3, :], gamma.partition_broadcast(P)),
                  (rows48[:, 4, :], beta.partition_broadcast(P)), (embt_sb[:], embt), (adaptt_sb[:], adaptt)]
        N_CONST = 16 * len(consts)

        FIRST, SECOND, STEP, LAST, LAYER1, LAYER2, LAYER3 = range(7)
        STEPS = K_STEPS - 3
        FULL = 2
        EDGE_LN, DENSE_LN = 3, 4
        PAIRS = 3
        EARLY_PAIRS = 1 + STEPS * PAIRS
        LATE_PAIRS = (UNITS // 2 - EARLY_PAIRS) // 3
        SCAT_ALL = BODIES * CH * 16
        UOW_ALL = (UNITS // 2 + 2 * BODIES * EDGE_LN) * 16
        UOW_EDGES = (EARLY_PAIRS + 2 * BODIES * EDGE_LN) * 16
        assert UNITS == 2 * (EARLY_PAIRS + 3 * LATE_PAIRS)
        GATHERED = {SECOND: 0, LAST: 2, LAYER1: 0, LAYER2: 1, LAYER3: 2}
        WRITTEN = {FIRST: 0, SECOND: 1, LAST: 0, LAYER1: 1, LAYER2: 2}

        def bodies_before(kind, s, nb):
            if kind <= SECOND:
                return kind * BODIES
            if kind == STEP:
                return s * nb + FULL * BODIES
            return nb * STEPS + (FULL + kind - LAST) * BODIES

        def gathers_before(kind, s, nb):
            if kind == SECOND:
                return 0
            return (s * nb if kind == STEP else nb * (STEPS + (kind - LAST))) + nb

        def counted_before(kind, s, nb):
            c = CHUNK_COUNTS
            if kind == FIRST:
                return 0
            if kind == SECOND:
                return c[FIRST] * BODIES
            if kind == STEP:
                return (s * nb) * c[STEP] + (c[FIRST] + c[SECOND]) * BODIES
            return (nb * STEPS) * c[STEP] + (c[FIRST] + c[SECOND] + sum(c[LAST:kind])) * BODIES

        def table_writes(kind, s, nb, i):
            if kind == FIRST:
                return i * 16
            if kind == SECOND:
                return i * 32 + BODIES * 16
            return (bodies_before(kind, s, nb) + i) * 16 + BODIES * 16

        def before_pair(q, late):
            return q + BODIES * (1 + late)

        def counted_units(kind, j):
            e, d = UNIT_COUNTS
            return j * e + (kind == LAST) * (BODIES * e + EARLY_PAIRS * d)

        def counted_pairs(q, late):
            e, d = UNIT_COUNTS
            return q * d + BODIES * e * (1 + late)

        def settled(eng):
            eng.sem_inc(s_settled, 1)

        def peeled(eng, chain, body):
            k0 = chain.k if chain else 0
            body(0, True)
            if chain:
                chain.loop(1, BODIES, chain.k - k0, lambda i: body(i, False))
            else:
                with eng.Fori(1, BODIES) as i:
                    body(i, False)

        def rest(eng, nb, body):
            with eng.If(nb > 2):
                with eng.Fori(2, nb) as i:
                    body(i)
            with eng.Else():
                settled(eng)

        def next_group(i, u, h):
            return (i, u, 1) if h == 0 else (i, 1, 0) if u == 0 else (i + 1, 0, 0)

        def peeled_ends(eng, chain, body):
            k0 = chain.k if chain else 0
            body(0, True, False)
            if chain:
                chain.loop(1, BODIES - 1, chain.k - k0, lambda i: body(i, False, False))
            else:
                with eng.Fori(1, BODIES - 1) as i:
                    body(i, False, False)
            body(BODIES - 1, False, True)

        def some_bodies(eng, nb, body):
            body(0)
            body(1)
            rest(eng, nb, body)

        def run_steps(eng, one_step):
            with eng.Fori(0, STEPS // 2) as o:
                for half in range(2):
                    one_step(o * 2 + half, half)
            one_step(STEPS - 1, 0)

        def load_bodies(eng):
            eng.wait_ge(s_nb, 1)
            return eng.value_load(nb_i[0:1, 0:1], min_val=2, max_val=BODIES)

        def load_last(eng):
            return eng.value_load(nb_i[0:1, 1:2], min_val=1, max_val=BODIES - 1)

        def ln_of_unit(kind, j, l):
            return j * EDGE_LN + (l + (kind == LAST) * (BODIES * EDGE_LN + EARLY_PAIRS * DENSE_LN * 2))

        def ln_of_pair(q, late, l):
            return q * (DENSE_LN * 2) + (BODIES * EDGE_LN * (1 + late) + 2 * l)

        def ln_of_chunk(kind, i, u, j=0):
            if kind == LAYER3:
                return i * 4 + (6 * BODIES + 2 * u + j)
            return i * 2 + ((kind - LAST) * 2 * BODIES + u)

        def chunk_cols(i, u, width=1, extra=0):
            return bass.ds(i * (2 * CH * width) + (u * CH * width + extra), CH * width)

        @block.sync
        def _(sp):
            sp.dma_start(idx_all, index_chunks).then_inc(s_index, 16)
            for dst, src in consts:
                sp.dma_start(dst, src).then_inc(s_const, 16)
            sp.wait_ge(s_rows, 1)
            for k in range(2):
                sp.dma_start(d_hilo[k].rearrange("w (q c) -> q w c", c=2 * P),
                             rows_h[:, k, :].rearrange("q (w c) -> q w c", w=2)).then_inc(s_hilo_w, 16)
            sp.dma_start(d_src[0].rearrange("(q c) -> q c", c=2 * P), rows_f).then_inc(s_hilo_w, 16)
            sp.wait_ge(s_hilo_w, 48)

            def flag_loads(i, first):
                for u in range(2):
                    for h in range(2):
                        at = bass.ds(i * (4 * GC) + (2 * u + h) * GC, GC)
                        if not (first and u == 0):
                            sp.wait_ge(s_oht[h], i * 2 + u)
                        sp.dma_start(hi_b[h], d_hilo[0, 1, at].partition_broadcast(P)).then_inc(s_bd[h], 16)
                        if not (first and u == 0):
                            sp.wait_ge(s_dhit[h], i * 2 + u)
                        sp.dma_start(lo_b[h], d_hilo[1, 1, at].partition_broadcast(P)).then_inc(s_bc[h], 16)
            peeled(sp, None, flag_loads)
            sp.wait_ge(s_ptr, 1)
            sp.dma_start(d_ptr.rearrange("(b p l) c -> p b (l c)", b=NB, p=P),
                         ptr_i.rearrange("p (b l) -> p b l", b=NB)).then_inc(s_ptrw, 16)
            sp.wait_ge(s_ptrw, 16)

            def rank_loads(i, first):
                for u in range(2):
                    for h in range(2):
                        at = bass.ds(i * (4 * GC) + (2 * u + h) * GC, GC)
                        if not (first and u == 0):
                            sp.wait_ge(s_oht[h], i * 2 + (u + 2 * BODIES))
                        sp.dma_start(hi_b[h], d_hilo[0, 0, at].partition_broadcast(P)).then_inc(s_bd[h], 16)
                        if not (first and u == 0):
                            sp.wait_ge(s_eq[h], i * 2 + u)
                            sp.wait_ge(s_hit[h], i * 2 + u)
                        sp.dma_start(lo_b[h], d_hilo[1, 0, at].partition_broadcast(P)).then_inc(s_bc[h], 16)
                        sp.dma_start(src_b[h], d_src[0, at].partition_broadcast(P)).then_inc(s_bc[h], 16)
            peeled(sp, None, rank_loads)
            for u in range(2):
                sp.wait_ge(s_scat[u], SCAT_ALL)

            def record_loads(i, first):
                for u in range(2):
                    if not first:
                        sp.wait_ge(s_yo[u], i * 16)
                        sp.wait_ge(s_pref[u], i)
                        sp.wait_ge(s_cols[u], i)
                        sp.wait_ge(s_at, i * 4 + (2 * u - 2))
                    sp.dma_start(rec[:, u], sorted_pt[:, bass.ds(i * (2 * CH) + u * CH, CH), :]).then_inc(s_rec[u], 16)
            peeled(sp, None, record_loads)
            for u in range(2):
                sp.wait_ge(s_prefw[u], BODIES * 16)
                sp.wait_ge(s_yo[u], BODIES * 16)
                sp.wait_ge(s_gw[u], 2 * BODIES * 16)
            sp.wait_ge(s_outi, 1)

            nb = load_bodies(sp)

            def results(kind, s, i, u, half=0, back=0):
                rows = ob[:, u].rearrange("p t c -> p (t c)")
                cols = chunk_cols(i, u, FW, -2 * CH * FW * back)
                if kind != LAYER3:
                    sp.dma_start(table_pt[2 - half if kind == STEP else WRITTEN[kind]][:, cols], rows).then_inc(s_outw[u], 16)
                if kind == SECOND:
                    sp.dma_start(table_pt[2][:, cols], rows).then_inc(s_outw[u], 16)
                if LAST <= kind < LAYER3:
                    sp.dma_start(d_y[kind in (LAST, LAYER2)][:, chunk_cols(i, u, F, -2 * CH * F * back)].rearrange("p (t c) -> p t c", c=F),
                                 ob[:, u, :, 0:F]).then_inc(s_yo[u], 16)

            def unit_values(kind, j, back=0):
                sp.wait_ge(s_uo, j + (1 - back + (kind == LAST) * (BODIES + EARLY_PAIRS)))
                at = bass.ds(j * (CH * FW) + ((kind == LAST) * BODIES - back) * CH * FW, CH * FW)
                for l in range(EDGE_LN):
                    sp.dma_start(d_pref[l + 1][:, at], uo[:, l].rearrange("p t c -> p (t c)")).then_inc(s_uow, 16)

            def body_traffic(kind, s, i, half=0, start=False, first=False):
                m = bodies_before(kind, s, nb) + i
                for u in range(2):
                    if not first:
                        sp.wait_ge(s_msg[u], m)
                    tiles = bass.ds(i * (2 * CH) + u * CH, CH)
                    if kind == FIRST:
                        sp.dma_start(stage[:, u, :, 0:F], sorted_pt[:, tiles, 0:F]).then_inc(s_st[u], 16)
                    else:
                        sp.dma_start(stage[:, u].rearrange("p t c -> p (t c)"),
                                     d_pref[max(0, kind - LAST)][:, chunk_cols(i, u, FW)]).then_inc(s_st[u], 16)
                    if kind == LAYER3:
                        sp.dma_start(gb[:, u].rearrange("p t c -> p (t c)"),
                                     d_gate[:, chunk_cols(i, u, F)]).then_inc(s_g[u], 16)
                if kind in (FIRST, LAST):
                    if not start:
                        unit_values(kind, i, 1)
                        sp.wait_ge(s_ucen, ln_of_unit(kind, i, 1 - EDGE_LN))
                    sp.dma_start(ux[:, 0], sorted_pt[:, bass.ds(i * CH + (kind == LAST) * BODIES * CH, CH), 0:F]).then_inc(s_ux, 16)
                for u in range(2):
                    if not first:
                        sp.wait_ge(s_out[u], m)
                    if not start:
                        results(kind, s, i, u, half, 1)
                    sp.dma_start(yb[:, u].rearrange("p t c -> p (t c)"),
                                 d_y[kind in (LAYER1, LAYER3)][:, chunk_cols(i, u, F)]).then_inc(s_y[u], 16)

            def pass_traffic(kind):
                body_traffic(kind, 0, 0, start=True, first=kind == FIRST)
                with sp.Fori(1, BODIES) as i:
                    body_traffic(kind, 0, i)
                if kind in (FIRST, LAST):
                    unit_values(kind, BODIES - 1)
                for u in range(2):
                    if kind != LAYER3:
                        sp.wait_ge(s_out[u], bodies_before(kind, 0, nb) + BODIES)
                        results(kind, 0, BODIES - 1, u)

            def step_traffic(s, half):
                body_traffic(STEP, s, 0, half, start=True)
                body_traffic(STEP, s, 1, half)
                rest(sp, nb, lambda i: body_traffic(STEP, s, i, half))
                for u in range(2):
                    sp.wait_ge(s_out[u], bodies_before(STEP, s, nb) + nb)
                    results(STEP, s, last_a, u, half)

            last_a = load_last(sp)
            pass_traffic(FIRST)
            pass_traffic(SECOND)
            run_steps(sp, step_traffic)
            sp.wait_ge(s_ucen, ln_of_pair(EARLY_PAIRS - 1, False, 0) + 2)
            for n, kind in enumerate((LAST, LAYER1, LAYER2, LAYER3)):
                if kind == LAYER1:
                    sp.wait_ge(s_uow, UOW_EDGES)
                for u in range(2):
                    if n:
                        sp.wait_ge(s_yo[u], (n + 1) * BODIES * 16)
                pass_traffic(kind)

        @block.gpsimd
        def _(pool):
            own = Chain(pool, s_own_p)
            pool.memset(shared[:], 0.0).then_inc(s_clear, 1)
            pool.wait_ge(s_clear, 1)

            def gather(dst, table, index, rows, done):
                pool.indirect_dma_start(dst, None, table, bass.IndirectOffsetOnAxis(ap=index, axis=0),
                                        bounds_check=rows - 1, oob_is_err=False).then_inc(done, 16)

            def scatter(table, index, rows, src, done):
                pool.indirect_dma_start(table, bass.IndirectOffsetOnAxis(ap=index, axis=0), src, None,
                                        bounds_check=rows - 1, oob_is_err=False).then_inc(done, 16)

            def chunk_index(i, u, count):
                settled(pool)
                pool.tensor_copy(idx[:, u, :], idx_all[:, chunk_cols(i, u, 2)]).then_inc(s_idx[u], 1)
                pool.wait_ge(s_idx[u], count)

            pool.wait_ge(s_index, 16)

            def keep(i, u):
                pool.wait_ge(s_gd[u], i * (32 * CH) + 32 * CH)
                settled(pool)
                pool.dma_start(d_nodes[:, chunk_cols(i, u, 2 * NODE_W)].rearrange("p (t c) -> p t c", c=2 * NODE_W),
                               rec[:, u, :, 0:2 * NODE_W]).then_inc(s_xres[u], 16)

            def at_nodes(i, first):
                for u in range(2):
                    if not first:
                        pool.wait_ge(s_xres[u], i * 16)
                    chunk_index(i, u, i + 1)
                    settled(pool)
                    for k in range(CH):
                        gather(rec[:, u, k, 0:NODE_W], node_table, idx[:, u, k:k + 1], NODES, s_gd[u])
                        gather(rec[:, u, k, C_SRCX:C_SRCX + NODE_W], node_table, idx[:, u, CH + k:CH + k + 1], NODES, s_gd[u])
                        if k == 3 and u == 1:
                            keep(i, 0)
                        elif k == 3 and not first:
                            keep(i - 1, 1)
                            settled(pool)
            at_nodes(0, True)
            with pool.Fori(1, BODIES) as i:
                at_nodes(i, False)
            keep(BODIES - 1, 1)

            def records(i, first):
                for u in range(2):
                    pool.wait_ge(s_edge[u], i * 32 + 32)
                    pool.wait_ge(s_keyc[u], i + 1)
                    pool.wait_ge(s_qh[u], i + 1)
                    settled(pool)
                    for k in range(CH):
                        scatter(d_sorted, qidx[:, u, k:k + 1], EPAD, rec[:, u, k, :], s_scat[u])
            peeled(pool, None, records)

            own.add(pool.memset(key[:], -1.0))
            own.add(pool.memset(key_s[:], -1.0))
            own.sync()

            def small_columns(i, first):
                for u in range(2):
                    at = chunk_cols(i, u)
                    pool.wait_ge(s_rec[u], i * 16 + 16)
                    if not first:
                        pool.wait_ge(s_same, i * 4 + (2 * u - 2))
                        pool.wait_ge(s_kt, i * 2 + (u - 1))
                        pool.wait_ge(s_tdb, i * 4 + (2 * u - 2))
                    if not (first and u == 0):
                        settled(pool)
                        own.link(pool.tensor_copy(key_s[:, u, 0:1], key_s[:, 1 - u, CH:CH + 1]))
                    settled(pool)
                    own.add(pool.tensor_copy(key_s[:, u, 1:CH + 1], rec[:, u, :, C_KEY]))
                    own.add(pool.tensor_copy(typ_f[:, u, :], rec[:, u, :, F + 1].bitcast(I32)))
                    own.sync()
                    settled(pool)
                    pool.tensor_copy(key[:, chunk_cols(i, u, 1, 1)], rec[:, u, :, C_KEY])
                    pool.tensor_copy(wcol[:, at], rec[:, u, :, C_W])
                    pool.tensor_copy(ptr[:, at], rec[:, u, :, C_DST])
                    pool.tensor_copy(vec_d[:, at], rec[:, u, :, F])
                    pool.tensor_copy(typ_s[:, at], rec[:, u, :, C_SRCX + F + 1].bitcast(I32)).then_inc(s_cols[u], 1)
            small_columns(0, True)
            own.loop(1, BODIES, 6, lambda i: small_columns(i, False))

            pool.wait_ge(s_ptrw, 16)

            def table_rows(i, first):
                for u in range(2):
                    if not first:
                        pool.wait_ge(s_gath[u], i * (16 * CH))
                        settled(pool)
                        own.link(pool.tensor_copy(ptr[:, chunk_cols(i, u, 1, -2 * CH)], row_st[:, u, :]))
                    settled(pool)
                    own.link(pool.tensor_copy(idx[:, u, 0:CH], ptr[:, chunk_cols(i, u)]))
                    settled(pool)
                    for k in range(CH):
                        gather(row_st[:, u, k:k + 1], d_ptr, idx[:, u, k:k + 1], NPAD, s_gath[u])
            own.sync()
            table_rows(0, True)
            own.loop(1, BODIES, 4, lambda i: table_rows(i, False))
            for u in range(2):
                pool.wait_ge(s_gath[u], BODIES * 16 * CH)
                settled(pool)
                own.link(pool.tensor_copy(ptr[:, chunk_cols(BODIES - 1, u)], row_st[:, u, :]))

            nb = load_bodies(pool)

            def pass_gathers(kind, s, table, i):
                m = bodies_before(kind, s, nb) + i
                g = gathers_before(kind, s, nb) + i if kind != SECOND else i
                for u in range(2):
                    pool.wait_ge(s_msg[u], m)
                    settled(pool)
                    pool.tensor_copy(pidx[:, u, :], ptr[:, chunk_cols(i, u)]).then_inc(s_pidx[u], 1)
                    pool.wait_ge(s_pidx[u], g + 1)
                    pool.wait_ge(s_st[u], m * 16 + 16)
                    settled(pool)
                    for k in range(CH):
                        gather(stage[:, u, k, :], d_table[table], pidx[:, u, k:k + 1], EPAD, s_gat[u])

            def gather_pass(kind, s, table):
                for u in range(2):
                    pool.wait_ge(s_outw[u], table_writes(kind, s, nb, 0))
                settled(pool)
                some_bodies(pool, nb, lambda i: pass_gathers(kind, s, table, i))
            gather_pass(SECOND, 0, GATHERED[SECOND])
            run_steps(pool, lambda s, half: gather_pass(STEP, s, 1 + half))
            for kind in (LAST, LAYER1, LAYER2):
                gather_pass(kind, 0, GATHERED[kind])

            def final_index(i, u):
                settled(pool)
                pool.tensor_copy(oidx[:, u, :], out_i[:, chunk_cols(i, u)]).then_inc(s_oidx[u], 1)
                pool.wait_ge(s_oidx[u], i + 1)

            def final_rows(i, first=False):
                for u in range(2):
                    if not first:
                        pool.wait_ge(s_final[u], i * (16 * CH))
                        final_index(i, u)
                for u in range(2):
                    pool.wait_ge(s_out[u], bodies_before(LAYER3, 0, nb) + i + 1)
                    settled(pool)
                    for k in range(CH):
                        scatter(out, oidx[:, u, k:k + 1], NODES, ob[:, u, k, 0:F], s_final[u])

            for u in range(2):
                pool.wait_ge(s_outw[u], table_writes(LAYER3, 0, nb, 0))
            pool.wait_ge(s_outi, 1)
            final_index(0, 0)
            final_index(0, 1)
            pass_gathers(LAYER3, 0, GATHERED[LAYER3], 0)
            pass_gathers(LAYER3, 0, GATHERED[LAYER3], 1)
            pool.wait_ge(s_uow, UOW_ALL)
            final_rows(0, True)
            last_a = load_last(pool)
            with pool.If(nb > 2):
                with pool.Fori(1, last_a) as i:
                    pass_gathers(LAYER3, 0, GATHERED[LAYER3], i + 1)
                    final_rows(i)
            with pool.Else():
                settled(pool)
            with pool.Fori(last_a, BODIES) as i:
                final_rows(i)
            for u in range(2):
                pool.wait_ge(s_final[u], SCAT_ALL)

        @block.scalar
        def _(act):
            act.wait_ge(s_vt, 1)
            nc.scalar.copy(vt_sb[:], bank(7, NTYPE, EMB)).then_inc(s_vtc, 1)
            act.wait_ge(s_clear, 1)

            def record_parts(i, u, first):
                if first and u == 0:
                    for w in range(2):
                        act.wait_ge(s_xres[w], 16 * BODIES)
                if not first:
                    act.wait_ge(s_scat[u], i * (16 * CH))
                act.dma_start(rec[:, u, :, 0:2 * NODE_W],
                              d_nodes[:, chunk_cols(i, u, 2 * NODE_W)].rearrange("p (t c) -> p t c", c=2 * NODE_W)).then_inc(s_edge[u], 16)
                act.dma_start(rec[:, u, :, C_ATTR:C_ATTR + EDGE_W],
                              edge_table[:, chunk_cols(i, u, EDGE_W)].rearrange("p (t c) -> p t c", c=EDGE_W)).then_inc(s_edge[u], 16)
                nc.scalar.copy(rec[:, u, :, C_DST], idx_all[:, bass.ds(i * (4 * CH) + u * 2 * CH, CH)])
                nc.scalar.copy(rec[:, u, :, C_KEY], src_f[:, chunk_cols(i, u)]).then_inc(s_keyc[u], 1)

            def group_tables(i, first):
                for u in range(2):
                    for h in range(2):
                        n = i * 2 + u
                        if h == 1:
                            act.wait_ge(s_upd[0], n + 1)
                        elif first and u == 0:
                            act.wait_ge(s_seed2, 1)
                        else:
                            act.wait_ge(s_upd[1], n)
                        if not (first and u == 0):
                            act.wait_ge(s_look[h], n)
                        nc.scalar.copy(tab_a[h], ps[:, 0:BINS]).then_inc(s_ta[h], 1)
                    if not first:
                        record_parts(i, u, first)
                if first:
                    record_parts(i, 0, first)
                    record_parts(i, 1, first)
            act.wait_ge(s_src, 1)
            peeled(act, None, group_tables)

            def act_gates(i, first):
                for u in range(2):
                    act.wait_ge(s_rec[u], i * 16 + 16)
                    if not first:
                        act.wait_ge(s_prefw[u], i * 16)
                    nc.scalar.mul(ob[:, u, :, 0:F], rec[:, u, :, 0:F], ALPHA).then_inc(s_pref[u], 1)
                    act.wait_ge(s_pref[u], i + 1)
                    act.dma_start(d_pref[0][:, chunk_cols(i, u, FW)], ob[:, u].rearrange("p t c -> p (t c)")).then_inc(s_prefw[u], 16)
                    act.dma_start(d_y[0][:, chunk_cols(i, u, F)].rearrange("p (t c) -> p t c", c=F),
                                  rec[:, u, :, C_SRCX:C_SRCX + F]).then_inc(s_yo[u], 16)
                    for h in range(2):
                        q = i * 4 + (2 * u + h)
                        free = not (first and u == 0 and h == 0)
                        act.wait_ge(s_at, q + 1)
                        if free:
                            act.wait_ge(s_h1, q)
                        nc.scalar.copy(attr_t, bank(4, GC, R_ATTR)).then_inc(s_atc, 1)
                        act.wait_ge(s_h1, q + 1)
                        if free:
                            act.wait_ge(s_gate, q)
                        nc.scalar.activation(h1_t, bank(6, GC, H), ACT.Silu, bias=gb1_sb[:, 0:1]).then_inc(s_h1s, 1)
                        act.wait_ge(s_gst, q + 1)
                        act.dma_start(d_gate[:, bass.ds(i * (4 * GR * F) + (2 * u + h) * GR * F, GR * F)],
                                      gst[:, h].rearrange("p t c -> p (t c)")).then_inc(s_gw[h], 16)
            act.wait_ge(s_tab, 1)
            nc.scalar.copy(tab_sb[:], bank(7, NTYPE, NTYPE, 128)).then_inc(s_tabc, 1)
            act.wait_ge(s_const, N_CONST)
            act.wait_ge(s_eps, 2)
            peeled(act, None, act_gates)
            act.wait_ge(s_ang, 1)
            nc.scalar.activation(cw_t[:, 2, :], cw_t[:, 1, :], ACT.Sin, bias=eps_c[:, 1:2], scale=-float(np.pi) / CUTOFF).then_inc(s_sin, 1)

            def square(n):
                cen, sq, _, _, buf, _ = ln_chunk
                act.wait_ge(cen, n + 1)
                nc.scalar.activation(buf[:, 1], buf[:, 0], ACT.Square).then_inc(sq, 1)

            def root(n):
                _, _, var, sd, _, st = ln_chunk
                act.wait_ge(var, n + 1)
                nc.scalar.activation(st[:, 2], st[:, 1], ACT.Sqrt, bias=eps_c[:, 0:1], scale=1.0 / F).then_inc(sd, 1)

            def unit_squares(n, units=1):
                for w in range(units):
                    act.wait_ge(s_ucen, n + (w + 1))
                    nc.scalar.activation(usq[:, w], ut[:, w], ACT.Square).then_inc(s_usq, 1)

            def unit_roots(n, l, units=1):
                for w in range(units):
                    act.wait_ge(s_uvar, n + (w + 1))
                    eps = eps_c[:, 2:3] if l == 0 else eps_c[:, 0:1]
                    nc.scalar.activation(uns[:, 2, w], uns[:, 1, w], ACT.Sqrt, bias=eps, scale=1.0 / F).then_inc(s_usd, 1)

            nb = load_bodies(act)

            out_dense = out.rearrange("(p t) c -> p (t c)", p=P)

            def load_pair(q):
                act.dma_start(ux.rearrange("p v t c -> p (v t c)"),
                              x_dense[:, bass.ds(q * (2 * CH * F), 2 * CH * F)]).then_inc(s_ux, 16)

            def positions(kind, s, i, u, first=False):
                if not first:
                    act.wait_ge(s_agg[u], bodies_before(kind, s, nb) + i)
                nc.scalar.copy(cont_s[:, u, :], cont_m[:, bass.ds(i * (2 * P) + u * P, P)]).then_inc(s_conts[u], 1)

            def sums(kind, s, i, u, first=False):
                m = bodies_before(kind, s, nb) + i
                width = XW if kind == FIRST else F
                act.wait_ge(s_tail[u], m + 1)
                if not (first and u == 0):
                    act.wait_ge(s_agg[1 - u], m + u)
                nc.scalar.copy(aggt[0:width, :], ps[0:width, 0:CH * P]).then_inc(s_aggt[u], 1)

            def chunk_end(kind, s, i, u, half=0):
                if kind == FIRST:
                    act.wait_ge(s_cnt, i * 2 + (u + 1))
                    nc.scalar.activation(small[:, 1], small[:, 0], ACT.Sqrt).then_inc(s_rt, 1)
                if kind >= LAST:
                    for l in range(2 if kind == LAYER3 else 1):
                        n = ln_of_chunk(kind, i, u, l)
                        square(n)
                        root(n)
            def body_with_unit(kind, i, first=False):
                sums(kind, 0, i, 0, first)
                positions(kind, 0, i, 0, first)
                positions(kind, 0, i, 1, first)
                for l in range(EDGE_LN):
                    n = ln_of_unit(kind, i, l)
                    unit_squares(n)
                    unit_roots(n, l)
                sums(kind, 0, i, 1, first)
                chunk_end(kind, 0, i, 0)
                chunk_end(kind, 0, i, 1)

            def plain_body(kind, s, i, half=0):
                sums(kind, s, i, 0)
                positions(kind, s, i, 0)
                positions(kind, s, i, 1)
                sums(kind, s, i, 1)
                chunk_end(kind, s, i, 0, half)
                chunk_end(kind, s, i, 1, half)

            def act_pair(q, late=False, more=True, around=None):
                if around is not None:
                    s, i, half = around
                    positions(STEP, s, i, 0)
                    positions(STEP, s, i, 1)
                for l in range(DENSE_LN):
                    n = ln_of_pair(q, late, l)
                    unit_squares(n, 2)
                    if l == 0 and more:
                        load_pair(q + 1)
                    unit_roots(n, l, 2)
                    if l == 0 and around is not None:
                        sums(STEP, s, i, 0)
                    if l == 2:
                        for w in range(2):
                            act.wait_ge(s_xvar, q * 2 + (w + 1))
                            nc.scalar.activation(uns[:, 5, w], uns[:, 4, w], ACT.Sqrt, bias=eps_c[:, 0:1], scale=1.0 / F).then_inc(s_xsd, 1)
                        if around is not None:
                            sums(STEP, s, i, 1)
                            chunk_end(STEP, s, i, 0, half)
                act.wait_ge(s_uo, before_pair(q, late) + 1)
                act.dma_start(out_dense[:, bass.ds(q * (2 * CH * F), 2 * CH * F)], udone.rearrange("p v t c -> p (v t c)")).then_inc(s_uow, 16)
                if around is not None:
                    chunk_end(STEP, s, i, 1, half)

            def act_step(s, half):
                q = s * PAIRS + 1
                act_pair(q, around=(s, 0, half))
                act_pair(q + 1, around=(s, 1, half))
                rest(act, nb, lambda i: plain_body(STEP, s, i, half))
                act_pair(q + 2, more=not isinstance(s, int))

            peeled(act, None, lambda i, first: body_with_unit(FIRST, i, first))
            act.wait_ge(s_uow, BODIES * EDGE_LN * 16)
            load_pair(0)
            act_pair(0)
            with act.Fori(0, BODIES) as i:
                plain_body(SECOND, 0, i)
            run_steps(act, act_step)
            with act.Fori(0, BODIES) as i:
                body_with_unit(LAST, i)
            act.wait_ge(s_uow, UOW_EDGES)
            load_pair(EARLY_PAIRS)
            for kind in (LAYER1, LAYER2, LAYER3):
                for p in range(LATE_PAIRS):
                    q = EARLY_PAIRS + (kind - LAYER1) * LATE_PAIRS + p
                    act_pair(q, late=True, more=q + 1 < UNITS // 2)
                with act.Fori(0, BODIES) as i:
                    plain_body(kind, 0, i)

        @block.vector
        def _(dve):
            own, own_c, own_u = Chain(dve, s_own_v), Chain(dve, s_own_c), Chain(dve, s_own_u)
            v = nc.vector

            v.memset(eps_c[:, 0:1], EPS)
            v.memset(eps_c[:, 2:3], EPS / (1.0 + ALPHA) ** 2)
            v.memset(eps_c[:, 1:2], float(np.pi) / 2).then_inc(s_eps, 1)
            v.memset(zero16, 0.0).then_inc(s_zero, 1)
            own.add(v.memset(state[:], 0.0))
            own.add(v.memset(last_k[:], -1.0))
            dve.wait_ge(s_const, N_CONST)
            own.add(v.tensor_scalar(rows_i[:, 1, :], rows_i[:, 0, :], 7, None, ALU.arith_shift_right))
            own.add(v.tensor_scalar(rows_i[:, 2, :], rows_i[:, 0, :], P - 1, None, ALU.bitwise_and))
            own.sync()
            own.add(v.tensor_copy(rows_h, rows_i[:, 1:3, :]))
            own.add(v.tensor_scalar(rows48[:, 5, :], rows48[:, 1, :], 0.0, None, ALU.max))
            own.sync()
            v.tensor_copy(rows_f, rows_i[:, 0, 0:2 * P]).then_inc(s_rows, 1)
            own.add(v.tensor_copy(rows48[:, 6, :], rows48[:, 0, :]))
            own.sync()
            own.link(v.tensor_reduce(rsum[:], rows48[:, 5:7, :], AX_X, ALU.add))
            own.link(v.scalar_tensor_tensor(rows48[:, 5:7, :], rsum[:].unsqueeze(2).broadcast_to([P, 2, F]), -1.0 / F,
                                            rows48[:, 5:7, :], ALU.mult, ALU.add))
            own.add(v.tensor_scalar(col_i[:, 0, :], src_i[:], 7, None, ALU.arith_shift_right))
            own.add(v.tensor_scalar(col_i[:, 1, :], src_i[:], P - 1, None, ALU.bitwise_and))
            own.sync()
            own.add(v.tensor_copy(hi_c[:], col_i[:, 0, :]))
            own.add(v.tensor_copy(lo_c[:], col_i[:, 1, :]))
            own.sync()
            v.tensor_copy(src_f[:], src_i[:]).then_inc(s_src, 1)
            iota = cj[:, J_IOTA:J_IOTA + BINS]

            def one_hots_high(h, first_tile):
                for k in range(GR):
                    v.tensor_scalar(ohh[h][:, k * BINS:(k + 1) * BINS], iota, hi_c[:, bass.ds(first_tile + k, 1)], None, ALU.is_equal)

            def one_hots_low(h, first_tile, done, flags=None):
                for k in range(GR):
                    args = (None, ALU.is_equal) if flags is None else (flags[:, k:k + 1], ALU.is_equal, ALU.mult)
                    ins = v.tensor_scalar(ohl[h][:, k * P:(k + 1) * P], iota[:, 0:P], lo_c[:, bass.ds(first_tile + k, 1)], *args)
                ins.then_inc(done, 1)

            def one_hots(h, first_tile, done):
                one_hots_high(h, first_tile)
                one_hots_low(h, first_tile, done)

            def one_hots_across(h, done):
                for b in range(NB):
                    ins = v.tensor_scalar(oht[h][:, b * GC:(b + 1) * GC], hi_b[h], cf[:, K_PART + b:K_PART + b + 1], None, ALU.is_equal)
                ins.then_inc(done, 1)

            def pick(h, done):
                v.scalar_tensor_tensor(hit[h], lo_b[h], part0, ps[:, (2 + 2 * h) * 512:(2 + 2 * h) * 512 + GC],
                                       ALU.is_equal, ALU.mult).then_inc(done, 1)

            def histogram(i, first):
                for u in range(2):
                    for h in range(2):
                        if not (first and u == 0):
                            dve.wait_ge(s_hist[h], i * 2 + u)
                        one_hots(h, i * (2 * CH) + (u * CH + h * GR), s_oh[h])
            peeled(dve, None, histogram)

            for h in range(2):
                dve.wait_ge(s_hist[h], 2 * BODIES)
            own.link(v.tensor_copy(cnt, ps[:, 0:BINS]))
            v.tensor_scalar(has16, cnt, 0.0, None, ALU.is_gt).then_inc(s_cnt1, 1)

            def flag_across(i, u, h, fresh):
                n = i * 2 + u
                dve.wait_ge(s_bd[h], n * 16 + 16)
                if not fresh:
                    dve.wait_ge(s_dlook[h], n)
                one_hots_across(h, s_oht[h])

            def active(i, first, last):
                for u in range(2):
                    for h in range(2):
                        n = i * 2 + u
                        fresh = first and u == 0
                        t0 = i * (2 * CH) + (u * CH + h * GR)
                        if not (last and u + h == 2):
                            flag_across(*next_group(i, u, h), fresh and h == 0)
                        dve.wait_ge(s_dlook[h], n + 1)
                        if not fresh:
                            dve.wait_ge(s_sum[h], n)
                        dve.wait_ge(s_bc[h], n * 16 + 16)
                        pick(h, s_dhit[h])
                        if not fresh:
                            dve.wait_ge(s_hist[h], n + 2 * BODIES)
                        one_hots_high(h, t0)
                        dve.wait_ge(s_sum[h], n + 1)
                        if not fresh:
                            dve.wait_ge(s_oh[h], n + 2 * BODIES)
                        settled(dve)
                        own.link(v.tensor_copy(flag[:, h, :], bank(6 + h, GR)))
                        one_hots_low(h, t0, s_oh[h], flag[:, h, :])
            flag_across(0, 0, 0, True)
            peeled_ends(dve, own, active)

            for h in range(2):
                dve.wait_ge(s_hist[h], 4 * BODIES)
            own.add(v.tensor_scalar(is_a, ps[:, 0:BINS], 0.0, None, ALU.is_gt))
            own.add(v.memset(ones_w, 1.0))
            own.sync()
            own.link(v.tensor_tensor(cnt_a, cnt, is_a, ALU.mult))
            own.add(v.tensor_tensor(cnt_b, cnt, cnt_a, ALU.subtract))
            own.add(v.tensor_tensor_scan(incl, ones_w, cnt_a, 0.0, ALU.mult, ALU.add))
            own.sync()
            v.tensor_tensor_scan(incl_b, ones_w, cnt_b, 0.0, ALU.mult, ALU.add).then_inc(s_incl, 1)
            dve.wait_ge(s_off, 1)
            own.link(v.tensor_copy(off_c[:, 0:3], bank(2, 3)))
            own.link(v.tensor_tensor(off_c[:, 3:4], off_c[:, 1:2], off_c[:, 2:3], ALU.add))
            own.add(v.scalar_tensor_tensor(base_x, incl, off_c[:, 0:1], cnt_a, ALU.add, ALU.subtract))
            own.add(v.scalar_tensor_tensor(base, incl_b, off_c[:, 3:4], cnt_b, ALU.add, ALU.subtract))
            own.sync()
            own.link(v.tensor_tensor(base_x, base_x, base, ALU.subtract))
            own.link(v.tensor_tensor(base_x, base_x, is_a, ALU.mult))
            own.link(v.tensor_tensor(base, base, base_x, ALU.add))
            own.link(v.tensor_copy(base_a, base))
            v.tensor_tensor(base_b, base, base_a, ALU.subtract).then_inc(s_base, 1)
            own.link(v.tensor_scalar(nb_f[:, 0:BODIES - 2], cf[0:1, K_LIMIT:K_LIMIT + BODIES - 2], off_c[0:1, 2:3], None, ALU.is_lt))
            own.link(v.tensor_reduce(nb_f[:, BODIES - 2:BODIES - 1], nb_f[:, 0:BODIES - 2], AX_X, ALU.add))
            own.add(v.tensor_scalar(nb_i[:, 1:2], nb_f[:, BODIES - 2:BODIES - 1], 1.0, None, ALU.add))
            v.tensor_scalar(nb_i[:, 0:1], nb_f[:, BODIES - 2:BODIES - 1], 2.0, None, ALU.add).then_inc(s_nb, 1)
            own.link(v.scalar_tensor_tensor(last_i, base, -1.0, cnt, ALU.add, ALU.add))
            own.add(v.tensor_scalar(low_i, last_i, P - 1, None, ALU.bitwise_and))
            own.add(v.tensor_scalar(high_i, last_i, 7, None, ALU.arith_shift_right))
            own.add(v.tensor_scalar(empty_f, cnt, 0.0, FAR, ALU.is_equal, ALU.mult))
            own.sync()
            own.link(v.scalar_tensor_tensor(qf, low_i, float(TILES), high_i, ALU.mult, ALU.add))
            v.tensor_tensor(ptr_i, qf, empty_f, ALU.add).then_inc(s_ptr, 1)
            dve.wait_ge(s_ptr, 1)
            dve.wait_ge(s_seed2, 1)

            def rank_one_hots(i, u, h, fresh):
                n = i * 2 + u
                dve.wait_ge(s_bd[h], n * 16 + (2 * BODIES + 1) * 16)
                if not fresh:
                    dve.wait_ge(s_look[h], n)
                    dve.wait_ge(s_upd[h], n)
                one_hots_across(h, s_oht[h])
                one_hots(h, i * (2 * CH) + (u * CH + h * GR), s_ohh[h])

            def ranks(i, first, last):
                for u in range(2):
                    for h in range(2):
                        n = i * 2 + u
                        fresh = first and u == 0
                        dve.wait_ge(s_ta[h], n + 1)
                        v.tensor_tensor(tab_b[h], ps[:, 0:BINS], tab_a[h], ALU.subtract).then_inc(s_tb[h], 1)
                        if not (last and u + h == 2):
                            rank_one_hots(*next_group(i, u, h), fresh and h == 0)
                        dve.wait_ge(s_bc[h], n * 32 + (2 * BODIES * 16 + 32))
                        if not (fresh and h == 0):
                            dve.wait_ge(s_eq[1 - h], n + h)
                        for k in range(GR):
                            w = (k + 1) * P
                            at = (k * (k + 1) // 2) * P
                            col = bass.ds(i * (2 * CH) + (u * CH + h * GR + k), 1)
                            ins = v.scalar_tensor_tensor(junk[:, at:at + w], src_b[h][:, 0:w], src_f[:, col],
                                                         cj[:, J_EARLIER + GC - w:J_EARLIER + GC], ALU.is_equal, ALU.mult,
                                                         accum_out=eqs[:, h, k:k + 1])
                        ins.then_inc(s_eq[h], 1)
                        dve.wait_ge(s_look[h], n + 1)
                        if not fresh:
                            dve.wait_ge(s_sum[h], n + 2 * BODIES)
                        pick(h, s_hit[h])
                        dve.wait_ge(s_sum[h], n + (2 * BODIES + 1))
                        dve.wait_ge(s_eq[h], n + 1)
                        v.tensor_tensor(rank_i[:, 0, :], bank(6 + h, GR), eqs[:, h, :], ALU.add).then_inc(s_q[h], 1)
                        dve.wait_ge(s_q[h], n + 1)
                        own.add(v.tensor_scalar(rank_i[:, 1, :], rank_i[:, 0, :], P - 1, None, ALU.bitwise_and))
                        own.add(v.tensor_scalar(rank_i[:, 2, :], rank_i[:, 0, :], 7, None, ALU.arith_shift_right))
                        own.sync()
                        if h == 0 and not first:
                            dve.wait_ge(s_scat[u], i * (16 * CH))
                        ins = v.scalar_tensor_tensor(qidx[:, u, h * GR:(h + 1) * GR], rank_i[:, 1, :], float(TILES),
                                                     rank_i[:, 2, :], ALU.mult, ALU.add)
                        if h == 0:
                            own.link(ins)
                        else:
                            ins.then_inc(s_qh[u], 1)
                            dve.wait_ge(s_qh[u], i + 1)
            rank_one_hots(0, 0, 0, True)
            peeled_ends(dve, own, ranks)

            dve.wait_ge(s_own_p, 2)
            v.memset(ob, 0.0).then_inc(s_eps, 1)

            def gates(i, first):
                for u in range(2):
                    for h in range(2):
                        q = i * 4 + (2 * u + h)
                        fresh = first and u == 0 and h == 0
                        t0 = i * (2 * CH) + (u * CH + h * GR)
                        dve.wait_ge(s_kb, q + 1)
                        kb = ps[:, 0:GC].rearrange("p (k c) -> p k c", c=P)
                        own.add(v.tensor_copy(first_k[:, bass.ds(t0, GR)], kb[:, :, 0]))
                        own.add(v.tensor_copy(last_k[:, bass.ds(t0 + 1, GR)], kb[:, :, P - 1]))
                        v.tensor_tensor(same[:, bass.ds(t0 * P, GC)].rearrange("p (k c) -> p k c", c=P), kb,
                                        key[:, bass.ds(t0 + 1, GR)].unsqueeze(2).broadcast_to([P, GR, P]),
                                        ALU.is_equal).then_inc(s_same, 1)
                        dve.wait_ge(s_tdb, q + 1)
                        if not fresh:
                            dve.wait_ge(s_u, q)
                        v.tensor_scalar(oh_td, ps[:, 1024:1024 + GC], part0, None, ALU.is_equal).then_inc(s_ohtd, 1)
                        if h == 1:
                            dve.wait_ge(s_kt, i * 2 + (u + 1))
                            own.add(v.tensor_copy(edgec[:, 0:1], bank(0, 1, CH)))
                            own.add(v.tensor_copy(edgec[:, 1:2], bank(1, 1, CH, P - 1)))
                            own.sync()
                            own.link(v.tensor_tensor(edgec[:, 2:3], edgec[:, 0:1], edgec[:, 1:2], ALU.is_equal))
                            v.tensor_scalar(cont_m[:, bass.ds(i * (2 * P) + u * P, P)], bank(0, P, CH), edgec[:, 0:1], edgec[:, 2:3],
                                            ALU.is_equal, ALU.mult).then_inc(s_cont, 1)
                            dve.wait_ge(s_cont, i * 2 + (u + 1))
                        dve.wait_ge(s_u, q + 1)
                        if not fresh:
                            dve.wait_ge(s_logit, q)
                            dve.wait_ge(s_gst, q)
                        for k in range(GR):
                            at = 1024 + (k * NTYPE if k < 4 else 512 + (k - 4) * NTYPE)
                            ins = v.scalar_tensor_tensor(ujunk[:, k, :], cf[:, K_ROW:K_ROW + NTYPE], typ_s[:, bass.ds(t0 + k, 1)],
                                                         ps[:, at:at + NTYPE], ALU.is_equal, ALU.mult, accum_out=logit[:, h, k:k + 1])
                        ins.then_inc(s_logit, 1)
                        dve.wait_ge(s_gate, q + 1)
                        if not (first and u == 0):
                            dve.wait_ge(s_gw[h], (i * 2 + u) * 16)
                        own.link(v.tensor_tensor(gst[:, h], bank(4, GR * F).rearrange("p (k c) -> p k c", c=F),
                                                 rows48[:, 2:3, :].broadcast_to([P, GR, F]), ALU.add))
                        dve.wait_ge(s_logit, q + 1)
                        v.tensor_tensor(gst[:, h], gst[:, h], logit[:, h, :].unsqueeze(2).broadcast_to([P, GR, F]), ALU.add).then_inc(s_gst, 1)
            peeled(dve, own, gates)

            own.sync()
            own.add(v.tensor_tensor(chainf[:], first_k[:], last_k[:, 1:TILES + 1], ALU.is_equal))
            own.add(v.tensor_tensor(chaint[:], first_k[:], last_k[:, 0:TILES], ALU.is_equal))
            own.sync()
            v.tensor_tensor(chainf[:], chainf[:], chaint[:], ALU.mult).then_inc(s_flags, 1)
            for u in range(2):
                dve.wait_ge(s_cols[u], BODIES)
            own.link(v.tensor_scalar(cw_i[:], wcol[:], 1.0 / (2 * CUTOFF), None, ALU.mult))
            own.link(v.scalar_tensor_tensor(cw_t[:, 0, :], cw_i[:], -2 * CUTOFF, wcol[:], ALU.mult, ALU.add))
            own.link(v.scalar_tensor_tensor(cw_t[:, 1, :], cw_t[:, 0, :], -1.0, cw_t[:, 0, :], ALU.mult, ALU.max))
            own.link(v.tensor_scalar(cw_t[:, 0, :], cw_t[:, 1, :], -CUTOFF, None, ALU.add))
            v.scalar_tensor_tensor(cw_t[:, 1, :], cw_t[:, 0, :], -1.0, cw_t[:, 0, :], ALU.mult, ALU.max).then_inc(s_ang, 1)
            dve.wait_ge(s_sin, 1)
            own.link(v.tensor_scalar(cw_t[:, 0, :], cw_t[:, 2, :], -0.5, 0.5, ALU.mult, ALU.add))
            own.link(v.scalar_tensor_tensor(cw_t[:, 1, :], wcol[:], CUTOFF, cw_t[:, 0, :], ALU.is_lt, ALU.mult))
            own.link(v.tensor_tensor(cwmj[:], cw_t[:, 1, :], vec_d[:], ALU.mult))
            dve.wait_ge(s_next, 1)
            own.link(v.tensor_tensor(cw_t[:, 0, :], bank(0, TILES), key[:, 1:TILES + 1], ALU.is_equal))
            v.scalar_tensor_tensor(out_i[:], cw_t[:, 0, :], FAR, key[:, 1:TILES + 1], ALU.mult, ALU.add).then_inc(s_outi, 1)
            for h in range(2):
                dve.wait_ge(s_gw[h], 2 * BODIES * 16)
            own.link(v.memset(uo, 0.0))

            def center(chain, ln, n, x):
                cen, _, _, _, buf, st = ln
                chain.link(v.tensor_reduce(st[:, 0], x, AX_X, ALU.add))
                v.scalar_tensor_tensor(buf[:, 0], st[:, 0].unsqueeze(2).broadcast_to([P, CH, F]), -1.0 / F, x, ALU.mult, ALU.add).then_inc(cen, 1)

            def variance(ln, n):
                _, sq, var, _, buf, st = ln
                dve.wait_ge(sq, n + 1)
                v.tensor_reduce(st[:, 1], buf[:, 1], AX_X, ALU.add).then_inc(var, 1)

            def scaled(chain, ln, n, dst):
                cen, _, _, sd, buf, st = ln
                dve.wait_ge(cen, n + 1)
                dve.wait_ge(sd, n + 1)
                chain.link(v.reciprocal(st[:, 3], st[:, 2]))
                return v.tensor_tensor(dst, buf[:, 0], st[:, 3].unsqueeze(2).broadcast_to([P, CH, F]), ALU.mult)

            def row(r):
                return rows48[:, r:r + 1, :].broadcast_to([P, CH, F])

            def agg_of(u, width, lo, hi):
                return ps[:, (4 + 2 * u) * 512:(6 + 2 * u) * 512].rearrange("p (b x) -> p b x", b=2)[:, :, 0:GR * width].rearrange(
                    "p b (t c) -> p b t c", c=width)[:, :, :, lo:hi]

            def halves(ap):
                return ap.rearrange("p (b t) c -> p b t c", b=2)

            def message(kind, s, i, u, first=False, gathers=True):
                m, width = bodies_before(kind, s, nb) + i, XW if kind == FIRST else F
                msg = msg_f[:, u, 0:CH * width].rearrange("p (t c) -> p t c", c=width)
                at = chunk_cols(i, u)
                dve.wait_ge(s_st[u], m * 16 + 16)
                if kind != FIRST and gathers:
                    dve.wait_ge(s_gat[u], (gathers_before(kind, s, nb) + i) * (16 * CH) + 16 * CH)
                if not first:
                    dve.wait_ge(s_agg[u], m)
                if kind == FIRST:
                    v.tensor_copy(msg[:, :, F], wcol[:, at])
                    v.memset(msg[:, :, F + 1:F + 2], 1.0)
                    v.tensor_copy(msg[:, :, F + 2], vec_d[:, at])
                x = stage[:, u, :, 0:F]
                if kind == LAYER3:
                    dve.wait_ge(s_g[u], i * 16 + 16)
                    v.tensor_tensor(msg, x, gb[:, u], ALU.mult).then_inc(s_gx, 1)
                    dve.wait_ge(s_gx, i * 2 + (u + 1))
                    x = msg
                scale = {LAYER2: stage[:, u, :, F:FW], LAYER3: cwmj[:, at].unsqueeze(2)}.get(kind, wcol[:, at].unsqueeze(2))
                v.tensor_tensor(msg[:, :, 0:F], x, scale.broadcast_to([P, CH, F]), ALU.mult).then_inc(s_msg[u], 1)

            def carry(kind, s, i, u, first=False):
                m, width = bodies_before(kind, s, nb) + i, XW if kind == FIRST else F
                dve.wait_ge(s_aggt[u], m + 1)
                if not first:
                    dve.wait_ge(s_stt[u], m)
                if not (first and u == 0):
                    dve.wait_ge(s_state[1 - u], m + u)
                    own_c.link(v.tensor_copy(state[:, u, 0:1], state[:, 1 - u, CH:CH + 1]))
                else:
                    own_c.link(v.memset(state[:, u, 0:1], 0.0))
                v.tensor_tensor_scan(state[0:width, u, 1:CH + 1], chainf[0:width, chunk_cols(i, u)],
                                     aggt[0:width, :].rearrange("p (t c) -> p t c", c=P)[:, :, P - 1],
                                     state[0:width, u, 0:1], ALU.mult, ALU.add).then_inc(s_state[u], 1)

            def spread(kind, s, i, u, first=False):
                m, width = bodies_before(kind, s, nb) + i, XW if kind == FIRST else F
                dve.wait_ge(s_stt[u], m + 1)
                v.tensor_tensor(cm[:, u, 0:CH * width].rearrange("p (t c) -> p t c", c=width),
                                bank(5 + 2 * u, width, CH, STT_AT).unsqueeze(1).broadcast_to([CH, CH, width]),
                                delta.unsqueeze(2).broadcast_to([CH, CH, width]), ALU.mult).then_inc(s_cm[u], 1)

            def finish(kind, s, i, u, first=False):
                m, width = bodies_before(kind, s, nb) + i, XW if kind == FIRST else F
                at = chunk_cols(i, u)
                dve.wait_ge(s_agg[u], m + 1)
                dve.wait_ge(s_y[u], m * 16 + 16)
                if not first:
                    dve.wait_ge(s_outw[u], table_writes(kind, s, nb, i if kind != LAYER3 else 0))
                if kind == FIRST and first:
                    dve.wait_ge(s_prefw[u], BODIES * 16)
                if LAST <= kind < LAYER3:
                    dve.wait_ge(s_yo[u], i * 16 + (kind - LAST + 1) * BODIES * 16)
                if kind == LAYER3:
                    dve.wait_ge(s_yo[u], 4 * BODIES * 16)
                    dve.wait_ge(s_oidx[u], i + 1)
                y, o = yb[:, u], ob[:, u, :, 0:F]
                agg = agg_of(u, width, 0, F)
                t1 = lnb[:, 2]
                if kind == FIRST:
                    def per_position(c):
                        return agg_of(u, width, c, c + 1).rearrange("p b t c -> p b (t c)")

                    def pair(ap):
                        return ap.rearrange("p (b t) -> p b t", b=2)
                    v.tensor_copy(pair(small[:, 0]), per_position(F + 1)).then_inc(s_cnt, 1)
                    own_c.add(v.tensor_scalar(pair(small[:, 2]), per_position(F), 1e-10, None, ALU.add))
                    own_c.add(v.tensor_scalar(pair(small[:, 3]), per_position(F + 2), 1e-8, None, ALU.max))
                    own_c.sync()
                    own_c.add(v.reciprocal(rtot[:, at], small[:, 3]))
                    own_c.link(v.reciprocal(small[:, 2], small[:, 2]))
                    own_c.link(v.tensor_scalar(coef[:, at], small[:, 2], 1.0 - ALPHA, None, ALU.mult))
                    dve.wait_ge(s_rt, m * 2 + (u + 1))
                    own_c.link(v.reciprocal(dis[:, at], small[:, 1]))
                settled(dve)
                if kind == LAYER1:
                    own_c.link(v.tensor_copy(ob[:, u, :, F], dis[:, at]))
                if kind <= LAST:
                    own_c.link(v.tensor_tensor(halves(t1), agg, halves(coef[:, at].unsqueeze(2).broadcast_to([P, CH, F])), ALU.mult))
                if kind < LAST:
                    v.scalar_tensor_tensor(o, y, ALPHA, t1, ALU.mult, ALU.add).then_inc(s_out[u], 1)
                    return
                if kind == LAST:
                    own_c.link(v.scalar_tensor_tensor(t1, y, 1.0 + ALPHA, t1, ALU.mult, ALU.add))
                elif kind in (LAYER1, LAYER2):
                    bias = rows48[:, kind - LAYER1:kind - LAYER1 + 1, :].broadcast_to([P, CH, F])
                    if kind == LAYER1:
                        own_c.link(v.tensor_tensor(halves(t1), agg, halves(bias), ALU.add))
                    else:
                        own_c.link(v.tensor_tensor(halves(t1), agg, halves(dis[:, at].unsqueeze(2).broadcast_to([P, CH, F])), ALU.mult))
                        own_c.link(v.tensor_tensor(t1, t1, bias, ALU.add))
                    if kind == LAYER1:
                        own_c.link(v.tensor_tensor(t1, t1, y, ALU.add))
                    else:
                        own_c.link(v.scalar_tensor_tensor(t1, t1, 0.0, y, ALU.max, ALU.add))
                else:
                    own_c.link(v.tensor_tensor(halves(t1), agg, halves(rtot[:, at].unsqueeze(2).broadcast_to([P, CH, F])), ALU.mult))
                    own_c.link(v.tensor_tensor(t1, t1, y, ALU.add))
                center(own_c, ln_chunk, ln_of_chunk(kind, i, u, 0), t1)

            def finish_norm(kind, i, u):
                if kind < LAST:
                    return
                y, o, t1 = yb[:, u], ob[:, u, :, 0:F], lnb[:, 2]
                n = ln_of_chunk(kind, i, u, 0)
                variance(ln_chunk, n)
                if kind == LAYER3:
                    own_c.link(scaled(own_c, ln_chunk, n, t1))
                    own_c.link(v.tensor_tensor(t1, t1, row(3), ALU.mult))
                    own_c.link(v.tensor_tensor(t1, t1, row(4), ALU.add))
                    own_c.link(v.tensor_tensor(t1, t1, y, ALU.add))
                    n = ln_of_chunk(kind, i, u, 1)
                    center(own_c, ln_chunk, n, t1)
                    variance(ln_chunk, n)
                scaled(own_c, ln_chunk, n, o).then_inc(s_out[u], 1)

            def each(units, ins):
                for w in range(units):
                    own_u.add(ins(w))
                own_u.sync()

            def wide(st):
                return st.unsqueeze(2).broadcast_to([P, CH, F])

            def unit_center(n, units, x):
                each(units, lambda w: v.tensor_reduce(uns[:, 0, w], x[:, w], AX_X, ALU.add))
                for w in range(units):
                    v.scalar_tensor_tensor(ut[:, w], wide(uns[:, 0, w]), -1.0 / F, x[:, w], ALU.mult, ALU.add).then_inc(s_ucen, 1)

            def unit_variance(n, units):
                for w in range(units):
                    dve.wait_ge(s_usq, n + (w + 1))
                    v.tensor_reduce(uns[:, 1, w], usq[:, w], AX_X, ALU.add).then_inc(s_uvar, 1)

            def unit_inverse(n, w):
                dve.wait_ge(s_ucen, n + (w + 1))
                dve.wait_ge(s_usd, n + (w + 1))
                own_u.link(v.reciprocal(uns[:, 3, w], uns[:, 2, w]))

            def edge_layer(kind, j, l, first=False):
                n = ln_of_unit(kind, j, l)
                unit_inverse(n, 0)
                if l == 0 and not first:
                    dve.wait_ge(s_uow, j * (16 * EDGE_LN) + (kind == LAST) * (BODIES * EDGE_LN + EARLY_PAIRS) * 16)
                ins = v.tensor_tensor(uo[:, l, :, 0:F], ut[:, 0], wide(uns[:, 3, 0]), ALU.mult)
                if l == EDGE_LN - 1:
                    ins.then_inc(s_uo, 1)
                    assert own_u.k == UNIT_COUNTS[0], f"UNIT_COUNTS 0 counts {own_u.k}"
                else:
                    own_u.link(ins)
                    v.tensor_tensor(ut[:, 0], uo[:, l, :, 0:F], row(6 - l), ALU.add).then_inc(s_ucen, 1)

            def messages(kind, s, i, gathers=True):
                message(kind, s, i, 0, gathers=gathers)
                message(kind, s, i, 1, gathers=gathers)

            def chunks(kind, s, i, first=False, gathers=None):
                finish(kind, s, i, 0, first)
                carry(kind, s, i, 1, first)
                spread(kind, s, i, 1, first)
                if gathers is not None:
                    message(kind, s, i + 1, 0, gathers=gathers)
                finish_norm(kind, i, 0)
                finish(kind, s, i, 1, first)
                if gathers is not None:
                    message(kind, s, i + 1, 1, gathers=gathers)
                finish_norm(kind, i, 1)
                assert own_c.k == CHUNK_COUNTS[kind], f"CHUNK_COUNTS {kind} counts {own_c.k}"

            def own_base(kind, s, i):
                own_c.base, own_c.k = i * CHUNK_COUNTS[kind] + counted_before(kind, s, nb), 0

            def body_with_unit(kind, i, gathers=None, first=False):
                own_base(kind, 0, i)
                own_u.base, own_u.k = counted_units(kind, i), 0
                carry(kind, 0, i, 0, first)
                dve.wait_ge(s_ux, i * 16 + (16 + (kind == LAST) * (BODIES + EARLY_PAIRS) * 16))
                unit_center(ln_of_unit(kind, i, 0), 1, ux)
                spread(kind, 0, i, 0, first)
                for l in range(EDGE_LN):
                    unit_variance(ln_of_unit(kind, i, l), 1)
                    edge_layer(kind, i, l, first)
                chunks(kind, 0, i, first, gathers)

            def plain_body(kind, s, i, gathers=None):
                own_base(kind, s, i)
                carry(kind, s, i, 0)
                spread(kind, s, i, 0)
                chunks(kind, s, i, gathers=gathers)

            def lone_body(kind, i, gathers=None):
                plain_body(kind, 0, i, gathers)

            def full_pass(kind, body):
                messages(kind, 0, 0)
                with dve.Fori(0, last_a) as i:
                    body(kind, i, True)
                with dve.If(nb < BODIES):
                    with dve.Fori(last_a, BODIES - 1) as i:
                        body(kind, i, False)
                with dve.Else():
                    settled(dve)
                body(kind, BODIES - 1)

            def dve_pair(q, late=False, around=None):
                s, i = around if around is not None else (0, None)
                own_u.base, own_u.k = counted_pairs(q, late), 0

                def part(f, u):
                    if i is not None:
                        f(STEP, s, i, u)
                if i is not None:
                    own_base(STEP, s, i)
                part(message, 0)
                dve.wait_ge(s_ux, before_pair(q, late) * 16 + 16)
                unit_center(ln_of_pair(q, late, 0), 2, ux)
                part(message, 1)
                for l in range(DENSE_LN):
                    n = ln_of_pair(q, late, l)
                    unit_variance(n, 2)
                    if l == 1:
                        part(spread, 0)
                    if l == 2:
                        part(finish, 0)
                    for w in range(2):
                        unit_inverse(n, w)
                        if l == 2:
                            own_u.link(v.tensor_tensor(uns[:, 4, w], uns[:, 1, w], uns[:, 3, w], ALU.mult))
                            v.tensor_tensor(uns[:, 4, w], uns[:, 4, w], uns[:, 3, w], ALU.mult).then_inc(s_xvar, 1)
                        if l == DENSE_LN - 1:
                            if w == 0:
                                dve.wait_ge(s_uow, q * 16 + BODIES * EDGE_LN * 16 * (1 + late))
                            ins = v.tensor_tensor(udone[:, w], ut[:, w], wide(uns[:, 3, w]), ALU.mult)
                            if w == 1:
                                ins.then_inc(s_uo, 1)
                        else:
                            own_u.add(v.tensor_tensor(ut[:, w], ut[:, w], wide(uns[:, 3, w]), ALU.mult))
                    if l < 2:
                        own_u.sync()
                        for w in range(2):
                            v.tensor_tensor(ut[:, w], ut[:, w], row(6 - l), ALU.add).then_inc(s_ucen, 1)
                        if l == 0:
                            part(carry, 0)
                    if l == 2:
                        for w in range(2):
                            dve.wait_ge(s_xsd, q * 2 + (w + 1))
                            own_u.link(v.reciprocal(uns[:, 4, w], uns[:, 5, w]))
                            own_u.add(v.tensor_tensor(usq[:, w], row(3), wide(uns[:, 4, w]), ALU.mult))
                        own_u.sync()
                        each(2, lambda w: v.scalar_tensor_tensor(ut[:, w], usq[:, w], 1.0, ut[:, w], ALU.add, ALU.mult))
                        part(carry, 1)
                        each(2, lambda w: v.tensor_tensor(ut[:, w], ut[:, w], row(4), ALU.add))
                        unit_center(ln_of_pair(q, late, 3), 2, ut)
                        part(spread, 1)
                assert own_u.k == UNIT_COUNTS[1], f"UNIT_COUNTS 1 counts {own_u.k}"
                part(finish, 1)
                if i is not None:
                    assert own_c.k == CHUNK_COUNTS[STEP], f"CHUNK_COUNTS {STEP} counts {own_c.k}"

            def dve_step(s, half):
                q = s * PAIRS + 1
                dve_pair(q, around=(s, 0))
                dve_pair(q + 1, around=(s, 1))

                def more(i):
                    messages(STEP, s, i)
                    plain_body(STEP, s, i)
                rest(dve, nb, more)
                dve_pair(q + 2)

            nb, last_a = load_bodies(dve), load_last(dve)
            message(FIRST, 0, 0, 0, True)
            message(FIRST, 0, 0, 1, True)
            body_with_unit(FIRST, 0, False, True)
            with dve.Fori(1, BODIES - 1) as i:
                body_with_unit(FIRST, i, False)
            body_with_unit(FIRST, BODIES - 1)
            dve_pair(0)
            full_pass(SECOND, lone_body)
            run_steps(dve, dve_step)
            dve.wait_ge(s_uow, (BODIES * EDGE_LN + EARLY_PAIRS) * 16)
            own.link(v.memset(uo, 0.0))
            full_pass(LAST, body_with_unit)
            for kind in (LAYER1, LAYER2, LAYER3):
                for p in range(LATE_PAIRS):
                    dve_pair(EARLY_PAIRS + (kind - LAYER1) * LATE_PAIRS + p, late=True)
                full_pass(kind, lone_body)

        @block.tensor
        def _(pe):
            mm = nc.tensor.matmul
            pe.wait_ge(s_const, N_CONST)
            mm(bank(7, NTYPE, EMB), adaptt_sb[:], embt_sb[:], start=True, stop=True).then_inc(s_vt, 1)
            pe.wait_ge(s_vtc, 1)
            pe.wait_ge(s_zero, 1)
            mm(bank(0), ident16, zero16, start=True, stop=True)
            mm(bank(1), ident16, zero16, start=True, stop=True)

            def count_edges(h):
                for k in range(GR):
                    for b in range(NB):
                        ins = mm(ps[:, b * P:(b + 1) * P], ohh[h][:, k * BINS + b * P:k * BINS + (b + 1) * P],
                                 ohl[h][:, k * P:(k + 1) * P], start=False, stop=(k == GR - 1), skip_group_check=True)
                return ins

            def look_up(h, tables, done):
                for at, w in ((0, 512), (512, GC - 512)):
                    for b in range(NB):
                        for t, tab in enumerate(tables):
                            ins = mm(ps[:, (2 + 2 * h) * 512 + at:(2 + 2 * h) * 512 + at + w], tab[:, b * P:(b + 1) * P],
                                     oht[h][:, b * GC + at:b * GC + at + w], start=(b == 0 and t == 0),
                                     stop=(b == NB - 1 and t == len(tables) - 1))
                ins.then_inc(done, 1)

            def column_sums(h, done):
                for k in range(GR):
                    ins = mm(bank(6 + h, 1, P, k), hit[h][:, k * P:(k + 1) * P], cf[:, K_ONE:K_ONE + 1], start=True, stop=True)
                ins.then_inc(done, 1)

            def histogram(i, first):
                for u in range(2):
                    for h in range(2):
                        pe.wait_ge(s_oh[h], i * 2 + (u + 1))
                        count_edges(h).then_inc(s_hist[h], 1)
            peeled(pe, None, histogram)
            pe.wait_ge(s_cnt1, 1)
            mm(bank(0), ident16, zero16, start=True, stop=True)
            mm(bank(1), ident16, zero16, start=True, stop=True)

            def flag_look_up(i, u, h, fresh):
                pe.wait_ge(s_oht[h], i * 2 + (u + 1))
                if not fresh:
                    pe.wait_ge(s_dhit[h], i * 2 + u)
                look_up(h, (has16,), s_dlook[h])

            def active(i, first, last):
                for u in range(2):
                    for h in range(2):
                        n = i * 2 + u
                        fresh = first and u == 0
                        pe.wait_ge(s_dhit[h], n + 1)
                        if not fresh:
                            pe.wait_ge(s_oh[h], n + 2 * BODIES)
                        column_sums(h, s_sum[h])
                        if not (last and u + h == 2):
                            flag_look_up(*next_group(i, u, h), fresh and h == 0)
                        pe.wait_ge(s_oh[h], n + (2 * BODIES + 1))
                        count_edges(h).then_inc(s_hist[h], 1)
            flag_look_up(0, 0, 0, True)
            peeled_ends(pe, None, active)
            pe.wait_ge(s_incl, 1)
            mm(bank(2, 1), cf[:, K_BEFORE:K_BEFORE + P], incl[:, BINS - 1:BINS], start=True, stop=True)
            mm(bank(2, 1, P, 1), cf[:, K_BEFORE:K_BEFORE + P], incl_b[:, BINS - 1:BINS], start=True, stop=True)
            mm(bank(2, 1, P, 2), cf[:, K_ALL:K_ALL + P], incl[:, BINS - 1:BINS], start=True, stop=True).then_inc(s_off, 1)
            pe.wait_ge(s_base, 1)
            for b, n in ((0, 512), (1, BINS - 512)):
                mm(bank(b, n), ident16, base_a[:, b * 512:b * 512 + n], start=True, stop=False)
                ins = mm(bank(b, n), ident16, base_b[:, b * 512:b * 512 + n], start=False, stop=True)
            ins.then_inc(s_seed2, 1)

            def ranks(i, first):
                for u in range(2):
                    for h in range(2):
                        n = i * 2 + u
                        fresh = first and u == 0
                        pe.wait_ge(s_oht[h], n + (2 * BODIES + 1))
                        pe.wait_ge(s_tb[h], n + 1)
                        if not fresh:
                            pe.wait_ge(s_hit[h], n)
                        look_up(h, (tab_a[h], tab_b[h]), s_look[h])
                        pe.wait_ge(s_ohh[h], n + 1)
                        count_edges(h).then_inc(s_upd[h], 1)
                        pe.wait_ge(s_hit[h], n + 1)
                        if not fresh:
                            pe.wait_ge(s_q[h], n)
                        column_sums(h, s_sum[h])
            peeled(pe, None, ranks)

            for h in range(2):
                pe.wait_ge(s_q[h], 2 * BODIES)
            mm(bank(7, NTYPE, NTYPE, 128), vt_sb[:], embt_sb[:], start=True, stop=True).then_inc(s_tab, 1)
            pe.wait_ge(s_tabc, 1)

            def gates(i, first):
                for u in range(2):
                    for h in range(2):
                        q = i * 4 + (2 * u + h)
                        fresh = first and u == 0 and h == 0
                        t0 = i * (2 * CH) + (u * CH + h * GR)
                        pe.wait_ge(s_cols[u], i + 1)
                        if not fresh:
                            pe.wait_ge(s_same, q)
                            if u + h:
                                pass
                            pe.wait_ge(s_cont, i * 2 + u)
                        for k in range(GR):
                            ins = mm(ps[:, k * P:(k + 1) * P], key_s[:, u, h * GR + k + 1:h * GR + k + 2].broadcast_to([P, P]), ident, start=True, stop=True)
                        ins.then_inc(s_kb, 1)
                        if not fresh:
                            pe.wait_ge(s_logit, q)
                        for k in range(GR):
                            ins = mm(ps[:, 1024 + k * P:1024 + (k + 1) * P], typ_f[:, u, h * GR + k:h * GR + k + 1].broadcast_to([P, P]), ident, start=True, stop=True)
                        ins.then_inc(s_tdb, 1)
                        pe.wait_ge(s_rec[u], i * 16 + 16)
                        if not fresh:
                            pe.wait_ge(s_gst, q)
                            pe.wait_ge(s_atc, q)
                        settled(pe)
                        for k in range(GR):
                            ins = nc.tensor.transpose(ps[0:R_ATTR, 2048 + k * P:2048 + (k + 1) * P],
                                                      rec[:, u, h * GR + k, C_ATTR:C_ATTR + R_ATTR], ident)
                        ins.then_inc(s_at, 1)
                        pe.wait_ge(s_atc, q + 1)
                        if not fresh:
                            pe.wait_ge(s_h1s, q)
                        settled(pe)
                        mm(bank(6, 512, H), g1t_sb[:], attr_t[:, 0:512], start=True, stop=True)
                        mm(bank(7, GC - 512, H), g1t_sb[:], attr_t[:, 512:GC], start=True, stop=True).then_inc(s_h1, 1)
                        if h == 1:
                            pe.wait_ge(s_same, q + 1)
                            settled(pe)
                            nc.tensor.transpose(bank(0, P, CH), key_s[:, u, 1:CH + 1], ident)
                            nc.tensor.transpose(bank(1, P, CH), key_s[:, u, 0:CH], ident).then_inc(s_kt, 1)
                        pe.wait_ge(s_ohtd, q + 1)
                        for k in range(GR):
                            at = 1024 + (k * NTYPE if k < 4 else 512 + (k - 4) * NTYPE)
                            ins = mm(ps[:, at:at + NTYPE], oh_td[0:NTYPE, k * P:(k + 1) * P], tab_sb[:], start=True, stop=True)
                        ins.then_inc(s_u, 1)
                        pe.wait_ge(s_h1s, q + 1)
                        for k in range(GR):
                            ins = mm(ps[:, 2048 + k * F:2048 + (k + 1) * F], h1_t[:, k * P:(k + 1) * P], g2t_sb[:], start=True, stop=True)
                        ins.then_inc(s_gate, 1)
            peeled(pe, None, gates)
            pe.wait_ge(s_same, 2 * CHUNKS)
            pe.wait_ge(s_flags, 1)
            mm(bank(0, TILES), cf[:, K_NEXT:K_NEXT + P], key[:, 1:TILES + 1], start=True, stop=False)
            mm(bank(0, TILES), cf[:, K_NEXTT:K_NEXTT + P], key[:, 2:TILES + 2], start=False, stop=True).then_inc(s_next, 1)
            pe.wait_ge(s_outi, 1)
            pe.wait_ge(s_gst, 2 * CHUNKS)

            nb = load_bodies(pe)

            def pe_body(kind, s, i, first=False):
                m = bodies_before(kind, s, nb) + i
                width = XW if kind == FIRST else F
                through = w_sb[:, kind - LAYER1, :] if kind in (LAYER1, LAYER2) else ident[0:width, 0:width]

                def tail(u):
                    pe.wait_ge(s_msg[u], m + 1)
                    if not (first and u == 0):
                        pe.wait_ge(s_aggt[1 - u], m + u)
                    for k in range(CH):
                        ins = mm(ps[0:width, k * P:(k + 1) * P], msg_f[:, u, k * width:(k + 1) * width],
                                 same[:, bass.ds(i * (2 * CH * P) + (u * CH + k) * P, P)], start=True, stop=True)
                    ins.then_inc(s_tail[u], 1)

                def back(u, b):
                    for k in range(b * GR, (b + 1) * GR):
                        mm(bank(4 + 2 * u + b, width, P, (k % GR) * width), aggt[0:width, k * P:(k + 1) * P], through,
                           start=(k % GR == 0), stop=False)

                def carried(u):
                    pe.wait_ge(s_state[u], m + 1)
                    settled(pe)
                    mm(bank(5 + 2 * u, width, CH, STT_AT), state[0:width, u, 0:CH], through, start=True, stop=True).then_inc(s_stt[u], 1)

                def complete(u):
                    pe.wait_ge(s_cm[u], m + 1)
                    back(u, 1)
                    pe.wait_ge(s_conts[u], m + 1)
                    for b in range(2):
                        ins = mm(bank(4 + 2 * u + b, GR * width), cont_s[:, u, :],
                                 cm[:, u, b * GR * width:(b + 1) * GR * width], start=False, stop=True)
                    ins.then_inc(s_agg[u], 1)

                tail(0)
                for u in range(2):
                    pe.wait_ge(s_aggt[u], m + 1)
                    if not first:
                        pe.wait_ge(s_out[u], m)
                    back(u, 0)
                    carried(u)
                    if u == 0:
                        tail(1)
                    complete(u)

            peeled(pe, None, lambda i, first: pe_body(FIRST, 0, i, first))
            with pe.Fori(0, BODIES) as i:
                pe_body(SECOND, 0, i)
            run_steps(pe, lambda s, half: some_bodies(pe, nb, lambda i: pe_body(STEP, s, i)))
            for kind in (LAST, LAYER1, LAYER2, LAYER3):
                with pe.Fori(0, BODIES) as i:
                    pe_body(kind, 0, i)


_OUT = (P * DROWS, F)


def kernel(**inputs):
    import concourse.bacc as bacc
    from concourse.bass_utils import run_bass_kernel_spmd as run

    a = {k: np.asarray(v) for k, v in inputs.items()}
    pad = EPAD - EDGES

    def tiles(x):
        x = np.concatenate([x, np.zeros((pad,) + x.shape[1:], x.dtype)])
        return np.ascontiguousarray(x.reshape(TILES, P, -1).transpose(1, 0, 2).reshape(P, -1))

    spare = np.full(pad, SPARE, a["src"].dtype)
    src, dst = (np.concatenate([a[n], spare]) for n in ("src", "dst"))
    by_chunk = np.stack([x.reshape(CHUNKS, CH, P) for x in (dst, src)], 1)
    x = a["x"]
    f, h = constants()
    arrays = {
        "node_table": np.concatenate([x, a["node_vec"][:, None], a["node_type_119"][:, None].view(np.float32)], 1),
        "x_dense": np.concatenate([x, np.zeros((P * DROWS - NODES, F), x.dtype)]).reshape(P, DROWS * F),
        "edge_table": tiles(np.concatenate([a["edge_attr_40"], a["edge_weight"][:, None]], 1)),
        "index_chunks": np.ascontiguousarray(by_chunk.transpose(3, 0, 1, 2).reshape(P, -1)),
        "src_cols": np.ascontiguousarray(src.reshape(TILES, P).T),
        "edge_rows": np.concatenate([src.reshape(TILES // 2, 2 * P), dst.reshape(TILES // 2, 2 * P)], 1),
        "const_f": f,
        "const_h": h,
        "w1": a["L1_gnn_weight"],
        "b1": a["L1_gnn_bias"],
        "w2t": np.ascontiguousarray(a["L2_gnn_W"].T),
        "b2": a["L2_gnn_b"],
        "g1t": np.ascontiguousarray(a["L3_gnn_W1"].T),
        "gb1": a["L3_gnn_b1"][:, None],
        "g2t": np.ascontiguousarray(a["L3_gnn_W2"].T),
        "gb2": a["L3_gnn_b2"],
        "embt": np.ascontiguousarray(a["L3_gnn_emb"].T),
        "adaptt": np.ascontiguousarray(a["L3_gnn_adaptW"].T),
        "gamma": a["L3_gnn_gamma"],
        "beta": a["L3_gnn_beta"],
    }
    nc = bacc.Bacc("TRN2", target_bir_lowering=False, num_devices=1)
    arrays = {f"in_{k}": np.ascontiguousarray(v) for k, v in arrays.items()}
    args = [nc.dram_tensor(k, v.shape, mybir.dt.from_np(v.dtype), kind="ExternalInput").ap() for k, v in arrays.items()]
    out = nc.dram_tensor("out", _OUT, F32, kind="ExternalOutput").ap()
    build(nc, *args, out)
    r = run(nc, [arrays], core_ids=[0])
    return r.results[0]["out"][:NODES]
```
